# Optimizing a Trainium2 kernel written in Bass

```python
import numpy as np
import jax
import jax.numpy as jnp

def _softmax(x, axis=-1):
    return jax.nn.softmax(x, axis=axis)

def _gelu(x):
    return jax.nn.gelu(x, approximate=True)

def _silu(x):
    return jax.nn.silu(x)

def _sigmoid(x):
    return jax.nn.sigmoid(x)

def _layernorm(x, axis=-1, eps=1e-05):
    m = jnp.mean(x, axis=axis, keepdims=True)
    v = jnp.var(x, axis=axis, keepdims=True)
    return (x - m) / jnp.sqrt(v + eps)

def _scatter_add(tgt, idx, src, axis=0):
    return tgt.at[idx].add(src)

def _segment_sum(src, seg, n):
    return jax.ops.segment_sum(src, seg, n)
kernel_name = 'mk_audio_tower_d1_tok_aud1d512_r4_b42581'

def setup_inputs(seed: int=0):
    np.random.seed(seed)
    _w = jnp.asarray

    def _rec_inputs():
        import jax
        import jax.numpy as jnp
        _rk = jax.random.key(seed)
        x = 0.000214012 + 1.00007 * jax.random.normal(jax.random.fold_in(_rk, 1), (32, 120000), jnp.float32)
        return x
    x = _rec_inputs()

    def _L0_tok_setup():
        import jax, jax.numpy as jnp
        import numpy as np
        HOP = 128

        def _dct_ortho_basis(n):
            k = np.arange(n)[:, None].astype(np.float64)
            t = np.arange(n)[None, :].astype(np.float64)
            D = np.cos(np.pi * (2.0 * t + 1.0) * k / (2.0 * n))
            scale = np.full((n, 1), np.sqrt(2.0 / n))
            scale[0, 0] = np.sqrt(1.0 / n)
            return jnp.asarray((scale * D).astype(np.float32))
        key = jax.random.key(seed)
        x = jax.random.normal(key, (32, 262000), dtype=jnp.float32)
        return {'x': x}
    _L0_tok_all = _L0_tok_setup()
    _L0_tok_in = {k: v for k, v in _L0_tok_all.items() if k in ()}
    del _L0_tok_all

    def _L0_attn_setup():
        import jax, jax.numpy as jnp
        import numpy as np
        B, L, D = (4, 2048, 128)
        key = jax.random.key(seed)
        k_x, k_nu, k_th, k_gr, k_gi = jax.random.split(key, 5)
        return {'x': jax.random.normal(k_x, (B, L, D), dtype=jnp.float32), 'nu': jax.random.normal(k_nu, (D,), dtype=jnp.float32), 'theta': jax.random.normal(k_th, (D,), dtype=jnp.float32), 'gamma_real': jax.random.normal(k_gr, (D,), dtype=jnp.float32), 'gamma_imag': jax.random.normal(k_gi, (D,), dtype=jnp.float32)}
    _L0_attn_all = _L0_attn_setup()
    _L0_attn_in = {k: v for k, v in _L0_attn_all.items() if k in ('nu', 'theta', 'gamma_real', 'gamma_imag')}
    del _L0_attn_all

    def _L0_ffn_setup():
        import jax, jax.numpy as jnp
        import numpy as np
        B, T, D = (4, 2048, 128)
        E, F, CAP = (8, 512, 1024)
        key = jax.random.key(seed)
        ks = jax.random.split(key, 6)
        s = 0.02
        return {'x': jax.random.normal(ks[0], (B, T, D), dtype=jnp.float32), 'Wr': jax.random.normal(ks[1], (D, E), dtype=jnp.float32) * s, 'W1': jax.random.normal(ks[2], (E, D, F), dtype=jnp.float32) * s, 'b1': jax.random.normal(ks[3], (E, F), dtype=jnp.float32) * s, 'W2': jax.random.normal(ks[4], (E, F, D), dtype=jnp.float32) * s, 'b2': jax.random.normal(ks[5], (E, D), dtype=jnp.float32) * s}
    _L0_ffn_all = _L0_ffn_setup()
    _L0_ffn_in = {k: v for k, v in _L0_ffn_all.items() if k in ('Wr', 'W1', 'b1', 'W2', 'b2')}
    del _L0_ffn_all
    return {'x': x, 'L0_attn_nu': _L0_attn_in['nu'], 'L0_attn_theta': _L0_attn_in['theta'], 'L0_attn_gamma_real': _L0_attn_in['gamma_real'], 'L0_attn_gamma_imag': _L0_attn_in['gamma_imag'], 'L0_ffn_Wr': _L0_ffn_in['Wr'], 'L0_ffn_W1': _L0_ffn_in['W1'], 'L0_ffn_b1': _L0_ffn_in['b1'], 'L0_ffn_W2': _L0_ffn_in['W2'], 'L0_ffn_b2': _L0_ffn_in['b2']}

def reference(x, L0_attn_nu, L0_attn_theta, L0_attn_gamma_real, L0_attn_gamma_imag, L0_ffn_Wr, L0_ffn_W1, L0_ffn_b1, L0_ffn_W2, L0_ffn_b2):
    import jax
    import jax.numpy as jnp

    def _L0_tok_ref(x):
        import jax, jax.numpy as jnp
        import numpy as np
        HOP = 128

        def _dct_ortho_basis(n):
            k = np.arange(n)[:, None].astype(np.float64)
            t = np.arange(n)[None, :].astype(np.float64)
            D = np.cos(np.pi * (2.0 * t + 1.0) * k / (2.0 * n))
            scale = np.full((n, 1), np.sqrt(2.0 / n))
            scale[0, 0] = np.sqrt(1.0 / n)
            return jnp.asarray((scale * D).astype(np.float32))
        x_len = x.shape[-1]
        pad_len = HOP - x_len % HOP
        x = jnp.pad(x, [(0, 0)] * (x.ndim - 1) + [(0, pad_len)])
        n_frames = x.shape[-1] // HOP
        frames = x.reshape(x.shape[:-1] + (n_frames, HOP))
        D = _dct_ortho_basis(HOP)
        return jnp.einsum('bfh,kh->bfk', frames, D)

    def _L0_attn_ref(x, nu, theta, gamma_real, gamma_imag):
        import jax, jax.numpy as jnp
        import numpy as np
        B, L, D = (4, 2048, 128)
        b, l, d = x.shape
        n = 2 * l
        log_lambda = -jnp.exp(nu) + 1j * theta
        t = jnp.arange(l, dtype=x.dtype)
        lambda_powers = jnp.exp(t[:, None] * log_lambda[None, :])
        gamma = gamma_real + 1j * gamma_imag
        kernel = gamma[None, :] * lambda_powers
        kernel_f = jnp.fft.fft(kernel, n=n, axis=0)
        x_f = jnp.fft.fft(x.astype(jnp.complex64), n=n, axis=1)
        y = jnp.fft.ifft(x_f * kernel_f[None, :, :], axis=1)
        return y[:, :l, :].real.astype(x.dtype)

    def _L0_ffn_ref(x, Wr, W1, b1, W2, b2):
        import jax, jax.numpy as jnp
        import numpy as np
        B, T, D = (4, 2048, 128)
        E, F, CAP = (8, 512, 1024)
        Bb, Tt, Dd = x.shape
        N = Bb * Tt
        C = min(CAP, N)
        x_flat = x.reshape(N, Dd)
        logits = x_flat @ Wr
        probs = jax.nn.softmax(logits, axis=0)
        vals, idx = jax.lax.top_k(probs.T, C)
        selected = x_flat[idx]
        h = jax.nn.gelu(jnp.einsum('ecd,edf->ecf', selected, W1) + b1[:, None, :], approximate=False)
        out_e = jnp.einsum('ecf,efd->ecd', h, W2) + b2[:, None, :]
        weighted = vals[..., None] * out_e
        output = jnp.zeros_like(x_flat).at[idx.reshape(-1)].add(weighted.reshape(-1, Dd))
        return output.reshape(Bb, Tt, Dd)
    h = _L0_tok_ref(x)
    h = h + _L0_attn_ref(_layernorm(h, axis=-1), L0_attn_nu, L0_attn_theta, L0_attn_gamma_real, L0_attn_gamma_imag)
    h = h + _L0_ffn_ref(_layernorm(h, axis=-1), L0_ffn_Wr, L0_ffn_W1, L0_ffn_b1, L0_ffn_W2, L0_ffn_b2)
    return h

_drawn_inputs = setup_inputs


def setup_inputs(seed=0):
    import zlib

    import numpy as np

    out = dict(_drawn_inputs(seed))
    spreads = {}
    factors = {'L0_ffn_Wr': 64.0,
     'L0_ffn_W1': 64.0,
     'L0_ffn_b1': 64.0,
     'L0_ffn_W2': 64.0,
     'L0_ffn_b2': 64.0}
    for name, (base, spread) in spreads.items():
        noise = np.random.default_rng([zlib.crc32(name.encode()), seed]).standard_normal(out[name].shape)
        drawn = base * np.exp(spread * noise) if base else spread * noise
        out[name] = jnp.asarray(drawn.astype(out[name].dtype))
    for name, factor in factors.items():
        out[name] = (out[name] * factor).astype(out[name].dtype)
    return out
```

```python
from contextlib import ExitStack

import numpy as np
import concourse.bass as bass
from concourse import mybir

ALU = mybir.AluOpType
ACT = mybir.ActivationFunctionType
AX = mybir.AxisListType
F32 = mybir.dt.float32
F16 = mybir.dt.float16
I32 = mybir.dt.int32
U32 = mybir.dt.uint32

P = 128
D = 128
ROWS, SAMPLES = 32, 120000
FRAMES = SAMPLES // D + 1
TAIL = SAMPLES % D
CHUNKS = 8
L = -(-FRAMES // CHUNKS)
LAST = FRAMES - (CHUNKS - 1) * L
HB = ROWS // 2
COLS = HB * CHUNKS
PADDED = L * CHUNKS
EPS = 1e-5
E, F, CAP = 8, 512, 1024
FC = F // P
SEGS = P // E
SEG = ROWS * PADDED // SEGS
ROWS_SEG = ROWS // SEGS
FAR = 1e38
SLOT_TILES = CAP // P
RING = 16
DVE_TILES = 10

TWO_PI = 2 * np.pi
C1 = 6.28125
C2 = float(np.float32(int((TWO_PI - C1) * 2**21) / 2**21))
C3 = float(np.float32(TWO_PI - C1 - C2))
MAGIC = 1.5 * 2.0**23
PI_IN = 3.1415925


def constants():
    k, t = np.arange(D)[:, None].astype(np.float64), np.arange(D)[None, :].astype(np.float64)
    scale = np.full((D, 1), np.sqrt(2.0 / D))
    scale[0, 0] = np.sqrt(1.0 / D)
    basis = (scale * np.cos(np.pi * (2.0 * t + 1.0) * k / (2.0 * D))).astype(np.float32)
    p = np.arange(P)
    times = np.concatenate([np.arange(L + 1), np.arange(L - 1, -1, -1)])
    group = (p[:, None] // SEGS == p[None, :] // SEGS).astype(np.float32)
    block = np.arange(2 * P).reshape(2, P).T
    base = (block // CHUNKS) * FRAMES + (block % CHUNKS) * L
    parts = {
        "basis_t": basis.T,
        "identity": np.eye(P),
        "times": np.tile(times, (P, 1)),
        "ones": np.ones((P, P)),
        "group": group,
        "other_group": (group - 1) * 3e38,
        "before": (p[:, None] < p[None, :]),
        "first_of_expert": (p[:, None] == SEGS * np.arange(E)[None, :]),
        "slot_numbers": p[:, None] + P * np.arange(SLOT_TILES)[None, :],
        "base_high": base // P,
        "base_low": base % P,
        "bits": np.tile(np.int32(1) << np.arange(30, -1, -1, dtype=np.int32), (P, 1)).view(np.float32),
        "slots_row": np.tile(np.arange(CAP), (P, 1)),
    }
    table, at = [], {}
    n = 0
    for name, a in parts.items():
        a = np.ascontiguousarray(a, np.float32) if a.dtype != np.float32 else a
        at[name] = (n, n + a.shape[1])
        n += a.shape[1]
        table.append(a)
    return np.concatenate(table, axis=1), at


class Steps:

    def __init__(self, eng):
        self.eng, self.n, self.base = eng, 0, 0

    def one(self):
        self.n += 1
        return 1

    def all(self):
        return self.base + self.n

    def loop(self, start, end, per, peel=False):
        at = self.n
        first = start
        if peel:
            yield start
            assert self.n == at + per, (self.n - at, per)
            first = start + 1
        with self.eng.Fori(first, end) as i:
            self.base, self.n = i * per + (at - start * per), 0
            yield i
            assert self.n == per, (self.n, per)
        self.base, self.n = 0, at + (end - start) * per


def turns(eng, start, end, peel=False):
    if peel:
        yield start
        start += 1
    with eng.Fori(start, end) as i:
        yield i




def due(value):
    return not isinstance(value, int) or value > 0




def build(nc, x, nu, theta, gamma_r, gamma_i, Wr, W1, b1, W2, b2, out):
    table, at = constants()
    const_dram = nc.inline_tensor(table, name="constants").ap()
    zeros_dram = nc.inline_tensor(np.zeros((HB, D - TAIL), np.float32), name="zeros").ap()
    toeplitz = nc.dram_tensor("toeplitz", [L + 2, D, P], F32).ap()
    away_dram = nc.dram_tensor("away", [E, ROWS * PADDED], F32).ap()
    logits_dram = nc.dram_tensor("logits", [E, ROWS * PADDED], F32).ap()
    NC1 = at["slots_row"][0]
    NT = 2 * L + 1

    with ExitStack() as ctx:
        def sb(name, shape, dt=F32):
            return ctx.enter_context(nc.sbuf_tensor(name, shape, dt))

        const = sb("const", [P, NC1])
        cut = {n: const[:, a:b] for n, (a, b) in at.items() if b <= NC1}
        wr_pad = sb("wr_pad", [P, 32])
        mu = sb("mu", [P, 3])
        state_w = sb("state_w", [L, D, 2])
        powers = sb("powers", [P, HB])
        hid_all = sb("hid", [P, COLS, D])
        hid = hid_all[0:L]
        xn_all = sb("xn", [P, D, COLS])
        xn = xn_all[0:L + 2]
        ring = sb("ring", [L + 2, 2, RING, P])
        xin_all = sb("xin", [P, 2, HB, D])
        xin = xin_all[0:L]
        xt_all = sb("xt", [P, 2, 4 * D])
        xt = xt_all[:, :, 0:4 * L].rearrange("p s (a b) -> p s a b", a=4)
        scaled = sb("scaled", [L, 2, 4, D])
        stats = sb("stats", [L, 2, HB, 6])
        small = sb("small", [L, 2, 8, HB])
        lstage = sb("lstage", [P, 2, 4 * L])
        setup = sb("setup", [P, 6, L + P])
        par = sb("par", [P, 8])
        e2 = sb("e2", [P, 2, COLS])
        s2 = sb("s2", [P, 2, COLS])
        carry = sb("carry", [P, 2, HB])
        ebuf = xin[:, :, :, :].rearrange("p a b c -> p (a b c)").rearrange("p (r i n) -> p r i n", r=8, i=4)
        w1_ring = sb("w1_ring", [P, 2, F])
        w2_ring = sb("w2_ring", [P, 2, FC, D])
        b2_all = sb("b2_all", [P, E, D])
        wr_all = sb("wr_all", [P, D, E])
        b1_rows = sb("b1_rows", [E * FC, P])
        b1_now = sb("b1_now", [P, 2, FC])
        b1_cols = sb("b1_cols", [P, E * FC])

        free = {"hid": [hid_all[:, :, :].rearrange("p a b -> p (a b)"), 0],
                "xn": [xn_all[:, :, :].rearrange("p a b -> p (a b)"), 0],
                "xin": [xin_all[:, :, :, :].rearrange("p a b c -> p (a b c)"), 0],
                "setup": [setup[:, :, :].rearrange("p a b -> p (a b)"), 0]}

        def take(where, words):
            region, n = free[where]
            free[where][1] = n + words
            assert n + words <= region.shape[1], where
            return region[:, n:n + words]

        TB = 2 * E
        found = take("hid", E * SLOT_TILES * D).rearrange("p (a b) -> p a b", b=D)
        adds = take("hid", E * SLOT_TILES * D).rearrange("p (a b) -> p a b", b=D)
        far = take("xn", SEG)
        seen = take("xn", SEG)
        hidden = take("xn", 512)
        acts = xn_all[:, :, :].rearrange("p a b -> p (a b)")[:, 0:2 * FC * 512].rearrange(
            "p (s f n) -> p s f n", s=2, f=FC)
        gone = take("xn", TB * L).rearrange("p (a b) -> p a b", b=L)
        normed_at = free["xn"][1]
        below = take("xn", TB * L).rearrange("p (a b) -> p a b", b=L)
        equal = take("xn", TB * L).rearrange("p (a b) -> p a b", b=L)
        n_below = take("xn", TB * L).rearrange("p (a b) -> p a b", b=L)
        n_equal = take("xn", TB * L).rearrange("p (a b) -> p a b", b=L)
        keep = take("xin", TB * L).rearrange("p (a b) -> p a b", b=L)
        rank = take("xn", TB * (L + 2) // 2).bitcast(F16).rearrange("p (a b) -> p a b", b=L + 2)
        slots = take("setup", CAP)
        slots16 = take("xin", CAP // 2).bitcast(F16)
        onehot = take("xn", 2 * CAP // 2).bitcast(F16).rearrange("p (a b) -> p a b", b=CAP)
        from_lo = take("xin", CAP // 2).bitcast(F16)
        sc = sb("sc", [P, 96])
        tot = sb("tot", [P, 2, 16])
        off = sb("off", [P, 2, 16])
        spread = sb("spread", [P, 4, E])
        spread_in = sb("spread_in", [P, 4, E])
        blocks_ = sb("blocks_", [P, 4, TB])
        mrow = sb("mrow", [1, P])
        mall = take("xin", P)
        normed = xn_all[:, :, :].rearrange("p a b -> p (a b)")[
            :, normed_at:normed_at + 2 * SLOT_TILES * D].rearrange("p (s m d) -> p s m d", s=2, m=SLOT_TILES)
        edge = sb("edge", [P, 2, 2])
        marked = take("xin", 4 * L).rearrange("p (a b) -> p a b", b=L)
        place = sb("place", [P, 3, 4])
        base2 = sb("base2", [P, 4, 2])
        index = sb("index", [P, E * SLOT_TILES], I32)
        fstats = sb("fstats", [P, SLOT_TILES, 6])
        fsmall = sb("fsmall", [P, 2, 10, SLOT_TILES])
        banks = ctx.enter_context(nc.psum_tensor("banks", [P, 8, 512], F32))
        def sem(name):
            return ctx.enter_context(nc.semaphore(name))

        const_in = sem("const_in")
        params_in = sem("params_in")
        wr_in = sem("wr_in")
        a_ready = sem("a_ready")
        rate_ready = sem("rate_ready")
        decay_ready = sem("decay_ready")
        reduced_ready = sem("reduced_ready")
        trig_ready = sem("trig_ready")
        tables_ready = sem("tables_ready")
        turned_tables = sem("turned_tables")
        toeplitz_out = sem("toeplitz_out")
        state_w_ready = sem("state_w_ready")
        wr_sum = sem("wr_sum")
        wr_ready = sem("wr_ready")
        kernel_ready = sem("kernel_ready")
        powers_ready = sem("powers_ready")
        dve_own = sem("dve_own")
        xt_ready = sem("xt_ready")
        xt_copied = sem("xt_copied")
        h_ready = sem("h_ready")
        h_copied = sem("h_copied")
        var_ready = sem("var_ready")
        rstd_ready = sem("rstd_ready")
        nb_ready = sem("nb_ready")
        xn_dve = sem("xn_dve")
        xn_act = sem("xn_act")
        e_ready = sem("e_ready")
        e_copied = sem("e_copied")
        e_moved = sem("e_moved")
        s_ready = sem("s_ready")
        s_moved = sem("s_moved")
        y_ready = sem("y_ready")
        y_added = sem("y_added")
        var2_ready = sem("var2_ready")
        rstd2_ready = sem("rstd2_ready")
        scaled_ready = sem("scaled_ready")
        t2_ready = sem("t2_ready")
        t2_copied = sem("t2_copied")
        l_used = sem("l_used")
        l_copied = sem("l_copied")
        rows_out = sem("rows_out")
        vectors_in = sem("vectors_in")
        logits_in = sem("logits_in")
        far_ready = sem("far_ready")
        far_out = sem("far_out")
        gone_in = sem("gone_in")
        sum_ready = sem("sum_ready")
        b1_turned = sem("b1_turned")
        b1_ready = sem("b1_ready")
        peak_ready = sem("peak_ready")
        peak_turned = sem("peak_turned")
        peak_row = sem("peak_row")
        peak_spread = sem("peak_spread")
        sum_spread = sem("sum_spread")
        count_ready = sem("count_ready")
        count_spread = sem("count_spread")
        spread_in_ready = sem("spread_in_ready")
        spread_done = sem("spread_done")
        totals_ready = sem("totals_ready")
        offsets_ready = sem("offsets_ready")
        onehot_half = sem("onehot_half")
        onehot_ready = sem("onehot_ready")
        row_ready = sem("row_ready")
        row_used = sem("row_used")
        index_ready = sem("index_ready")
        var3_ready = sem("var3_ready")
        rstd3_ready = sem("rstd3_ready")
        norm_ready = sem("norm_ready")
        score_ready = sem("score_ready")
        weight_ready = sem("weight_ready")
        ft_ready = sem("ft_ready")
        ft_copied = sem("ft_copied")
        up_ready = sem("up_ready")
        gelu_ready = sem("gelu_ready")
        down_ready = sem("down_ready")
        down_copied = sem("down_copied")
        adds_ready = sem("adds_ready")
        added = sem("added")
        x_in = [sem(f"x_in{slot}") for slot in range(2)]
        ring_in = [sem(f"ring_in{slot}") for slot in range(2)]
        l_out = [sem(f"l_out{slot}") for slot in range(2)]
        weights_in = [sem(f"weights_in{slot}") for slot in range(2)]
        found_in = [sem(f"found_in{slot}") for slot in range(2)]

        def frames(h, c, rows):
            return bass.AP(x.tensor, c * (L * D) + h * HB * SAMPLES, [[D, rows], [SAMPLES, HB], [1, D]])

        def out_rows(h, c, rows):
            return bass.AP(out.tensor, c * (L * D) + h * HB * FRAMES * D, [[D, rows], [FRAMES * D, HB], [1, D]])

        R_, ANG, RED, SIN, COS, Q = (setup[:, n, 0:NT] for n in range(6))
        KPAD = setup[:, 0, 0:L - 1 + P]

        block = ctx.enter_context(nc.Block())

        @block.sync
        def _(sp):
            sp.dma_start(const[:, :], const_dram[:, 0:NC1]).then_inc(const_in, 16)
            for n, v in enumerate((nu, theta, gamma_r, gamma_i)):
                sp.dma_start(par[:, n:n + 1], v.rearrange("(p a) -> p a", a=1)).then_inc(params_in, 16)
            sp.dma_start(wr_pad[:, 0:E], Wr).then_inc(wr_in, 16)
            step = setup[:, 0, :].ap[0][0]

            def toeplitz_rows(j):
                rows = bass.AP(KPAD.tensor, KPAD.offset + 16 * j * step + L - 1, [[step, 16], [-1, L], [1, P]])
                sp.dma_start(bass.AP(toeplitz.tensor, 16 * j * P, [[P, 16], [D * P, L], [1, P]]),
                             rows).then_inc(toeplitz_out, 16)

            for h in range(2):
                if h:
                    sp.wait_ge(e_moved, 128 * h)
                for cc in turns(sp, 0, CHUNKS // 2 - 1, peel=h == 0):
                    for slot in range(2):
                        if due(8 * cc + (4 * slot + 32 * h - 4)):
                            sp.wait_ge(xt_ready, 8 * cc + (4 * slot + 32 * h - 4))
                        sp.dma_start(xin[:, slot], frames(h, 2 * cc + slot, L)).then_inc(x_in[slot], 16)
                        if h == 0 and isinstance(cc, int) and slot:
                            sp.wait_ge(kernel_ready, 4)
                            for j in range(D // 16):
                                toeplitz_rows(j)
                            sp.dma_start(bass.AP(toeplitz.tensor, L * D * P, [[P, D], [D * P, 2], [1, P]]),
                                         setup[:, 3:5, 1:P + 1]).then_inc(toeplitz_out, 16)
                sp.wait_ge(xt_ready, 32 * h + 20)
                sp.dma_start(xin[:, 0], frames(h, CHUNKS - 2, L)).then_inc(x_in[0], 16)
                sp.wait_ge(xt_ready, 32 * h + 24)
                sp.dma_start(xin[0:LAST - 1, 1], frames(h, CHUNKS - 1, LAST - 1)).then_inc(x_in[1], 16)
                tail = bass.AP(x.tensor, h * HB * SAMPLES + (FRAMES - 1) * D, [[1, 1], [SAMPLES, HB], [1, TAIL]])
                sp.dma_start(xin[LAST - 1:LAST, 1, :, 0:TAIL], tail).then_inc(x_in[1], 16)
                sp.dma_start(xin[LAST - 1:LAST, 1, :, TAIL:D],
                             zeros_dram.rearrange("(a b) c -> a b c", a=1)).then_inc(x_in[1], 16)

                if h == 0:
                    sp.wait_ge(toeplitz_out, 16 * 9)
                def fill(i, slot):
                    if due(8 * i + (4 * slot + 32 * h - 4)):
                        sp.wait_ge(y_ready, 8 * i + (4 * slot + 32 * h - 4))
                    sp.dma_start(ring[:, slot].rearrange("p k t -> p (k t)"), bass.AP(
                        toeplitz.tensor, i * (2 * RING * P) + slot * RING * P,
                        [[D * P, L + 2], [1, RING * P]])).then_inc(ring_in[slot], 16)

                for slot in range(2):
                    fill(0, slot)

                sp.wait_ge(e_copied, 8 * (h + 1))
                for j in range(4):
                    for ri in range(2):
                        sp.dma_start(e2[32 * j:32 * j + 32, ri, :],
                                     ebuf[32 * j + ri:32 * j + ri + 1]).then_inc(e_moved, 16)
                sp.wait_ge(s_ready, h + 1)
                if due(32 * h):
                    sp.wait_ge(y_ready, 32 * h)
                for ri in range(2):
                    sp.dma_start(xn[L + ri:L + ri + 1, :, :], s2[:, ri, :]).then_inc(s_moved, 16)

                with sp.Fori(1, D // RING // 2) as i:
                    for slot in range(2):
                        fill(i, slot)

                def store_logits(c, slot):
                    for j in range(4):
                        sp.dma_start(
                            bass.AP(logits_dram.tensor, c * L + (h * HB + 4 * j) * PADDED,
                                    [[ROWS * PADDED, E], [PADDED, 4], [1, L]]),
                            lstage[32 * j:32 * j + E, slot, :].rearrange("p (b t) -> p b t", b=4),
                        ).then_inc(l_out[slot], 16)

                sp.wait_ge(y_added, 32 * (h + 1))
                for cc in turns(sp, 0, CHUNKS // 2 - 1):
                    for slot in range(2):
                        c = 2 * cc + slot
                        sp.dma_start(out_rows(h, c, L), hid[:, bass.ds(c * HB, HB), :]).then_inc(rows_out, 16)
                        sp.wait_ge(l_copied, 2 * cc + (slot + CHUNKS * h + 1))
                        store_logits(c, slot)
                for slot, rows in ((0, L), (1, LAST)):
                    c = CHUNKS - 2 + slot
                    sp.dma_start(out_rows(h, c, rows), hid[0:rows, HB * c:HB * (c + 1), :]).then_inc(rows_out, 16)
                    sp.wait_ge(l_copied, c + 1 + CHUNKS * h)
                    store_logits(c, slot)
            sp.dma_start(b2_all[:, :, :].rearrange("p e d -> p (e d)"),
                         bass.AP(b2.tensor, 0, [[0, P], [1, E * D]])).then_inc(vectors_in, 16)
            sp.dma_start(wr_all[:, :, :].rearrange("p d e -> p (d e)"),
                         bass.AP(Wr.tensor, 0, [[0, P], [1, E * D]])).then_inc(vectors_in, 16)
            sp.dma_start(b1_rows[:, :], b1.rearrange("e (f p) -> (e f) p", p=P)).then_inc(vectors_in, 16)
            sp.wait_ge(toeplitz_out, 16 * 9)
            sp.wait_ge(kernel_ready, 4)
            sp.dma_start(slots, const_dram[:, NC1:NC1 + CAP]).then_inc(vectors_in, 16)

            def weights(e, slot):
                sp.dma_start(w1_ring[:, slot], bass.AP(W1.tensor, e * (D * F) + slot * D * F,
                                                       [[F, D], [1, F]])).then_inc(weights_in[slot], 16)
                sp.dma_start(w2_ring[:, slot], bass.AP(W2.tensor, e * (D * F) + slot * D * F,
                                                       [[D, P], [P * D, FC], [1, D]])).then_inc(weights_in[slot], 16)

            for slot in range(2):
                weights(0, slot)
            sp.wait_ge(rows_out, 16 * 16)
            sp.wait_ge(l_out[0], 64 * 8)
            sp.wait_ge(l_out[1], 64 * 8)
            sp.wait_ge(y_ready, 64)
            sp.dma_start(far, logits_dram.rearrange("e (s n) -> (e s) n", n=SEG)).then_inc(logits_in, 16)
            sp.wait_ge(far_ready, 1)
            sp.dma_start(away_dram.rearrange("e (s n) -> (e s) n", n=SEG), far).then_inc(far_out, 16)
            sp.wait_ge(far_out, 16)
            for half in range(2):
                sp.dma_start(gone[:, half * E:(half + 1) * E, :],
                             bass.AP(away_dram.tensor, half * P * L, [[L, P], [ROWS * PADDED, E], [1, L]])
                             ).then_inc(gone_in, 16)
            with sp.Fori(1, E // 2) as i:
                for slot in range(2):
                    sp.wait_ge(down_ready, i * 4 + (2 * slot - 2))
                    weights(i * 2, slot)

        @block.scalar
        def _(act):
            act.wait_ge(params_in, 64)
            act.activation(par[:, 4:5], par[:, 0:1], ACT.Exp).then_inc(a_ready, 1)
            act.wait_ge(const_in, 16)
            act.wait_ge(rate_ready, 1)
            act.activation(R_, cut["times"], ACT.Exp, scale=par[:, 5:6]).then_inc(decay_ready, 1)
            act.wait_ge(reduced_ready, 1)
            act.activation(SIN, RED, ACT.Sin).then_inc(trig_ready, 1)
            act.wait_ge(reduced_ready, 2)
            act.activation(COS, ANG, ACT.Sin).then_inc(trig_ready, 1)
            for n in range(2):
                act.wait_ge(turned_tables, n + 1)
                act.activation(state_w[:, :, n], banks[0:L, n, 0:D], ACT.Copy).then_inc(state_w_ready, 1)
            for h in range(2):
                def copy_xt(n, G):
                    act.wait_ge(xt_ready, G + 1)
                    if due(G - 1):
                        act.wait_ge(h_ready, G - 1)
                    act.activation(xt[:, n % 2], banks[:, n % 2, 0:4 * L].rearrange("p (a b) -> p a b", a=4),
                                   ACT.Copy).then_inc(xt_copied, 1)

                def copy_h(n, G, cc):
                    act.wait_ge(h_ready, G + 1)
                    act.activation(hid[:, bass.ds(cc * (2 * HB) + 4 * n, 4), :],
                                   banks[0:L, 2 + n % 2, :].rearrange("p (a b) -> p a b", a=4),
                                   ACT.Copy).then_inc(h_copied, 1)

                def normalise(cc, slot):
                    act.wait_ge(nb_ready, 2 * cc + (slot + CHUNKS * h + 1))
                    for b in range(DVE_TILES, HB):
                        col = cc * (2 * HB) + (HB * slot + b)
                        ins = act.activation(xn[0:L, :, bass.ds(col, 1)].rearrange("p k a -> p (k a)"),
                                             hid[:, bass.ds(col, 1), :].rearrange("p a k -> p (a k)"),
                                             ACT.Identity, bias=small[:, slot, 6, b:b + 1],
                                             scale=small[:, slot, 4, b:b + 1])
                    ins.then_inc(xn_act, 1)

                if h:
                    act.wait_ge(rows_out, 16 * CHUNKS)
                    act.wait_ge(scaled_ready, 4 * CHUNKS)
                    act.wait_ge(l_used, 4 * CHUNKS)
                for cc in turns(act, 0, CHUNKS // 2, peel=h == 0):
                    G0 = 8 * cc + 32 * h
                    copy_xt(0, G0)
                    for n in range(8):
                        if n < 7:
                            copy_xt(n + 1, G0 + (n + 1))
                        copy_h(n, G0 + n, cc)
                        if n % 4 == 3:
                            normalise(cc, n // 4)

                for r in range(8):
                    act.wait_ge(e_ready, 8 * h + r + 1)
                    act.activation(ebuf[0:98, r], banks[0:98, 6 + r % 2, :].rearrange("p (a b) -> p a b", a=4),
                                   ACT.Copy).then_inc(e_copied, 1)

                for cc in turns(act, 0, CHUNKS // 2, peel=h == 0):
                    for slot in range(2):
                        it = 2 * cc + (slot + CHUNKS * h)
                        for n in range(4):
                            G = 4 * it + n
                            act.wait_ge(t2_ready, G + 1)
                            if due(G - 1):
                                act.wait_ge(l_used, G - 1)
                            act.activation(xt[:, n % 2], banks[:, n % 2, 0:4 * L].rearrange("p (a b) -> p a b", a=4),
                                           ACT.Copy).then_inc(t2_copied, 1)
                        act.wait_ge(l_used, 4 * it + 4)
                        if due(64 * cc + 256 * h):
                            act.wait_ge(l_out[slot], 64 * cc + 256 * h)
                        act.activation(lstage[:, slot], banks[:, 4 + slot, 0:4 * L], ACT.Copy).then_inc(l_copied, 1)

            act.wait_ge(far_ready, 1)
            act.activation(seen, far, ACT.Exp, scale=-1.0, accum_out=sc[:, 4:5]).then_inc(sum_ready, 1)
            act.wait_ge(b1_turned, 1)
            act.activation(b1_cols[:, :], banks[:, 2, 0:E * FC], ACT.Copy).then_inc(b1_ready, 1)
            for i in turns(act, 0, E // 2, peel=True):
                for slot in range(2):
                    act.wait_ge(score_ready, i * 2 + (slot + 1))
                    act.activation(fsmall[:, slot, 8, :], fsmall[:, slot, 7, :], ACT.Exp).then_inc(weight_ready, 1)
                    for g in range(2):
                        n = 2 * slot + g
                        act.wait_ge(ft_ready, i * 4 + (n + 1))
                        act.activation(xt_all[:, g], banks[:, 0, :], ACT.Copy).then_inc(ft_copied, 1)
                        if due(i * 4 + (n - 1)):
                            act.wait_ge(down_ready, i * 4 + (n - 1))
                        for f in range(FC):
                            act.wait_ge(up_ready, i * 16 + (4 * n + f + 1))
                            act.activation(acts[:, g, f], banks[:, 1 + f, :], ACT.Gelu,
                                           bias=b1_now[:, slot, f:f + 1]
                                           ).then_inc(gelu_ready, 1)

        @block.tensor
        def _(pe):
            pe.wait_ge(const_in, 16)
            pe.wait_ge(wr_in, 16)
            pe.matmul(banks[:, 2, 0:E], cut["ones"], wr_pad[:, 0:E], start=True, stop=True).then_inc(wr_sum, 1)
            pe.wait_ge(tables_ready, 2)
            for n, src in enumerate((ANG, RED)):
                pe.transpose(banks[0:L, n, 0:D], src[:, L + 1:NT], cut["identity"]).then_inc(turned_tables, 1)
            pe.wait_ge(state_w_ready, 2)
            pe.wait_ge(wr_ready, 2)
            for h in range(2):
                def turn(n, G, cc, x1):
                    if n == 0:
                        pe.wait_ge(x_in[0], 16 * cc + (64 * h + 16))
                    if n == 4:
                        pe.wait_ge(x_in[1], x1)
                    if due(G - 1):
                        pe.wait_ge(xt_copied, G - 1)
                    for i in range(4):
                        mm = pe.transpose(banks[:, n % 2, i * L:(i + 1) * L], xin[:, n // 4, 4 * (n % 4) + i, :],
                                          cut["identity"][0:L, 0:L])
                    mm.then_inc(xt_ready, 1)

                def dct(n, G):
                    pe.wait_ge(xt_copied, G + 1)
                    if due(G - 1):
                        pe.wait_ge(h_copied, G - 1)
                    for i in range(4):
                        mm = pe.matmul(banks[0:L, 2 + n % 2, i * D:(i + 1) * D], xt[:, n % 2, i, :],
                                       cut["basis_t"], start=True, stop=True)
                    mm.then_inc(h_ready, 1)

                def eight(cc, x1):
                    G0 = 8 * cc + 32 * h
                    turn(0, G0, cc, x1)
                    for n in range(8):
                        if n < 7:
                            turn(n + 1, G0 + (n + 1), cc, x1)
                        dct(n, G0 + n)

                if due(32 * h):
                    pe.wait_ge(t2_copied, 32 * h)
                for cc in turns(pe, 0, CHUNKS // 2 - 1, peel=h == 0):
                    eight(cc, 16 * cc + (96 * h + 16))
                eight(CHUNKS // 2 - 1, 96 * h + 96)

                pe.wait_ge(xn_dve, CHUNKS * (h + 1))
                pe.wait_ge(xn_act, CHUNKS * (h + 1))
                for r in range(8):
                    if due(8 * h + r - 1):
                        pe.wait_ge(e_copied, 8 * h + r - 1)
                    for i in range(4):
                        for j in range(4):
                            k = 32 * j + 4 * r + i
                            mm = pe.matmul(banks[32 * j:32 * j + 2, 6 + r % 2, i * COLS:(i + 1) * COLS],
                                           state_w[:, k, :], xn[0:L, k, :], start=True, stop=True)
                    mm.then_inc(e_ready, 1)

                if due(CHUNKS * h):
                    pe.wait_ge(l_copied, CHUNKS * h)
                pe.wait_ge(s_moved, 32 * (h + 1))
                for i in turns(pe, 0, D // RING // 2, peel=h == 0):
                    for slot in range(2):
                        pe.wait_ge(ring_in[slot], 16 * i + (64 * h + 16))
                        for g in range(4):
                            if due(8 * i + (4 * slot + g + 32 * h - 1)):
                                pe.wait_ge(y_added, 8 * i + (4 * slot + g + 32 * h - 1))
                            for q in range(4):
                                kk = RING * slot + 4 * g + q
                                mm = pe.matmul(banks[0:L, 4 + g % 2, q * COLS:(q + 1) * COLS], ring[:, slot, 4 * g + q, 0:L],
                                               xn[:, bass.ds(i * (2 * RING) + kk, 1), :].rearrange("p a n -> p (a n)"),
                                               start=True, stop=True)
                            mm.then_inc(y_ready, 1)

                def turn2(n, G):
                    pe.wait_ge(scaled_ready, G + 1)
                    if due(G - 1):
                        pe.wait_ge(t2_copied, G - 1)
                    for i in range(4):
                        mm = pe.transpose(banks[:, n % 2, i * L:(i + 1) * L], scaled[:, n % 2, i, :],
                                          cut["identity"][0:L, 0:L])
                    mm.then_inc(t2_ready, 1)

                def logits(n, G, it):
                    pe.wait_ge(t2_copied, G + 1)
                    if n % 4 == 0:
                        if due(it - 1):
                            pe.wait_ge(l_copied, it - 1)
                    j = n % 4
                    pe.matmul(banks[32 * j:32 * j + 32, 4 + n // 4, 0:4 * L], wr_pad[:, :],
                              xt_all[:, n % 2, 0:4 * L], start=True, stop=True).then_inc(l_used, 1)

                pe.wait_ge(y_added, 32 * (h + 1))
                for cc in turns(pe, 0, CHUNKS // 2, peel=h == 0):
                    G0 = 8 * cc + 32 * h
                    turn2(0, G0)
                    for n in range(8):
                        if n < 7:
                            turn2(n + 1, G0 + (n + 1))
                        logits(n, G0 + n, 2 * cc + (n // 4 + CHUNKS * h))

            pe.wait_ge(peak_ready, 1)
            pe.wait_ge(l_copied, 16)
            pe.transpose(banks[0:1, 0, 0:P], sc[:, 0:1], cut["identity"]).then_inc(peak_turned, 1)
            pe.wait_ge(peak_row, 1)
            pe.matmul(banks[:, 1, 0:P], cut["ones"][0:1, :], mrow[:, :], start=True, stop=True).then_inc(peak_spread, 1)
            pe.wait_ge(vectors_in, 64)
            pe.transpose(banks[:, 2, 0:E * FC], b1_rows[:, :], cut["identity"][0:E * FC, 0:E * FC]).then_inc(b1_turned, 1)
            pe.wait_ge(sum_ready, 1)
            pe.matmul(banks[:, 3, 0:1], cut["group"], sc[:, 4:5], start=True, stop=True).then_inc(sum_spread, 1)
            for i in turns(pe, 0, 32):
                pe.wait_ge(count_ready, i + 1)
                pe.matmul(banks[:, 4, 0:1], cut["group"], sc[:, 2:3], start=True, stop=True).then_inc(count_spread, 1)
            pe.wait_ge(spread_in_ready, 1)
            pe.matmul(banks[:, 5, 0:4 * E], cut["ones"], spread_in[:, :, :].rearrange("p a b -> p (a b)"),
                      start=True, stop=True).then_inc(spread_done, 1)
            pe.wait_ge(totals_ready, 2)
            pe.matmul(banks[:, 6, 0:32], cut["before"], tot[:, :, :].rearrange("p a b -> p (a b)"), start=True, stop=False)
            pe.matmul(banks[:, 6, 16:32], cut["ones"], tot[:, 0, :], start=False, stop=True).then_inc(offsets_ready, 1)
            for e in turns(pe, 0, E, peel=True):
                pe.wait_ge(onehot_ready, e + 1)
                for q in range(2):
                    if due(e * 2 + q):
                        pe.wait_ge(row_used, e * 2 + q)
                    for m in range(4):
                        for half in range(2):
                            mm = pe.matmul(banks[:, 7, m * (L + 2):(m + 1) * (L + 2)],
                                           onehot[:, half, (4 * q + m) * P:(4 * q + m + 1) * P],
                                           rank[:, bass.ds(e + half * E, 1), :].rearrange("p a b -> p (a b)"),
                                           start=half == 0, stop=half == 1)
                    mm.then_inc(row_ready, 1)

            def ffn_turn(n, i):
                slot, g = n // 2, n % 2
                pe.wait_ge(norm_ready, i * 2 + (slot + 1))
                if due(i * 4 + n):
                    pe.wait_ge(ft_copied, i * 4 + n)
                for m in range(4):
                    mm = pe.transpose(banks[:, 0, m * P:(m + 1) * P], normed[:, slot, 4 * g + m, :], cut["identity"])
                mm.then_inc(ft_ready, 1)

            for i in turns(pe, 0, E // 2, peel=True):
                ffn_turn(0, i)
                for n in range(4):
                    slot, g = n // 2, n % 2
                    if g == 0:
                        pe.wait_ge(weights_in[slot], i * 32 + 32)
                    pe.wait_ge(ft_copied, i * 4 + (n + 1))
                    if due(i * 16 + 4 * n):
                        pe.wait_ge(gelu_ready, i * 16 + 4 * n)
                    for f in range(FC):
                        pe.matmul(banks[:, 1 + f, :], w1_ring[:, slot, f * P:(f + 1) * P], xt_all[:, g],
                                  start=True, stop=True).then_inc(up_ready, 1)
                    if n < 3:
                        ffn_turn(n + 1, i)
                    pe.wait_ge(gelu_ready, i * 16 + (4 * n + 4))
                    if due(i * 4 + (n - 1)):
                        pe.wait_ge(down_copied, i * 4 + (n - 1))
                    for m in range(4):
                        for f in range(FC):
                            mm = pe.matmul(banks[:, 5 + g, m * D:(m + 1) * D], acts[:, g, f, m * P:(m + 1) * P],
                                           w2_ring[:, slot, f, :], start=f == 0, stop=f == FC - 1)
                    mm.then_inc(down_ready, 1)

        @block.vector
        def _(dve):
            own = Steps(dve)
            dve.memset(banks[0:98, 6:8, :], 0.0)
            dve.memset(s2[:, :, 0:HB], 0.0)
            dve.memset(wr_pad[:, E:32], 0.0).then_inc(wr_ready, 1)
            dve.wait_ge(wr_sum, 1)
            dve.scalar_tensor_tensor(wr_pad[:, 0:E], banks[:, 2, 0:E], -1.0 / D, wr_pad[:, 0:E],
                                     ALU.mult, ALU.add).then_inc(wr_ready, 1)
            dve.wait_ge(params_in, 64)
            dve.wait_ge(a_ready, 1)
            dve.tensor_scalar(par[:, 5:6], par[:, 4:5], -1.0, None, ALU.mult).then_inc(rate_ready, 1)
            dve.wait_ge(const_in, 16)
            dve.tensor_scalar(ANG, cut["times"], par[:, 1:2], None, ALU.mult).then_inc(dve_own, own.one())
            for n, (dst, quarter) in enumerate(((RED, 0.0), (ANG, 0.25))):
                dve.wait_ge(dve_own, own.all())
                dve.tensor_scalar(Q, ANG, float(1 / TWO_PI), quarter, ALU.mult, ALU.add).then_inc(dve_own, own.one())
                dve.wait_ge(dve_own, own.all())
                dve.tensor_scalar(Q, Q, MAGIC, -MAGIC, ALU.add, ALU.add).then_inc(dve_own, own.one())
                src = ANG
                for part in (C1, C2, C3):
                    dve.wait_ge(dve_own, own.all())
                    dve.scalar_tensor_tensor(dst, Q, -part, src, ALU.mult, ALU.add).then_inc(dve_own, own.one())
                    src = dst
                if n:
                    dve.wait_ge(dve_own, own.all())
                    dve.tensor_scalar(dst, dst, float(np.pi / 2), None, ALU.add).then_inc(dve_own, own.one())
                dve.wait_ge(dve_own, own.all())
                dve.tensor_scalar(dst, dst, PI_IN, -PI_IN, ALU.min, ALU.max).then_inc(reduced_ready, 1)
            dve.wait_ge(decay_ready, 1)
            dve.wait_ge(trig_ready, 2)
            dve.tensor_tensor(ANG, COS, R_, ALU.mult).then_inc(tables_ready, 1)
            dve.tensor_tensor(RED, SIN, R_, ALU.mult).then_inc(tables_ready, 1)
            dve.wait_ge(tables_ready, 2)
            dve.tensor_copy(mu[:, 0:1], ANG[:, L:L + 1]).then_inc(dve_own, own.one())
            dve.tensor_copy(mu[:, 1:2], RED[:, L:L + 1]).then_inc(dve_own, own.one())
            dve.tensor_scalar(mu[:, 2:3], RED[:, L:L + 1], -1.0, None, ALU.mult).then_inc(dve_own, own.one())
            N1 = L + 1
            dve.tensor_scalar(Q[:, 0:N1], RED[:, 0:N1], par[:, 3:4], None, ALU.mult).then_inc(dve_own, own.one())
            dve.memset(KPAD[:, 0:L - 1], 0.0).then_inc(dve_own, own.one())
            dve.memset(KPAD[:, 2 * L - 1:], 0.0)
            dve.memset(setup[:, 3:5, L + 1:P + 1], 0.0).then_inc(kernel_ready, 1)
            dve.wait_ge(dve_own, own.all())
            dve.scalar_tensor_tensor(SIN[:, 0:N1], ANG[:, 0:N1], par[:, 2:3], Q[:, 0:N1],
                                     ALU.mult, ALU.subtract).then_inc(kernel_ready, 1)
            dve.wait_ge(kernel_ready, 2)
            dve.tensor_scalar(Q[:, 0:N1], ANG[:, 0:N1], par[:, 3:4], None, ALU.mult).then_inc(dve_own, own.one())
            dve.tensor_copy(KPAD[:, L - 1:2 * L - 1], SIN[:, 0:L]).then_inc(kernel_ready, 1)
            dve.wait_ge(dve_own, own.all())
            dve.scalar_tensor_tensor(COS[:, 0:N1], RED[:, 0:N1], par[:, 2:3], Q[:, 0:N1], ALU.mult, ALU.add).then_inc(dve_own, own.one())
            dve.wait_ge(dve_own, own.all())
            dve.tensor_scalar(COS[:, 0:N1], COS[:, 0:N1], -1.0, None, ALU.mult).then_inc(kernel_ready, 1)

            def moments(cols, slot, ready):
                for b in range(HB):
                    ins = dve.bn_stats(stats[:, slot, b, :], hid[:, bass.ds(cols + b, 1), :].rearrange("p a k -> p (a k)"))
                ins.then_inc(dve_own, own.one())
                dve.wait_ge(dve_own, own.all())
                mean0, sq0, mean1, sq1 = (stats[:, slot, :, n] for n in (1, 2, 4, 5))
                diff, total, var, mean_sum, _, mean = (small[:, slot, n, :] for n in range(6))
                dve.tensor_tensor(diff, mean0, mean1, ALU.subtract).then_inc(dve_own, own.one())
                dve.tensor_tensor(total, sq0, sq1, ALU.add).then_inc(dve_own, own.one())
                dve.tensor_tensor(mean_sum, mean0, mean1, ALU.add).then_inc(dve_own, own.one())
                dve.wait_ge(dve_own, own.all())
                dve.tensor_tensor(diff, diff, diff, ALU.mult).then_inc(dve_own, own.one())
                dve.tensor_scalar(mean, mean_sum, 0.5, None, ALU.mult).then_inc(dve_own, own.one())
                dve.wait_ge(dve_own, own.all())
                dve.scalar_tensor_tensor(total, diff, D / 4.0, total, ALU.mult, ALU.add).then_inc(dve_own, own.one())
                dve.wait_ge(dve_own, own.all())
                dve.tensor_scalar(var, total, 1.0 / D, EPS, ALU.mult, ALU.add).then_inc(ready, 1)

            for h in range(2):
                if due(32 * h):
                    dve.wait_ge(y_ready, 32 * h)
                for cc in own.loop(0, CHUNKS // 2, 14, peel=h == 0):
                    for slot in range(2):
                        it = 2 * cc + (slot + CHUNKS * h)
                        dve.wait_ge(h_copied, 4 * it + 4)
                        if due(it - 1):
                            dve.wait_ge(xn_act, it - 1)
                        if due(32 * h):
                            dve.wait_ge(scaled_ready, 32 * h)
                        moments(cc * (2 * HB) + HB * slot, slot, var_ready)
                        dve.wait_ge(rstd_ready, it + 1)
                        own_nb = small[:, slot, 6, :]
                        dve.scalar_tensor_tensor(own_nb, small[:, slot, 5, :], -1.0, small[:, slot, 4, :],
                                                 ALU.mult, ALU.mult).then_inc(nb_ready, 1)
                        for b in range(DVE_TILES):
                            col = cc * (2 * HB) + (HB * slot + b)
                            ins = dve.tensor_scalar(xn[0:L, :, bass.ds(col, 1)].rearrange("p k a -> p (k a)"),
                                                    hid[:, bass.ds(col, 1), :].rearrange("p a k -> p (a k)"),
                                                    small[:, slot, 5, b:b + 1], small[:, slot, 4, b:b + 1],
                                                    ALU.subtract, ALU.mult)
                        ins.then_inc(xn_dve, 1)

                dve.wait_ge(e_moved, 128 * (h + 1))
                if due(32 * h):
                    dve.wait_ge(s_moved, 32 * h)
                def state(ri, c):
                    return s2[:, ri, HB * c:HB * (c + 1)]
                for ri in range(2):
                    dve.tensor_copy(state(ri, 1), e2[:, ri, 0:HB]).then_inc(dve_own, own.one())
                for c in range(2, CHUNKS):
                    dve.wait_ge(dve_own, own.all())
                    for ri in range(2):
                        dve.scalar_tensor_tensor(carry[:, ri, :], state(0, c - 1), mu[:, (0, 1)[ri]:(0, 1)[ri] + 1],
                                                 e2[:, ri, HB * (c - 1):HB * c], ALU.mult, ALU.add).then_inc(dve_own, own.one())
                    dve.wait_ge(dve_own, own.all())
                    for ri in range(2):
                        m = (2, 0)[ri]
                        dve.scalar_tensor_tensor(state(ri, c), state(1, c - 1), mu[:, m:m + 1],
                                                 carry[:, ri, :], ALU.mult, ALU.add).then_inc(dve_own, own.one())
                dve.wait_ge(dve_own, own.all())
                dve.nop().then_inc(s_ready, 1)

                for i in turns(dve, 0, D // RING // 2):
                    for n in range(8):
                        dve.wait_ge(y_ready, 8 * i + (n + 32 * h + 1))
                        rows = hid[:, :, bass.ds(i * (2 * RING) + 4 * n, 4)]
                        dve.tensor_tensor(rows, rows, banks[0:L, 4 + n % 2, :].rearrange("p (k n) -> p n k", k=4),
                                          ALU.add).then_inc(y_added, 1)
                dve.wait_ge(y_added, 32 * (h + 1))
                for cc in own.loop(0, CHUNKS // 2, 14, peel=h == 0):
                    for slot in range(2):
                        it = 2 * cc + (slot + CHUNKS * h)
                        if due(4 * it - 4):
                            dve.wait_ge(scaled_ready, 4 * it - 4)
                        moments(cc * (2 * HB) + HB * slot, slot, var2_ready)

            dve.wait_ge(logits_in, 16)
            dve_far = far.rearrange("p (r n) -> p r n", r=ROWS_SEG)
            dve.memset(dve_far[:, :, FRAMES:PADDED], -FAR).then_inc(dve_own, own.one())
            dve.wait_ge(dve_own, own.all())
            dve.tensor_reduce(sc[:, 0:1], far, AX.X, ALU.max).then_inc(peak_ready, 1)
            dve.wait_ge(peak_turned, 1)
            dve.tensor_copy(mrow[:, :], banks[0:1, 0, 0:P]).then_inc(peak_row, 1)
            dve.wait_ge(peak_spread, 1)
            dve.tensor_tensor(mall, banks[:, 1, 0:P], cut["group"], ALU.mult).then_inc(dve_own, own.one())
            dve.wait_ge(dve_own, own.all())
            dve.tensor_tensor(mall, mall, cut["other_group"], ALU.add).then_inc(dve_own, own.one())
            dve.wait_ge(dve_own, own.all())
            dve.tensor_reduce(sc[:, 1:2], mall, AX.X, ALU.max).then_inc(dve_own, own.one())
            dve.wait_ge(dve_own, own.all())
            dve.tensor_scalar(far, far, -1.0, sc[:, 1:2], ALU.mult, ALU.add).then_inc(far_ready, 1)
            dve.wait_ge(sum_spread, 1)
            dve.reciprocal(sc[:, 5:6], banks[:, 3, 0:1]).then_inc(dve_own, own.one())

            prefix, trial = sc[:, 8:9].bitcast(I32), sc[:, 9:10].bitcast(I32)
            fewer = sc[:, 10:11].bitcast(I32)
            bits = cut["bits"].bitcast(I32)
            dve.memset(sc[:, 8:9], 0.0).then_inc(dve_own, own.one())
            dve.wait_ge(far_ready, 1)
            dve.wait_ge(sum_ready, 1)
            for i in own.loop(0, 31, 3, peel=False):
                dve.wait_ge(dve_own, own.all())
                dve.tensor_tensor(trial, prefix, bits[:, bass.ds(i, 1)], ALU.bitwise_or).then_inc(dve_own, own.one())
                dve.wait_ge(dve_own, own.all())
                dve.tensor_scalar(seen, far, trial.bitcast(F32), None, ALU.is_lt, ALU.add,
                                  accum_out=sc[:, 2:3]).then_inc(count_ready, 1)
                dve.wait_ge(count_spread, i + 1)
                dve.tensor_scalar(fewer, banks[:, 4, 0:1], CAP - 0.5, -1.0, ALU.is_lt, ALU.mult).then_inc(dve_own, own.one())
                dve.wait_ge(dve_own, own.all())
                dve.scalar_tensor_tensor(prefix, bits[:, bass.ds(i, 1)], fewer, prefix,
                                         ALU.bitwise_and, ALU.bitwise_or).then_inc(dve_own, own.one())
            dve.wait_ge(dve_own, own.all())
            dve.tensor_scalar(seen, far, sc[:, 8:9], None, ALU.is_lt, ALU.add,
                              accum_out=sc[:, 2:3]).then_inc(count_ready, 1)
            dve.wait_ge(count_spread, 32)
            dve.tensor_scalar(sc[:, 11:12], banks[:, 4, 0:1], -1.0, float(CAP), ALU.mult, ALU.add).then_inc(dve_own, own.one())
            dve.wait_ge(dve_own, own.all())
            for n, column in enumerate((8, 11, 1, 5)):
                ins = dve.tensor_scalar(spread_in[:, n, :], cut["first_of_expert"], sc[:, column:column + 1], None, ALU.mult)
            ins.then_inc(spread_in_ready, 1)
            dve.wait_ge(spread_done, 1)
            dve.tensor_copy(spread[:, :, :].rearrange("p a b -> p (a b)"), banks[:, 5, 0:4 * E]).then_inc(dve_own, own.one())

            dve.memset(keep[:, :, :], 1.0).then_inc(dve_own, own.one())
            dve.wait_ge(dve_own, own.all())
            dve.memset(keep[:, :, 0:1], 0.0).then_inc(dve_own, own.one())
            dve.wait_ge(gone_in, 32)
            dve.wait_ge(dve_own, own.all())
            for half in range(2):
                part = slice(half * E, (half + 1) * E)
                cutoff = spread[:, 0, :].unsqueeze(2).broadcast_to([P, E, L])
                dve.tensor_tensor(below[:, part], gone[:, part], cutoff, ALU.is_lt).then_inc(dve_own, own.one())
                dve.tensor_tensor(equal[:, part], gone[:, part], cutoff, ALU.is_equal).then_inc(dve_own, own.one())
            dve.wait_ge(dve_own, own.all())
            flat = lambda a: a[:, :, :].rearrange("p a b -> p (a b)")
            dve.tensor_tensor_scan(flat(n_below), flat(keep), flat(below), 0.0, ALU.mult, ALU.add).then_inc(dve_own, own.one())
            dve.tensor_tensor_scan(flat(n_equal), flat(keep), flat(equal), 0.0, ALU.mult, ALU.add).then_inc(dve_own, own.one())
            dve.wait_ge(dve_own, own.all())
            for n, a in enumerate((n_below, n_equal)):
                dve.tensor_copy(tot[:, :, n * E:(n + 1) * E],
                                a[:, :, L - 1:L].rearrange("p (h e) a -> p h (e a)", h=2)).then_inc(totals_ready, 1)
            dve.wait_ge(offsets_ready, 1)
            dve.tensor_copy(off[:, :, :].rearrange("p a b -> p (a b)"), banks[:, 6, 0:32]).then_inc(dve_own, own.one())
            dve.wait_ge(dve_own, own.all())
            wanted = spread[:, 1, :].unsqueeze(1).broadcast_to([P, 2, E])
            halves = lambda n: blocks_[:, n, :].rearrange("p (h e) -> p h e", h=2)
            dve.tensor_tensor(halves(0), wanted, off[:, :, E:2 * E], ALU.subtract).then_inc(dve_own, own.one())
            dve.tensor_tensor(halves(1), wanted, off[:, :, E:2 * E], ALU.min).then_inc(dve_own, own.one())
            dve.wait_ge(dve_own, own.all())
            dve.tensor_scalar(blocks_[:, 0, :], blocks_[:, 0, :], 0.0, None, ALU.max).then_inc(dve_own, own.one())
            dve.tensor_tensor(halves(1), halves(1), off[:, :, 0:E], ALU.add).then_inc(dve_own, own.one())
            dve.wait_ge(dve_own, own.all())
            dve.tensor_tensor(n_equal[:, :, :], n_equal[:, :, :],
                              blocks_[:, 0, :].unsqueeze(2).broadcast_to([P, TB, L]), ALU.min).then_inc(dve_own, own.one())
            dve.tensor_tensor(n_below[:, :, :], n_below[:, :, :],
                              blocks_[:, 1, :].unsqueeze(2).broadcast_to([P, TB, L]), ALU.add).then_inc(dve_own, own.one())
            dve.wait_ge(dve_own, own.all())
            dve.tensor_tensor(rank[:, :, 0:L], n_below[:, :, :], n_equal[:, :, :], ALU.add).then_inc(dve_own, own.one())
            for n, name in enumerate(("base_high", "base_low")):
                dve.tensor_copy(rank[:, :, L + n:L + n + 1].rearrange("p (h e) a -> p h (e a)", h=2),
                                cut[name].unsqueeze(2).broadcast_to([P, 2, E])).then_inc(dve_own, own.one())
            dve.wait_ge(vectors_in, 64)
            dve.tensor_copy(slots16, slots).then_inc(dve_own, own.one())
            dve.wait_ge(dve_own, own.all())
            dve.tensor_copy(blocks_[:, 2, :], rank[:, :, L - 1:L].rearrange("p a b -> p (a b)")).then_inc(dve_own, own.one())
            dve.wait_ge(dve_own, own.all())

            edges = blocks_[:, :, :].rearrange("p q (h e) -> p q h e", h=2)
            for e in own.loop(0, E, 3 + 2 * 5, peel=True):
                dve.tensor_copy(edge[:, :, :], edges[:, 1:3, :, bass.ds(e, 1)].rearrange("p q h a -> p q (h a)")).then_inc(dve_own, own.one())
                dve.wait_ge(dve_own, own.all())
                if due(e * 2):
                    dve.wait_ge(row_ready, e * 2)
                for half in range(2):
                    dve.tensor_scalar(from_lo, slots16, edge[:, 0, half:half + 1], None, ALU.is_ge).then_inc(dve_own, own.one())
                    dve.wait_ge(dve_own, own.all())
                    ins = dve.scalar_tensor_tensor(onehot[:, half, :], slots16, edge[:, 1, half:half + 1], from_lo,
                                                   ALU.is_lt, ALU.mult)
                    if half == 0:
                        ins.then_inc(onehot_half, 1)
                        dve.wait_ge(onehot_half, e + 1)
                ins.then_inc(onehot_ready, 1)
                for q in range(2):
                    dve.wait_ge(row_ready, e * 2 + (q + 1))
                    rows = banks[:, 7, 0:4 * (L + 2)].rearrange("p (m t) -> p m t", m=4)
                    dve.tensor_tensor(marked[:, :, :], rows[:, :, 0:L],
                                      cut["slot_numbers"][:, 4 * q:4 * q + 4].unsqueeze(2).broadcast_to([P, 4, L]),
                                      ALU.is_le).then_inc(dve_own, own.one())
                    dve.tensor_copy(base2[:, :, :], rows[:, :, L:L + 2]).then_inc(dve_own, own.one())
                    dve.wait_ge(dve_own, own.all())
                    dve.nop().then_inc(row_used, 1)
                    dve.tensor_reduce(place[:, 0, :], marked[:, :, :], AX.X, ALU.add).then_inc(dve_own, own.one())
                    dve.scalar_tensor_tensor(place[:, 1, :], base2[:, :, 0], float(P), base2[:, :, 1],
                                             ALU.mult, ALU.add).then_inc(dve_own, own.one())
                    dve.wait_ge(dve_own, own.all())
                    dve.tensor_tensor(index[:, bass.ds(e * SLOT_TILES + 4 * q, 4)], place[:, 0, :], place[:, 1, :],
                                      ALU.add).then_inc(dve_own, own.one())
                    dve.wait_ge(dve_own, own.all())
                    dve.nop().then_inc(index_ready, 1)

            def prepare(e, slot, turn):
                dve.wait_ge(found_in[slot], turn * 128 + 128)
                for m in range(SLOT_TILES):
                    ins = dve.bn_stats(fstats[:, m, :], found[:, bass.ds(e * SLOT_TILES + m, 1), :].rearrange("p a k -> p (a k)"))
                ins.then_inc(dve_own, own.one())
                dve.wait_ge(dve_own, own.all())
                mean0, sq0, mean1, sq1 = (fstats[:, :, n] for n in (1, 2, 4, 5))
                diff, total, var, mean_sum, rstd, mean, score, rel = (fsmall[:, slot, n, :] for n in range(8))
                dve.tensor_tensor(diff, mean0, mean1, ALU.subtract).then_inc(dve_own, own.one())
                dve.tensor_tensor(total, sq0, sq1, ALU.add).then_inc(dve_own, own.one())
                dve.tensor_tensor(mean_sum, mean0, mean1, ALU.add).then_inc(dve_own, own.one())
                dve.wait_ge(dve_own, own.all())
                dve.tensor_tensor(diff, diff, diff, ALU.mult).then_inc(dve_own, own.one())
                dve.tensor_scalar(mean, mean_sum, 0.5, None, ALU.mult).then_inc(dve_own, own.one())
                dve.wait_ge(dve_own, own.all())
                dve.scalar_tensor_tensor(total, diff, D / 4.0, total, ALU.mult, ALU.add).then_inc(dve_own, own.one())
                dve.wait_ge(dve_own, own.all())
                dve.tensor_scalar(var, total, 1.0 / D, EPS, ALU.mult, ALU.add).then_inc(var3_ready, 1)
                dve.wait_ge(rstd3_ready, e + 1)
                if due(e * 2 - 2):
                    dve.wait_ge(ft_copied, e * 2 - 2)
                for m in range(SLOT_TILES):
                    ins = dve.tensor_scalar(normed[:, slot, m, :],
                                            found[:, bass.ds(e * SLOT_TILES + m, 1), :].rearrange("p a k -> p (a k)"),
                                            fsmall[:, slot, 5, m:m + 1], fsmall[:, slot, 4, m:m + 1],
                                            ALU.subtract, ALU.mult)
                ins.then_inc(norm_ready, 1)
                dve.wait_ge(norm_ready, e + 1)
                for m in range(SLOT_TILES):
                    ins = dve.scalar_tensor_tensor(found[:, bass.ds(e * SLOT_TILES + m, 1), :].rearrange("p a k -> p (a k)"), normed[:, slot, m, :], 1.0,
                                                   wr_all[:, :, bass.ds(e, 1)].rearrange("p k a -> p (k a)"),
                                                   ALU.mult, ALU.mult, accum_out=fsmall[:, slot, 6, m:m + 1])
                ins.then_inc(dve_own, own.one())
                dve.tensor_copy(b1_now[:, slot, :], b1_cols[:, bass.ds(e * FC, FC)]).then_inc(dve_own, own.one())
                dve.wait_ge(dve_own, own.all())
                dve.tensor_tensor(rel, score, spread[:, 2, bass.ds(e, 1)].broadcast_to([P, SLOT_TILES]),
                                  ALU.subtract).then_inc(score_ready, 1)

            def collect(e, slot):
                dve.wait_ge(weight_ready, e + 1)
                dve.tensor_tensor(fsmall[:, slot, 9, :], fsmall[:, slot, 8, :],
                                  spread[:, 3, bass.ds(e, 1)].broadcast_to([P, SLOT_TILES]), ALU.mult).then_inc(dve_own, own.one())
                for g in range(2):
                    dve.wait_ge(down_ready, e * 2 + (g + 1))
                    dst = adds[:, bass.ds(e * SLOT_TILES + 4 * g, 4), :]
                    dve.tensor_tensor(dst, banks[:, 5 + g, :].rearrange("p (m d) -> p m d", m=4),
                                      b2_all[:, bass.ds(e, 1), :].broadcast_to([P, 4, D]), ALU.add).then_inc(dve_own, own.one())
                    dve.wait_ge(dve_own, own.all())
                    dve.nop().then_inc(down_copied, 1)
                    dve.tensor_tensor(dst, dst, fsmall[:, slot, 9, 4 * g:4 * g + 4].unsqueeze(2).broadcast_to([P, 4, D]),
                                      ALU.mult).then_inc(adds_ready, 1)

            dve.wait_ge(b1_ready, 1)
            prepare(0, 0, 0)
            for i in own.loop(0, E // 2 - 1, 2 * (9 + 3), peel=True):
                prepare(i * 2 + 1, 1, i)
                collect(i * 2, 0)
                prepare(i * 2 + 2, 0, i + 1)
                collect(i * 2 + 1, 1)
            i = E // 2 - 1
            prepare(i * 2 + 1, 1, i)
            collect(i * 2, 0)
            collect(i * 2 + 1, 1)

        @block.gpsimd
        def _(pool):
            pool.memset(powers[:, :], -0.5).then_inc(powers_ready, 1)
            pool.wait_ge(powers_ready, 1)
            for h in range(2):
                for cc in turns(pool, 0, CHUNKS // 2):
                    for slot in range(2):
                        pool.wait_ge(var_ready, 2 * cc + (slot + CHUNKS * h + 1))
                        pool.tensor_tensor(small[:, slot, 4, :], small[:, slot, 2, :], powers[0:L, :],
                                           ALU.pow).then_inc(rstd_ready, 1)
                for cc in turns(pool, 0, CHUNKS // 2, peel=h == 0):
                    for slot in range(2):
                        it = 2 * cc + (slot + CHUNKS * h)
                        pool.wait_ge(var2_ready, it + 1)
                        pool.tensor_tensor(small[:, slot, 4, :], small[:, slot, 2, :], powers[0:L, :],
                                           ALU.pow).then_inc(rstd2_ready, 1)
                        pool.wait_ge(rstd2_ready, it + 1)
                        for g in range(4):
                            if due(4 * it + (g - 1)):
                                pool.wait_ge(t2_ready, 4 * it + (g - 1))
                            pool.tensor_tensor(scaled[:, g % 2], hid[:, bass.ds(cc * (2 * HB) + (HB * slot + 4 * g), 4), :],
                                               small[:, slot, 4, 4 * g:4 * g + 4].unsqueeze(2).broadcast_to([L, 4, D]),
                                               ALU.mult).then_inc(scaled_ready, 1)
            rows = out.rearrange("b f d -> (b f) d")

            def power(e):
                pool.wait_ge(var3_ready, e + 1)
                pool.tensor_tensor(fsmall[:, e % 2, 4, :], fsmall[:, e % 2, 2, :], powers[:, 0:SLOT_TILES],
                                   ALU.pow).then_inc(rstd3_ready, 1)

            pool.wait_ge(rows_out, 16 * 16)
            for e in range(E):
                if due(128 * (e // 2)):
                    pool.wait_ge(found_in[e % 2], 128 * (e // 2))
                for m in range(SLOT_TILES):
                    pool.wait_ge(index_ready, 2 * e + m // 4 + 1)
                    n = e * SLOT_TILES + m
                    pool.indirect_dma_start(found[:, n, :], None, rows,
                                            bass.IndirectOffsetOnAxis(ap=index[:, n:n + 1], axis=0)
                                            ).then_inc(found_in[e % 2], 16)
                if e:
                    power(e - 1)
            power(E - 1)
            for slot in range(2):
                pool.wait_ge(found_in[slot], 128 * (E // 2))
            for e in range(E):
                if due(128 * e):
                    pool.wait_ge(added, 128 * e)
                for m in range(SLOT_TILES):
                    pool.wait_ge(adds_ready, 2 * e + m // 4 + 1)
                    n = e * SLOT_TILES + m
                    pool.indirect_dma_start(rows, bass.IndirectOffsetOnAxis(ap=index[:, n:n + 1], axis=0),
                                            adds[:, n, :], None, compute_op=ALU.add, oob_is_err=True,
                                            bounds_check=ROWS * FRAMES - 1).then_inc(added, 16)
            pool.wait_ge(added, 128 * E)


_INS = ["x", "L0_attn_nu", "L0_attn_theta", "L0_attn_gamma_real", "L0_attn_gamma_imag",
        "L0_ffn_Wr", "L0_ffn_W1", "L0_ffn_b1", "L0_ffn_W2", "L0_ffn_b2"]


def kernel(**inputs):
    import numpy as _np
    import concourse.bacc as _bacc
    from concourse import mybir as _mybir
    from concourse.bass_utils import run_bass_kernel_spmd as _run

    nc = _bacc.Bacc("TRN2", target_bir_lowering=False, num_devices=1)
    arrays, args = {}, []
    for name in _INS:
        a = _np.ascontiguousarray(inputs[name])
        arrays[f"in_{name}"] = a
        args.append(nc.dram_tensor(f"in_{name}", a.shape, _mybir.dt.from_np(a.dtype), kind="ExternalInput").ap())
    args.append(nc.dram_tensor("out_0", (ROWS, FRAMES, D), _mybir.dt.float32, kind="ExternalOutput").ap())
    build(nc, *args)
    r = _run(nc, [arrays], core_ids=[0])
    return r.results[0]["out_0"]
```

```python
from contextlib import ExitStack

import numpy as np
import concourse.bass as bass
from concourse import mybir

ALU = mybir.AluOpType
ACT = mybir.ActivationFunctionType
AX = mybir.AxisListType
F32 = mybir.dt.float32
F16 = mybir.dt.float16
I32 = mybir.dt.int32
U16 = mybir.dt.uint16

P = 128
D = 128
ROWS, SAMPLES = 32, 120000
FRAMES = SAMPLES // D + 1
TAIL = SAMPLES % D
CHUNKS = 8
L = -(-FRAMES // CHUNKS)
LAST = FRAMES - (CHUNKS - 1) * L
HB = ROWS // 2
COLS = HB * CHUNKS
PADDED = L * CHUNKS
EPS = 1e-5
E, F, CAP = 8, 512, 1024
FC = F // P
HALF = D // 2
SEGS = P // E
SEG = ROWS * PADDED // SEGS
ROWS_SEG = ROWS // SEGS
FAR = 1e38
ROUNDS = 8
SLOT_TILES = CAP // P
AHEAD = 3
RING = 16
DVE_TILES = 8
ACT_TILES = 4
ACT_MID, ACT_END = DVE_TILES + ACT_TILES // 2, DVE_TILES + ACT_TILES
ACT_GROUPS = 3

TWO_PI = 2 * np.pi
C1 = 6.28125
C2 = float(np.float32(int((TWO_PI - C1) * 2**21) / 2**21))
C3 = float(np.float32(TWO_PI - C1 - C2))
MAGIC = 1.5 * 2.0**23
PI_IN = 3.1415925


def constants():
    k, t = np.arange(D)[:, None].astype(np.float64), np.arange(D)[None, :].astype(np.float64)
    scale = np.full((D, 1), np.sqrt(2.0 / D))
    scale[0, 0] = np.sqrt(1.0 / D)
    basis = (scale * np.cos(np.pi * (2.0 * t + 1.0) * k / (2.0 * D))).astype(np.float32)
    p = np.arange(P)
    times = np.concatenate([np.arange(L + 1), np.arange(L - 1, -1, -1)])
    group = (p[:, None] // SEGS == p[None, :] // SEGS).astype(np.float32)
    block = np.arange(2 * P).reshape(2, P).T
    base = (block // CHUNKS) * FRAMES + (block % CHUNKS) * L
    unit = np.append(4.0 ** np.arange(ROUNDS - 1, -1, -1), 0.0)
    trials = (unit[:, None] * np.array([1, 2, 3, 0]) - np.array([0, 0, 0.5, 0])).reshape(-1)
    units = np.repeat(unit, 3)
    parts = {
        "basis_t": basis.T,
        "identity": np.eye(P),
        "times": np.tile(times, (P, 1)),
        "ones": np.ones((P, P)),
        "group": group,
        "other_group": (group - 1) * 3e38,
        "before": (p[:, None] < p[None, :]),
        "first_of_expert": (p[:, None] == SEGS * np.arange(E)[None, :]),
        "slot_numbers": p[:, None] + P * np.arange(SLOT_TILES)[None, :],
        "base_high": base // P,
        "base_low": base % P,
        "trials": np.tile(trials, (P, 1)),
        "units": np.tile(units, (P, 1)),
        "slots_row": np.tile(np.arange(CAP), (P, 1)),
    }
    table, at = [], {}
    n = 0
    for name, a in parts.items():
        a = np.ascontiguousarray(a, np.float32) if a.dtype != np.float32 else a
        at[name] = (n, n + a.shape[1])
        n += a.shape[1]
        table.append(a)
    return np.concatenate(table, axis=1), at


class Steps:

    def __init__(self, eng):
        self.eng, self.n, self.base = eng, 0, 0

    def one(self):
        self.n += 1
        return 1

    def all(self):
        return self.base + self.n

    def loop(self, start, end, per, peel=False):
        at = self.n
        first = start
        if peel:
            yield start
            assert self.n == at + per, (self.n - at, per)
            first = start + 1
        with self.eng.Fori(first, end) as i:
            self.base, self.n = i * per + (at - start * per), 0
            yield i
            assert self.n == per, (self.n, per)
        self.base, self.n = 0, at + (end - start) * per


def turns(eng, start, end, peel=False):
    if peel:
        yield start
        start += 1
    with eng.Fori(start, end) as i:
        yield i




def due(value):
    return not isinstance(value, int) or value > 0




def build(nc, x, nu, theta, gamma_r, gamma_i, Wr, W1, b1, W2, b2, out):
    table, at = constants()
    const_dram = nc.inline_tensor(table, name="constants").ap()
    zeros_dram = nc.inline_tensor(np.zeros((HB, D - TAIL), np.float32), name="zeros").ap()
    toeplitz = nc.dram_tensor("toeplitz", [L + 2, D, P], F32).ap()
    away_dram = nc.dram_tensor("away", [E, ROWS * PADDED], F32).ap()
    scales_dram = nc.dram_tensor("scales", [ROWS * PADDED], F32).ap()
    logits_dram = nc.dram_tensor("logits", [E, ROWS * PADDED], F32).ap()
    NC1 = at["slots_row"][0]
    NT = 2 * L + 1

    with ExitStack() as ctx:
        def sb(name, shape, dt=F32):
            return ctx.enter_context(nc.sbuf_tensor(name, shape, dt))

        const = sb("const", [P, NC1])
        cut = {n: const[:, a:b] for n, (a, b) in at.items() if b <= NC1}
        wr_c = sb("wr_c", [P, E])
        mu = sb("mu", [P, 3])
        state_w = sb("state_w", [L, D, 2])
        powers = sb("powers", [P, HB])
        hid_all = sb("hid", [P, COLS, D])
        hid = hid_all[0:L]
        xn_all = sb("xn", [P, D, COLS])
        xn = xn_all[0:L + 2]
        ring = sb("ring", [L + 2, 2, RING, P])
        xin_all = sb("xin", [P, 2, HB, D])
        xin = xin_all[0:L]
        xt_all = sb("xt", [P, 2, 4 * D])
        xt = xt_all[:, :, 0:4 * L].rearrange("p s (a b) -> p s a b", a=4)
        staged = sb("staged", [L, 3, 4, D])
        stats = sb("stats", [L, 2, HB, 6])
        small = sb("small", [L, 2, 8, HB])
        lstage = sb("lstage", [P, 2, 4 * L])
        scales = cut["times"][0:HB, 0:2 * L].rearrange("p (s t) -> p s t", s=2)
        setup = sb("setup", [P, 6, L + P])
        par = sb("par", [P, 8])
        ends = xin_all[:, :, :, :].rearrange("p a b c -> p (a b c)").rearrange("p (g r i n) -> p g r i n", g=2, r=4, i=4)
        e2 = sb("e2", [P, 2, COLS])
        s2 = sb("s2", [P, 2, COLS])
        carry = sb("carry", [P, 2, HB])
        w1_ring = sb("w1_ring", [P, 2, F])
        w2_ring = sb("w2_ring", [P, 2, FC, D])
        b2_all = sb("b2_all", [P, E, D])
        wr_all = sb("wr_all", [P, D, E])
        b1_rows = sb("b1_rows", [E * FC, P])
        b1_cols = sb("b1_cols", [P, E * FC])

        free = {"hid": [hid_all[:, :, :].rearrange("p a b -> p (a b)"), 0],
                "xn": [xn_all[:, :, :].rearrange("p a b -> p (a b)"), 0],
                "xin": [xin_all[:, :, :, :].rearrange("p a b c -> p (a b c)"), 0],
                "setup": [setup[:, :, :].rearrange("p a b -> p (a b)"), 0]}

        def take(where, words):
            region, n = free[where]
            free[where][1] = n + words
            assert n + words <= region.shape[1], where
            return region[:, n:n + words]

        TB = 2 * E
        found = take("hid", E * SLOT_TILES * D).rearrange("p (a b) -> p a b", b=D)
        adds = take("hid", E * SLOT_TILES * D).rearrange("p (a b) -> p a b", b=D)
        far = take("xn", SEG)
        seen = take("xn", SEG)
        hidden = take("xn", 512)
        acts = xn_all[:, :, :].rearrange("p a b -> p (a b)")[:, 0:2 * FC * 512].rearrange(
            "p (s f n) -> p s f n", s=2, f=FC)
        gone = take("xn", TB * L).rearrange("p (a b) -> p a b", b=L)
        normed_at = free["xn"][1]
        below = take("xn", TB * L).rearrange("p (a b) -> p a b", b=L)
        equal = take("xn", TB * L).rearrange("p (a b) -> p a b", b=L)
        flat16 = lambda a: a[:, :, :].rearrange("p a b -> p (a b)").bitcast(U16)
        upper, lower = flat16(below)[:, 0:SEG], flat16(below)[:, SEG:2 * SEG]
        marks = [seen.bitcast(U16)[:, n * SEG:(n + 1) * SEG] for n in range(2)]
        far_scale = below[:, :, :].rearrange("p a b -> p (a b)")
        marks_act = flat16(equal)[:, 0:SEG]
        n_below = take("xn", TB * L).rearrange("p (a b) -> p a b", b=L)
        n_equal = take("xn", TB * L).rearrange("p (a b) -> p a b", b=L)
        keep = take("xin", TB * L).rearrange("p (a b) -> p a b", b=L)
        rank = take("xn", TB * (L + 2) // 2).bitcast(F16).rearrange("p (a b) -> p a b", b=L + 2)
        slots = take("setup", CAP)
        slots16 = take("xin", CAP // 2).bitcast(F16)
        onehot = take("xn", 2 * CAP // 2).bitcast(F16).rearrange("p (a b) -> p a b", b=CAP)
        in_front = take("xin", TB * (L + 2) // 2).bitcast(F16).rearrange("p (a b) -> p a b", b=L + 2)
        sc = sb("sc", [P, 16])
        tot = sb("tot", [P, 2, 16])
        off = sb("off", [P, 2, 16])
        trial = sb("trial", [P, 2, 4])
        passed = sb("passed", [P, 3])
        spread = sb("spread", [P, 4, E])
        spread_in = sb("spread_in", [P, 4, E])
        blocks_ = sb("blocks_", [P, 4, TB])
        mall = take("xin", P)
        mrow = take("xin", P)[0:1, :]
        normed = xn_all[:, :, :].rearrange("p a b -> p (a b)")[
            :, normed_at:normed_at + 2 * SLOT_TILES * D].rearrange("p (s m d) -> p s m d", s=2, m=SLOT_TILES)
        marked = take("xin", 4 * L).rearrange("p (a b) -> p a b", b=L)
        place = sb("place", [P, 3, 4])
        base2 = sb("base2", [P, 4, 2])
        index = sb("index", [P, E * SLOT_TILES], I32)
        fstats = sb("fstats", [P, SLOT_TILES, 6])
        fsmall = sb("fsmall", [P, 3, 8, SLOT_TILES])
        natural = sb("natural", [P, SLOT_TILES])
        banks = ctx.enter_context(nc.psum_tensor("banks", [P, 8, 512], F32))
        def sem(name):
            return ctx.enter_context(nc.semaphore(name))

        const_in = sem("const_in")
        params_in = sem("params_in")
        wr_in = sem("wr_in")
        a_ready = sem("a_ready")
        rate_ready = sem("rate_ready")
        decay_ready = sem("decay_ready")
        reduced_ready = sem("reduced_ready")
        trig_ready = sem("trig_ready")
        tables_ready = sem("tables_ready")
        turned_tables = sem("turned_tables")
        toeplitz_out = sem("toeplitz_out")
        state_w_ready = sem("state_w_ready")
        wr_sum = sem("wr_sum")
        wr_ready = sem("wr_ready")
        kernel_ready = sem("kernel_ready")
        powers_ready = sem("powers_ready")
        dve_own = sem("dve_own")
        xt_ready = sem("xt_ready")
        xt_copied = sem("xt_copied")
        h_ready = sem("h_ready")
        h_copied = sem("h_copied")
        var_ready = sem("var_ready")
        rstd_ready = sem("rstd_ready")
        nb_ready = sem("nb_ready")
        xn_dve = sem("xn_dve")
        xn_act = sem("xn_act")
        centred = sem("centred")
        xn_pool = sem("xn_pool")
        e_ready = sem("e_ready")
        e_copied = sem("e_copied")
        e_moved = sem("e_moved")
        s_ready = sem("s_ready")
        s_moved = sem("s_moved")
        y_ready = sem("y_ready")
        y_added = sem("y_added")
        var2_ready = sem("var2_ready")
        rstd2_ready = sem("rstd2_ready")
        staged_act = sem("staged_act")
        staged_pool = sem("staged_pool")
        t2_ready = sem("t2_ready")
        l_part = sem("l_part")
        t2_copied = sem("t2_copied")
        scales_turned = sem("scales_turned")
        l_copied = sem("l_copied")
        rows_out = sem("rows_out")
        vectors_in = sem("vectors_in")
        logits_in = sem("logits_in")
        far_ready = sem("far_ready")
        far_out = sem("far_out")
        gone_in = sem("gone_in")
        sum_ready = sem("sum_ready")
        b1_turned = sem("b1_turned")
        b1_ready = sem("b1_ready")
        peak_ready = sem("peak_ready")
        peak_turned = sem("peak_turned")
        peak_row = sem("peak_row")
        peak_spread = sem("peak_spread")
        sum_spread = sem("sum_spread")
        trials_ready = sem("trials_ready")
        count_ready = sem("count_ready")
        sign_ready = sem("sign_ready")
        count_act = sem("count_act")
        count_spread = sem("count_spread")
        spread_in_ready = sem("spread_in_ready")
        spread_done = sem("spread_done")
        totals_ready = sem("totals_ready")
        offsets_ready = sem("offsets_ready")
        onehot_ready = sem("onehot_ready")
        row_ready = sem("row_ready")
        row_used = sem("row_used")
        index_ready = sem("index_ready")
        rank_ready = sem("rank_ready")
        front_in = sem("front_in")
        rstd3_ready = sem("rstd3_ready")
        norm_ready = sem("norm_ready")
        score_ready = sem("score_ready")
        weight_ready = sem("weight_ready")
        ft_ready = sem("ft_ready")
        ft_copied = sem("ft_copied")
        up_ready = sem("up_ready")
        gelu_ready = sem("gelu_ready")
        down_ready = sem("down_ready")
        down_copied = sem("down_copied")
        adds_ready = sem("adds_ready")
        added = sem("added")
        x_in = [sem(f"x_in{slot}") for slot in range(2)]
        ring_in = [sem(f"ring_in{slot}") for slot in range(2)]
        l_out = [sem(f"l_out{slot}") for slot in range(2)]
        weights_in = [sem(f"weights_in{slot}") for slot in range(2)]
        found_in = [sem(f"found_in{slot}") for slot in range(2)]

        def frames(h, c, rows):
            return bass.AP(x.tensor, c * (L * D) + h * HB * SAMPLES, [[D, rows], [SAMPLES, HB], [1, D]])

        def out_rows(h, c, rows):
            return bass.AP(out.tensor, c * (L * D) + h * HB * FRAMES * D, [[D, rows], [FRAMES * D, HB], [1, D]])

        R_, ANG, RED, SIN, COS, Q = (setup[:, n, 0:NT] for n in range(6))
        KPAD = setup[:, 0, 0:L - 1 + P]

        block = ctx.enter_context(nc.Block())

        @block.sync
        def _(sp):
            sp.dma_start(const[:, :], const_dram[:, 0:NC1]).then_inc(const_in, 16)
            for n, v in enumerate((nu, theta, gamma_r, gamma_i)):
                sp.dma_start(par[:, n:n + 1], v.rearrange("(p a) -> p a", a=1)).then_inc(params_in, 16)
            sp.dma_start(wr_c[:, :], Wr).then_inc(wr_in, 16)
            step = setup[:, 0, :].ap[0][0]

            def toeplitz_rows(j):
                rows = bass.AP(KPAD.tensor, KPAD.offset + 16 * j * step + L - 1, [[step, 16], [-1, L], [1, P]])
                sp.dma_start(bass.AP(toeplitz.tensor, 16 * j * P, [[P, 16], [D * P, L], [1, P]]),
                             rows).then_inc(toeplitz_out, 16)

            def weights(e, slot):
                sp.dma_start(w1_ring[:, slot], bass.AP(W1.tensor, e * (D * F) + slot * D * F,
                                                       [[F, D], [1, F]])).then_inc(weights_in[slot], 16)
                sp.dma_start(w2_ring[:, slot], bass.AP(W2.tensor, e * (D * F) + slot * D * F,
                                                       [[D, P], [P * D, FC], [1, D]])).then_inc(weights_in[slot], 16)

            for h in range(2):
                if h == 0:
                    for c in range(CHUNKS - 2):
                        if c >= 2:
                            sp.wait_ge(xt_ready, 4 * c - 4)
                        sp.dma_start(xin[:, c % 2], frames(h, c, L)).then_inc(x_in[c % 2], 16)
                        if c == 2:
                            sp.wait_ge(kernel_ready, 4)
                            sp.dma_start(bass.AP(toeplitz.tensor, L * D * P, [[P, D], [D * P, 2], [1, P]]),
                                         setup[:, 3:5, 1:P + 1]).then_inc(toeplitz_out, 16)
                        if c >= 2:
                            toeplitz_rows(2 * c - 4)
                            toeplitz_rows(2 * c - 3)
                else:
                    with sp.Fori(1, CHUNKS // 2 - 1) as cc:
                        for slot in range(2):
                            sp.wait_ge(xt_ready, 8 * cc + (4 * slot + 32 * h - 4))
                            sp.dma_start(xin[:, slot], frames(h, 2 * cc + slot, L)).then_inc(x_in[slot], 16)
                sp.wait_ge(xt_ready, 32 * h + 20)
                sp.dma_start(xin[:, 0], frames(h, CHUNKS - 2, L)).then_inc(x_in[0], 16)
                sp.wait_ge(xt_ready, 32 * h + 24)
                sp.dma_start(xin[0:LAST - 1, 1], frames(h, CHUNKS - 1, LAST - 1)).then_inc(x_in[1], 16)
                tail = bass.AP(x.tensor, h * HB * SAMPLES + (FRAMES - 1) * D, [[1, 1], [SAMPLES, HB], [1, TAIL]])
                sp.dma_start(xin[LAST - 1:LAST, 1, :, 0:TAIL], tail).then_inc(x_in[1], 16)
                sp.dma_start(xin[LAST - 1:LAST, 1, :, TAIL:D],
                             zeros_dram.rearrange("(a b) c -> a b c", a=1)).then_inc(x_in[1], 16)

                if h == 0:
                    sp.wait_ge(toeplitz_out, 16 * 9)
                def fill(i, slot):
                    if due(8 * i + (4 * slot + 32 * h - 4)):
                        sp.wait_ge(y_ready, 8 * i + (4 * slot + 32 * h - 4))
                    sp.dma_start(ring[:, slot].rearrange("p k t -> p (k t)"), bass.AP(
                        toeplitz.tensor, i * (2 * RING * P) + slot * RING * P,
                        [[D * P, L + 2], [1, RING * P]])).then_inc(ring_in[slot], 16)

                for slot in range(2):
                    fill(0, slot)

                def move_ends(g):
                    sp.wait_ge(e_copied, 8 * h + 4 * (g + 1))
                    for ri in range(2):
                        sp.dma_start(e2[HALF * g:HALF * (g + 1), ri, :],
                                     ends[ri:97 + ri:32, g]).then_inc(e_moved, 16)

                def move_states(g):
                    sp.wait_ge(s_ready, 2 * h + g + 1)
                    for ri in range(2):
                        sp.dma_start(xn[L + ri:L + ri + 1, HALF * g:HALF * (g + 1), :],
                                     s2[HALF * g:HALF * (g + 1), ri, :]).then_inc(s_moved, 16)

                move_ends(0)
                move_states(0)
                move_ends(1)
                for slot in range(2):
                    fill(1, slot)
                move_states(1)
                with sp.Fori(2, D // RING // 2) as i:
                    for slot in range(2):
                        fill(i, slot)

                if h == 0:
                    for slot in range(2):
                        sp.dma_start(xin[:, slot], frames(1, slot, L)).then_inc(x_in[slot], 16)
                else:
                    sp.dma_start(b2_all[:, :, :].rearrange("p e d -> p (e d)"),
                                 bass.AP(b2.tensor, 0, [[0, P], [1, E * D]])).then_inc(vectors_in, 16)
                    sp.dma_start(wr_all[:, :, :].rearrange("p d e -> p (d e)"),
                                 bass.AP(Wr.tensor, 0, [[0, P], [1, E * D]])).then_inc(vectors_in, 16)
                    sp.dma_start(b1_rows[:, :], b1.rearrange("e (f p) -> (e f) p", p=P)).then_inc(vectors_in, 16)
                    sp.dma_start(slots, const_dram[:, NC1:NC1 + CAP]).then_inc(vectors_in, 16)
                    for slot in range(2):
                        weights(0, slot)

                def store_logits(c, slot):
                    for j in range(4):
                        sp.dma_start(
                            bass.AP(logits_dram.tensor, c * L + (h * HB + 4 * j) * PADDED,
                                    [[ROWS * PADDED, E], [PADDED, 4], [1, L]]),
                            lstage[32 * j:32 * j + E, slot, :].rearrange("p (b t) -> p b t", b=4),
                        ).then_inc(l_out[slot], 16)
                    sp.dma_start(bass.AP(scales_dram.tensor, c * L + h * HB * PADDED, [[PADDED, HB], [1, L]]),
                                 scales[:, slot, :]).then_inc(l_out[slot], 16)

                sp.wait_ge(y_added, 32 * (h + 1))
                for cc in turns(sp, 0, CHUNKS // 2 - 1):
                    for slot in range(2):
                        c = 2 * cc + slot
                        sp.dma_start(out_rows(h, c, L), hid[:, bass.ds(c * HB, HB), :]).then_inc(rows_out, 16)
                        sp.wait_ge(l_copied, 2 * cc + (slot + CHUNKS * h + 1))
                        store_logits(c, slot)
                for slot, rows in ((0, L), (1, LAST)):
                    c = CHUNKS - 2 + slot
                    sp.dma_start(out_rows(h, c, rows), hid[0:rows, HB * c:HB * (c + 1), :]).then_inc(rows_out, 16)
                for slot in range(2):
                    c = CHUNKS - 2 + slot
                    sp.wait_ge(l_copied, c + 1 + CHUNKS * h)
                    store_logits(c, slot)
            sp.wait_ge(rows_out, 16 * 16)
            sp.wait_ge(l_out[0], 80 * 8)
            sp.wait_ge(l_out[1], 80 * 8)
            sp.wait_ge(y_ready, 64)
            sp.dma_start(far_scale, bass.AP(scales_dram.tensor, 0, [[0, E], [SEG, SEGS], [1, SEG]])).then_inc(logits_in, 16)
            sp.dma_start(far, logits_dram.rearrange("e (s n) -> (e s) n", n=SEG)).then_inc(logits_in, 16)
            sp.wait_ge(far_ready, 1)
            sp.dma_start(away_dram.rearrange("e (s n) -> (e s) n", n=SEG), far).then_inc(far_out, 16)
            sp.wait_ge(far_out, 16)
            for half in range(2):
                sp.dma_start(gone[:, half * E:(half + 1) * E, :],
                             bass.AP(away_dram.tensor, half * P * L, [[L, P], [ROWS * PADDED, E], [1, L]])
                             ).then_inc(gone_in, 16)
            sp.wait_ge(rank_ready, 1)
            sp.dma_start(in_front[1:P, :, :], rank[0:P - 1, :, :]).then_inc(front_in, 16)
            sp.dma_start(in_front[0:1, E:TB, :], rank[P - 1:P, 0:E, :]).then_inc(front_in, 16)
            with sp.Fori(1, E // 2) as i:
                for slot in range(2):
                    sp.wait_ge(down_ready, i * 4 + (2 * slot - 2))
                    weights(i * 2, slot)

        @block.scalar
        def _(act):
            act.wait_ge(params_in, 64)
            act.activation(par[:, 4:5], par[:, 0:1], ACT.Exp).then_inc(a_ready, 1)
            act.wait_ge(const_in, 16)
            act.wait_ge(rate_ready, 1)
            act.activation(R_, cut["times"], ACT.Exp, scale=par[:, 5:6]).then_inc(decay_ready, 1)
            act.wait_ge(reduced_ready, 1)
            act.activation(SIN, RED, ACT.Sin).then_inc(trig_ready, 1)
            act.wait_ge(reduced_ready, 2)
            act.activation(COS, ANG, ACT.Sin).then_inc(trig_ready, 1)
            for n in range(2):
                act.wait_ge(turned_tables, n + 1)
                act.activation(state_w[:, :, n], banks[0:L, n, 0:D], ACT.Copy).then_inc(state_w_ready, 1)
            for h in range(2):
                def copy_xt(n, G):
                    act.wait_ge(xt_ready, G + 1)
                    if due(G - 1):
                        act.wait_ge(h_ready, G - 1)
                    act.activation(xt[:, n % 2], banks[:, n % 2, 0:4 * L].rearrange("p (a b) -> p a b", a=4),
                                   ACT.Copy).then_inc(xt_copied, 1)

                def copy_h(n, slot, G, cc):
                    act.wait_ge(h_ready, G + 1)
                    act.activation(hid[:, bass.ds(cc * (2 * HB) + (HB * slot + 4 * n), 4), :],
                                   banks[0:L, 2 + n % 2, :].rearrange("p (a b) -> p a b", a=4),
                                   ACT.Copy).then_inc(h_copied, 1)

                def normalise(c, slot, first, last):
                    if first == DVE_TILES:
                        act.wait_ge(nb_ready, c + (CHUNKS * h + 1))
                    for b in range(first, last):
                        ins = act.activation(xn[0:L, :, bass.ds(c * HB + b, 1)].rearrange("p k a -> p (k a)"),
                                             hid[:, bass.ds(c * HB + b, 1), :].rearrange("p a k -> p (a k)"),
                                             ACT.Identity, bias=small[:, slot, 6, b:b + 1],
                                             scale=small[:, slot, 4, b:b + 1])
                    if last == ACT_END:
                        ins.then_inc(xn_act, 1)


                def chunk(cc, slot, first=False, last=False):
                    G0 = 8 * cc + (4 * slot + 32 * h)
                    for n in range(4):
                        if not (last and n == 3):
                            copy_xt(n + 1, G0 + (n + 1))
                        copy_h(n, slot, G0 + n, cc)
                        if n >= 2 and not first:
                            normalise(2 * cc + (slot - 1), 1 - slot, *((DVE_TILES, ACT_MID), (ACT_MID, ACT_END))[n - 2])

                if h:
                    act.wait_ge(rows_out, 16 * CHUNKS)
                    act.wait_ge(l_part, 4 * CHUNKS)
                copy_xt(0, 32 * h)
                chunk(0, 0, first=True)
                chunk(0, 1)
                for cc in turns(act, 1, CHUNKS // 2 - 1):
                    for slot in range(2):
                        chunk(cc, slot)
                chunk(CHUNKS // 2 - 1, 0)
                chunk(CHUNKS // 2 - 1, 1, last=True)
                normalise(CHUNKS - 1, 1, DVE_TILES, ACT_END)

                for r in range(8):
                    act.wait_ge(e_ready, 8 * h + r + 1)
                    act.activation(ends[0:98, r // 4, r % 4], banks[0:98, 6 + r % 2, :].rearrange("p (a b) -> p a b", a=4),
                                   ACT.Copy).then_inc(e_copied, 1)

                def stage(c, n):
                    it = c + CHUNKS * h
                    before = (4 * it - 1, 4 * it - 2, 4 * it + 1)[n]
                    if due(before):
                        act.wait_ge(t2_ready, before)
                    act.activation(staged[:, n % 2], hid[:, bass.ds(c * HB + 4 * n, 4), :], ACT.Copy).then_inc(staged_act, 1)

                def logits_out(c, slot, stored):
                    it = c + CHUNKS * h
                    act.wait_ge(l_part, 4 * it + 4)
                    if due(stored):
                        act.wait_ge(l_out[slot], stored)
                    act.activation(lstage[0:104, slot, :], banks[0:104, 4 + slot, 0:4 * L], ACT.Copy)
                    act.wait_ge(scales_turned, it + 1)
                    act.activation(scales[:, slot, :], banks[0:HB, 6 + slot, 0:L], ACT.Copy).then_inc(l_copied, 1)

                def turned(cc, slot, stored=None, last=False):
                    c = 2 * cc + slot
                    for n in range(4):
                        if n < ACT_GROUPS - 1:
                            stage(c, n + 1)
                        elif n == 3 and not last:
                            stage(c + 1, 0)
                        G = 4 * c + (n + 32 * h)
                        act.wait_ge(t2_ready, G + 1)
                        if due(G - 1):
                            act.wait_ge(l_part, G - 1)
                        act.activation(xt[:, n % 2], banks[:, n % 2, 0:4 * L].rearrange("p (a b) -> p a b", a=4),
                                       ACT.Copy).then_inc(t2_copied, 1)
                        if n == 1 and stored is not None:
                            logits_out(c - 1, 1 - slot, stored)

                act.wait_ge(y_added, 32 * (h + 1))
                stage(0, 0)
                turned(0, 0)
                turned(0, 1, 320 * h)
                with act.Fori(1, CHUNKS // 2 - 1) as cc:
                    turned(cc, 0, 80 * cc + (320 * h - 80))
                    turned(cc, 1, 80 * cc + 320 * h)
                cc = CHUNKS // 2 - 1
                turned(cc, 0, 80 * cc + (320 * h - 80))
                turned(cc, 1, 80 * cc + 320 * h, last=True)
                logits_out(2 * cc + 1, 1, 80 * cc + 320 * h)

            act.wait_ge(far_ready, 1)
            act.activation(seen, far, ACT.Exp, scale=-1.0, accum_out=sc[:, 4:5]).then_inc(sum_ready, 1)
            for phase, source in enumerate((upper, lower)):
                for i in turns(act, 0, ROUNDS // 2):
                    for k in range(2):
                        act.wait_ge(trials_ready, 2 * i + ((ROUNDS + 1) * phase + k + 1))
                        act.activation(marks_act, source, ACT.Sign, scale=-1.0, bias=trial[:, k, 2:3],
                                       accum_out=sc[:, 7:8]).then_inc(sign_ready, 1)
                        act.wait_ge(sign_ready, 2 * i + (ROUNDS * phase + k + 1))
                        act.activation(sc[:, 14:15], sc[:, 7:8], ACT.Identity, scale=0.5, bias=sc[:, 6:7]
                                       ).then_inc(count_act, 1)
            act.wait_ge(b1_turned, 1)
            act.activation(b1_cols[:, :], banks[:, 2, 0:E * FC], ACT.Copy).then_inc(b1_ready, 1)

            def normalise_rows(e):
                act.wait_ge(rstd3_ready, e + 1)
                for m in range(SLOT_TILES):
                    ins = act.activation(normed[:, e % 2, m, :], found[:, e * SLOT_TILES + m, :], ACT.Identity,
                                         bias=fsmall[:, e % 3, 6, m:m + 1], scale=fsmall[:, e % 3, 4, m:m + 1])
                ins.then_inc(norm_ready, 1)

            normalise_rows(0)
            for e in range(E):
                for g in range(2):
                    n = 2 * e + g
                    act.wait_ge(ft_ready, n + 1)
                    act.activation(xt_all[:, g], banks[:, 0, :], ACT.Copy).then_inc(ft_copied, 1)
                    if g and e + 1 < E:
                        normalise_rows(e + 1)
                    if n >= 2:
                        act.wait_ge(down_ready, n - 1)
                    for f in range(FC):
                        act.wait_ge(up_ready, FC * n + f + 1)
                        act.activation(acts[:, g, f], banks[:, 1 + f, :], ACT.Gelu,
                                       bias=b1_cols[:, FC * e + f:FC * e + f + 1]).then_inc(gelu_ready, 1)

        @block.tensor
        def _(pe):
            pe.wait_ge(const_in, 16)
            pe.wait_ge(wr_in, 16)
            pe.matmul(banks[:, 2, 0:E], cut["ones"], wr_c[:, :], start=True, stop=True).then_inc(wr_sum, 1)
            pe.wait_ge(tables_ready, 2)
            for n, src in enumerate((ANG, RED)):
                pe.transpose(banks[0:L, n, 0:D], src[:, L + 1:NT], cut["identity"]).then_inc(turned_tables, 1)
            pe.wait_ge(state_w_ready, 2)
            pe.wait_ge(wr_ready, 1)
            for h in range(2):
                def turn(n, G, cc, x1):
                    if n == 0:
                        pe.wait_ge(x_in[0], 16 * cc + (64 * h + 16))
                    if n == 4:
                        pe.wait_ge(x_in[1], x1)
                    if due(G - 1):
                        pe.wait_ge(xt_copied, G - 1)
                    for i in range(4):
                        mm = pe.transpose(banks[:, n % 2, i * L:(i + 1) * L], xin[:, n // 4, 4 * (n % 4) + i, :],
                                          cut["identity"][0:L, 0:L])
                    mm.then_inc(xt_ready, 1)

                def dct(n, G):
                    pe.wait_ge(xt_copied, G + 1)
                    if due(G - 1):
                        pe.wait_ge(h_copied, G - 1)
                    for i in range(4):
                        mm = pe.matmul(banks[0:L, 2 + n % 2, i * D:(i + 1) * D], xt[:, n % 2, i, :],
                                       cut["basis_t"], start=True, stop=True)
                    mm.then_inc(h_ready, 1)

                def eight(cc, x1):
                    G0 = 8 * cc + 32 * h
                    turn(0, G0, cc, x1)
                    for n in range(8):
                        if n < 7:
                            turn(n + 1, G0 + (n + 1), cc, x1)
                        dct(n, G0 + n)

                if due(32 * h):
                    pe.wait_ge(t2_copied, 32 * h)
                for cc in turns(pe, 0, CHUNKS // 2 - 1, peel=h == 0):
                    eight(cc, 16 * cc + (96 * h + 16))
                eight(CHUNKS // 2 - 1, 96 * h + 96)

                pe.wait_ge(xn_dve, CHUNKS * (h + 1))
                pe.wait_ge(xn_act, CHUNKS * (h + 1))
                pe.wait_ge(xn_pool, CHUNKS * (h + 1))
                if due(CHUNKS * h):
                    pe.wait_ge(l_copied, CHUNKS * h)
                for r in range(8):
                    if due(8 * h + r - 1):
                        pe.wait_ge(e_copied, 8 * h + r - 1)
                    for i in range(4):
                        for j in range(4):
                            k = HALF * (r // 4) + 16 * j + 4 * (r % 4) + i
                            mm = pe.matmul(banks[32 * j:32 * j + 2, 6 + r % 2, i * COLS:(i + 1) * COLS],
                                           state_w[:, k, :], xn[0:L, k, :], start=True, stop=True)
                    mm.then_inc(e_ready, 1)

                def products(i):
                    for slot in range(2):
                        pe.wait_ge(ring_in[slot], 16 * i + (64 * h + 16))
                        for g in range(4):
                            if due(8 * i + (4 * slot + g + 32 * h - 3)):
                                pe.wait_ge(y_added, 8 * i + (4 * slot + g + 32 * h - 3))
                            for q in range(4):
                                kk = RING * slot + 4 * g + q
                                mm = pe.matmul(banks[0:L, 2 + g, q * COLS:(q + 1) * COLS], ring[:, slot, 4 * g + q, 0:L],
                                               xn[:, bass.ds(i * (2 * RING) + kk, 1), :].rearrange("p a n -> p (a n)"),
                                               start=True, stop=True)
                            mm.then_inc(y_ready, 1)

                for g in range(2):
                    pe.wait_ge(s_moved, 64 * h + 32 * (g + 1))
                    for i in range(2):
                        products(2 * g + i)

                def turn2(n, c):
                    it = c + CHUNKS * h
                    if n < ACT_GROUPS:
                        pe.wait_ge(staged_act, it * ACT_GROUPS + (n + 1))
                    else:
                        pe.wait_ge(staged_pool, it * (4 - ACT_GROUPS) + (n - ACT_GROUPS + 1))
                    if due(4 * it + (n - 1)):
                        pe.wait_ge(t2_copied, 4 * it + (n - 1))
                    for i in range(4):
                        mm = pe.transpose(banks[:, n % 2, i * L:(i + 1) * L], staged[:, 2 if n == 3 else n % 2, i, :],
                                          cut["identity"][0:L, 0:L])
                    mm.then_inc(t2_ready, 1)

                def logits(n, c, slot):
                    it = c + CHUNKS * h
                    pe.wait_ge(t2_copied, 4 * it + (n + 1))
                    if n == 0 and due(it - 1):
                        pe.wait_ge(l_copied, it - 1)
                    pe.matmul(banks[32 * n:32 * n + E, 4 + slot, 0:4 * L], wr_c[:, :], xt_all[:, n % 2, 0:4 * L],
                              start=True, stop=True).then_inc(l_part, 1)

                def turn_scales(c, slot):
                    it = c + CHUNKS * h
                    pe.wait_ge(rstd2_ready, it + 1)
                    if due(it - 1):
                        pe.wait_ge(l_copied, it - 1)
                    pe.transpose(banks[0:HB, 6 + slot, 0:L], small[:, slot, 4, :], cut["identity"][0:L, 0:L]
                                 ).then_inc(scales_turned, 1)

                def rows_chunk(cc, slot, first=False, last=False):
                    c = 2 * cc + slot
                    for n in range(4):
                        if n < 3:
                            turn2(n + 1, c)
                        elif not last:
                            turn2(0, c + 1)
                        if n == 0 and not first:
                            turn_scales(c - 1, 1 - slot)
                        logits(n, c, slot)

                pe.wait_ge(y_added, 32 * (h + 1))
                turn2(0, 0)
                rows_chunk(0, 0, first=True)
                rows_chunk(0, 1)
                for cc in turns(pe, 1, CHUNKS // 2 - 1):
                    rows_chunk(cc, 0)
                    rows_chunk(cc, 1)
                rows_chunk(CHUNKS // 2 - 1, 0)
                rows_chunk(CHUNKS // 2 - 1, 1, last=True)
                turn_scales(CHUNKS - 1, 1)

            pe.wait_ge(peak_ready, 1)
            pe.wait_ge(l_copied, 16)
            pe.transpose(banks[0:1, 0, 0:P], sc[:, 0:1], cut["identity"]).then_inc(peak_turned, 1)
            pe.wait_ge(peak_row, 1)
            pe.matmul(banks[:, 1, 0:P], cut["ones"][0:1, :], mrow[:, :], start=True, stop=True).then_inc(peak_spread, 1)
            pe.wait_ge(vectors_in, 64)
            pe.transpose(banks[:, 2, 0:E * FC], b1_rows[:, :], cut["identity"][0:E * FC, 0:E * FC]).then_inc(b1_turned, 1)
            pe.wait_ge(sum_ready, 1)
            pe.matmul(banks[:, 3, 0:1], cut["group"], sc[:, 4:5], start=True, stop=True).then_inc(sum_spread, 1)
            for phase in range(2):
                for i in turns(pe, 0, ROUNDS):
                    pe.wait_ge(count_ready, i + ((ROUNDS + 1) * phase + 1))
                    pe.wait_ge(count_act, i + (ROUNDS * phase + 1))
                    pe.matmul(banks[:, 4, 0:3], cut["group"], sc[:, 12:15], start=True, stop=True).then_inc(count_spread, 1)
                pe.wait_ge(count_ready, (ROUNDS + 1) * (phase + 1))
                pe.matmul(banks[:, 4, 3 + phase:4 + phase], cut["group"], sc[:, 2:3], start=True, stop=True).then_inc(count_spread, 1)
            pe.wait_ge(spread_in_ready, 1)
            pe.matmul(banks[:, 5, 0:4 * E], cut["ones"], spread_in[:, :, :].rearrange("p a b -> p (a b)"),
                      start=True, stop=True).then_inc(spread_done, 1)
            pe.wait_ge(totals_ready, 2)
            pe.matmul(banks[:, 6, 0:32], cut["before"], tot[:, :, :].rearrange("p a b -> p (a b)"), start=True, stop=False)
            pe.matmul(banks[:, 6, 16:32], cut["ones"], tot[:, 0, :], start=False, stop=True).then_inc(offsets_ready, 1)
            def ranks(e, q):
                if q == 0:
                    pe.wait_ge(onehot_ready, e + 1)
                if 2 * e + q:
                    pe.wait_ge(row_used, 2 * e + q)
                for m in range(4):
                    for half in range(2):
                        mm = pe.matmul(banks[:, 7, m * (L + 2):(m + 1) * (L + 2)],
                                       onehot[:, half, (4 * q + m) * P:(4 * q + m + 1) * P],
                                       rank[:, e + half * E, :], start=half == 0, stop=half == 1)
                mm.then_inc(row_ready, 1)

            def ffn_turn(n):
                if n < 2 * E:
                    pe.wait_ge(norm_ready, n // 2 + 1)
                    if n:
                        pe.wait_ge(ft_copied, n)
                    for m in range(4):
                        mm = pe.transpose(banks[:, 0, m * P:(m + 1) * P], normed[:, n // 2 % 2, 4 * (n % 2) + m, :],
                                          cut["identity"])
                    mm.then_inc(ft_ready, 1)

            for e in range(AHEAD):
                for q in range(2):
                    ranks(e, q)
            ffn_turn(0)
            for n in range(2 * E):
                e, g = n // 2, n % 2
                if g == 0:
                    pe.wait_ge(weights_in[e % 2], 32 * (e // 2 + 1))
                pe.wait_ge(ft_copied, n + 1)
                if n:
                    pe.wait_ge(gelu_ready, FC * n)
                for f in range(FC):
                    pe.matmul(banks[:, 1 + f, :], w1_ring[:, e % 2, f * P:(f + 1) * P], xt_all[:, g],
                              start=True, stop=True).then_inc(up_ready, 1)
                ffn_turn(n + 1)
                if n + AHEAD < E:
                    ranks(n + AHEAD, 0)
                pe.wait_ge(gelu_ready, FC * (n + 1))
                if n >= 2:
                    pe.wait_ge(down_copied, n - 1)
                for m in range(4):
                    for f in range(FC):
                        mm = pe.matmul(banks[:, 5 + g, m * D:(m + 1) * D], acts[:, g, f, m * P:(m + 1) * P],
                                       w2_ring[:, e % 2, f, :], start=f == 0, stop=f == FC - 1)
                mm.then_inc(down_ready, 1)
                if n + AHEAD < E:
                    ranks(n + AHEAD, 1)

        @block.vector
        def _(dve):
            own = Steps(dve)
            dve.memset(banks[0:98, 6:8, :], 0.0)
            dve.memset(s2[:, :, 0:HB], 0.0)
            dve.wait_ge(wr_sum, 1)
            dve.scalar_tensor_tensor(wr_c[:, :], banks[:, 2, 0:E], -1.0 / D, wr_c[:, :],
                                     ALU.mult, ALU.add).then_inc(wr_ready, 1)
            dve.wait_ge(params_in, 64)
            dve.wait_ge(a_ready, 1)
            dve.tensor_scalar(par[:, 5:6], par[:, 4:5], -1.0, None, ALU.mult).then_inc(rate_ready, 1)
            dve.wait_ge(const_in, 16)
            dve.tensor_scalar(ANG, cut["times"], par[:, 1:2], None, ALU.mult).then_inc(dve_own, own.one())
            for n, (dst, quarter) in enumerate(((RED, 0.0), (ANG, 0.25))):
                dve.wait_ge(dve_own, own.all())
                dve.tensor_scalar(Q, ANG, float(1 / TWO_PI), quarter, ALU.mult, ALU.add).then_inc(dve_own, own.one())
                dve.wait_ge(dve_own, own.all())
                dve.tensor_scalar(Q, Q, MAGIC, -MAGIC, ALU.add, ALU.add).then_inc(dve_own, own.one())
                src = ANG
                for part in (C1, C2, C3):
                    dve.wait_ge(dve_own, own.all())
                    dve.scalar_tensor_tensor(dst, Q, -part, src, ALU.mult, ALU.add).then_inc(dve_own, own.one())
                    src = dst
                if n:
                    dve.wait_ge(dve_own, own.all())
                    dve.tensor_scalar(dst, dst, float(np.pi / 2), None, ALU.add).then_inc(dve_own, own.one())
                dve.wait_ge(dve_own, own.all())
                dve.tensor_scalar(dst, dst, PI_IN, -PI_IN, ALU.min, ALU.max).then_inc(reduced_ready, 1)
            dve.wait_ge(decay_ready, 1)
            dve.wait_ge(trig_ready, 2)
            dve.tensor_tensor(ANG, COS, R_, ALU.mult).then_inc(tables_ready, 1)
            dve.tensor_tensor(RED, SIN, R_, ALU.mult).then_inc(tables_ready, 1)
            dve.wait_ge(tables_ready, 2)
            dve.tensor_copy(mu[:, 0:1], ANG[:, L:L + 1]).then_inc(dve_own, own.one())
            dve.tensor_copy(mu[:, 1:2], RED[:, L:L + 1]).then_inc(dve_own, own.one())
            dve.tensor_scalar(mu[:, 2:3], RED[:, L:L + 1], -1.0, None, ALU.mult).then_inc(dve_own, own.one())
            N1 = L + 1
            dve.tensor_scalar(Q[:, 0:N1], RED[:, 0:N1], par[:, 3:4], None, ALU.mult).then_inc(dve_own, own.one())
            dve.memset(KPAD[:, 0:L - 1], 0.0).then_inc(dve_own, own.one())
            dve.memset(KPAD[:, 2 * L - 1:], 0.0)
            dve.memset(setup[:, 3:5, L + 1:P + 1], 0.0).then_inc(kernel_ready, 1)
            dve.wait_ge(dve_own, own.all())
            dve.scalar_tensor_tensor(SIN[:, 0:N1], ANG[:, 0:N1], par[:, 2:3], Q[:, 0:N1],
                                     ALU.mult, ALU.subtract).then_inc(kernel_ready, 1)
            dve.wait_ge(kernel_ready, 2)
            dve.tensor_scalar(Q[:, 0:N1], ANG[:, 0:N1], par[:, 3:4], None, ALU.mult).then_inc(dve_own, own.one())
            dve.tensor_copy(KPAD[:, L - 1:2 * L - 1], SIN[:, 0:L]).then_inc(kernel_ready, 1)
            dve.wait_ge(dve_own, own.all())
            dve.scalar_tensor_tensor(COS[:, 0:N1], RED[:, 0:N1], par[:, 2:3], Q[:, 0:N1], ALU.mult, ALU.add).then_inc(dve_own, own.one())
            dve.wait_ge(dve_own, own.all())
            dve.tensor_scalar(COS[:, 0:N1], COS[:, 0:N1], -1.0, None, ALU.mult).then_inc(kernel_ready, 1)

            def halves_stats(c, slot, n):
                for b in range(4 * n, 4 * n + 4):
                    ins = dve.bn_stats(stats[:, slot, b, :], hid[:, bass.ds(c * HB + b, 1), :].rearrange("p a k -> p (a k)"))
                if n == 3:
                    ins.then_inc(dve_own, own.one())

            def moments(slot, ready):
                dve.wait_ge(dve_own, own.all())
                mean0, sq0, mean1, sq1 = (stats[:, slot, :, n] for n in (1, 2, 4, 5))
                diff, total, var, mean_sum, _, mean = (small[:, slot, n, :] for n in range(6))
                dve.tensor_tensor(diff, mean0, mean1, ALU.subtract).then_inc(dve_own, own.one())
                dve.tensor_tensor(total, sq0, sq1, ALU.add).then_inc(dve_own, own.one())
                dve.tensor_tensor(mean_sum, mean0, mean1, ALU.add).then_inc(dve_own, own.one())
                dve.wait_ge(dve_own, own.all())
                dve.tensor_tensor(diff, diff, diff, ALU.mult).then_inc(dve_own, own.one())
                dve.tensor_scalar(mean, mean_sum, 0.5, None, ALU.mult).then_inc(dve_own, own.one())
                dve.wait_ge(dve_own, own.all())
                dve.scalar_tensor_tensor(total, diff, D / 4.0, total, ALU.mult, ALU.add).then_inc(dve_own, own.one())
                dve.wait_ge(dve_own, own.all())
                dve.tensor_scalar(var, total, 1.0 / D, EPS, ALU.mult, ALU.add).then_inc(ready, 1)

            for h in range(2):
                def normalise(c, slot, first, last):
                    for b in range(first, last):
                        ins = dve.tensor_scalar(xn[0:L, :, bass.ds(c * HB + b, 1)].rearrange("p k a -> p (k a)"),
                                                hid[:, bass.ds(c * HB + b, 1), :].rearrange("p a k -> p (a k)"),
                                                small[:, slot, 5, b:b + 1], small[:, slot, 4, b:b + 1],
                                                ALU.subtract, ALU.mult)
                    if last == DVE_TILES:
                        ins.then_inc(xn_dve, 1)

                def bias(c, slot):
                    dve.wait_ge(rstd_ready, c + (CHUNKS * h + 1))
                    dve.scalar_tensor_tensor(small[:, slot, 6, :], small[:, slot, 5, :], -1.0, small[:, slot, 4, :],
                                             ALU.mult, ALU.mult).then_inc(nb_ready, 1)

                def front(cc, slot, first=False):
                    c = 2 * cc + slot
                    it = c + CHUNKS * h
                    for n in range(4):
                        dve.wait_ge(h_copied, 4 * it + (n + 1))
                        halves_stats(c, slot, n)
                        if n == 1 and not first:
                            bias(c - 1, 1 - slot)
                        if n in (1, 2) and not first:
                            normalise(c - 1, 1 - slot, 3 * n - 3, 3 * n)
                    if due(it - 1):
                        dve.wait_ge(xn_act, it - 1)
                        dve.wait_ge(xn_pool, it - 1)
                    moments(slot, var_ready)
                    if not first:
                        normalise(c - 1, 1 - slot, 6, DVE_TILES)

                if due(32 * h):
                    dve.wait_ge(y_ready, 32 * h)
                front(0, 0, first=True)
                front(0, 1)
                for cc in own.loop(1, CHUNKS // 2 - 1, 14):
                    front(cc, 0)
                    front(cc, 1)
                front(CHUNKS // 2 - 1, 0)
                front(CHUNKS // 2 - 1, 1)
                bias(CHUNKS - 1, 1)
                normalise(CHUNKS - 1, 1, 0, DVE_TILES)

                def states(g):
                    part = slice(HALF * g, HALF * (g + 1))

                    def state(ri, c):
                        return s2[part, ri, HB * c:HB * (c + 1)]

                    def end(ri, c):
                        return e2[part, ri, HB * c:HB * (c + 1)]

                    dve.wait_ge(e_moved, 64 * h + 32 * (g + 1))
                    for ri in range(2):
                        dve.tensor_copy(state(ri, 1), end(ri, 0)).then_inc(dve_own, own.one())
                    for c in range(2, CHUNKS):
                        dve.wait_ge(dve_own, own.all())
                        for ri in range(2):
                            dve.scalar_tensor_tensor(carry[part, ri, :], state(0, c - 1), mu[part, ri:ri + 1],
                                                     end(ri, c - 1), ALU.mult, ALU.add).then_inc(dve_own, own.one())
                        dve.wait_ge(dve_own, own.all())
                        for ri in range(2):
                            m = (2, 0)[ri]
                            dve.scalar_tensor_tensor(state(ri, c), state(1, c - 1), mu[part, m:m + 1],
                                                     carry[part, ri, :], ALU.mult, ALU.add).then_inc(dve_own, own.one())
                    dve.wait_ge(dve_own, own.all())
                    dve.nop().then_inc(s_ready, 1)

                def add_products(i):
                    for n in range(8):
                        dve.wait_ge(y_ready, 8 * i + (n + 32 * h + 1))
                        rows = hid[:, :, bass.ds(i * (2 * RING) + 4 * n, 4)]
                        dve.tensor_tensor(rows, rows, banks[0:L, 2 + n % 4, :].rearrange("p (k n) -> p n k", k=4),
                                          ALU.add).then_inc(y_added, 1)

                if due(64 * h):
                    dve.wait_ge(s_moved, 64 * h)
                states(0)
                add_products(0)
                states(1)
                for i in turns(dve, 1, D // RING // 2):
                    add_products(i)
                dve.wait_ge(y_added, 32 * (h + 1))

                def rows_moments(cc, slot):
                    c = 2 * cc + slot
                    it = c + CHUNKS * h
                    for n in range(4):
                        halves_stats(c, slot, n)
                    if due(it - 1):
                        dve.wait_ge(scales_turned, it - 1)
                    moments(slot, var2_ready)

                rows_moments(0, 0)
                rows_moments(0, 1)
                for cc in own.loop(1, CHUNKS // 2 - 1, 14):
                    rows_moments(cc, 0)
                    rows_moments(cc, 1)
                rows_moments(CHUNKS // 2 - 1, 0)
                rows_moments(CHUNKS // 2 - 1, 1)

            dve.wait_ge(logits_in, 32)
            dve_far = far.rearrange("p (r n) -> p r n", r=ROWS_SEG)
            dve.tensor_tensor(far, far, far_scale, ALU.mult).then_inc(dve_own, own.one())
            dve.wait_ge(dve_own, own.all())
            dve.memset(dve_far[:, :, FRAMES:PADDED], -FAR).then_inc(dve_own, own.one())
            dve.wait_ge(dve_own, own.all())
            dve.tensor_reduce(sc[:, 0:1], far, AX.X, ALU.max).then_inc(peak_ready, 1)
            dve.wait_ge(peak_turned, 1)
            dve.tensor_copy(mrow[:, :], banks[0:1, 0, 0:P]).then_inc(peak_row, 1)
            dve.wait_ge(peak_spread, 1)
            dve.tensor_tensor(mall, banks[:, 1, 0:P], cut["group"], ALU.mult).then_inc(dve_own, own.one())
            dve.wait_ge(dve_own, own.all())
            dve.tensor_tensor(mall, mall, cut["other_group"], ALU.add).then_inc(dve_own, own.one())
            dve.wait_ge(dve_own, own.all())
            dve.tensor_reduce(sc[:, 1:2], mall, AX.X, ALU.max).then_inc(dve_own, own.one())
            dve.wait_ge(dve_own, own.all())
            dve.tensor_scalar(far, far, -1.0, sc[:, 1:2], ALU.mult, ALU.add).then_inc(far_ready, 1)
            dve.wait_ge(sum_spread, 1)
            dve.reciprocal(sc[:, 5:6], banks[:, 3, 0:1]).then_inc(dve_own, own.one())

            prefix, delta, wanted_below = trial[:, 0, 3:4], sc[:, 3:4], sc[:, 9:10]
            dve.memset(sc[:, 6:7], SEG / 2.0).then_inc(dve_own, own.one())
            dve.memset(wanted_below, CAP - 0.5).then_inc(dve_own, own.one())
            dve.wait_ge(far_ready, 1)
            pairs = far.bitcast(U16).rearrange("p (n a) -> p n a", a=2)
            for half, dst in ((1, upper), (0, lower)):
                dve.tensor_copy(dst, pairs[:, :, half:half + 1].rearrange("p n a -> p (n a)")).then_inc(dve_own, own.one())
            dve.wait_ge(sum_ready, 1)
            for phase, source in enumerate((upper, lower)):
                dve.tensor_copy(trial[:, 0, :], cut["trials"][:, 0:4]).then_inc(trials_ready, 1)
                for i in own.loop(0, ROUNDS // 2, 2):
                    for k in range(2):
                        turn = 2 * i + ((ROUNDS + 1) * phase + k + 1)
                        dve.wait_ge(trials_ready, turn)
                        for n in range(2):
                            ins = dve.tensor_scalar(marks[n], source, trial[:, k, n:n + 1], None, ALU.is_lt, ALU.add,
                                                    accum_out=sc[:, 12 + n:13 + n])
                        ins.then_inc(count_ready, 1)
                        dve.wait_ge(count_spread, turn)
                        dve.scalar_tensor_tensor(passed[:, :], banks[:, 4, 0:3], wanted_below,
                                                 cut["units"][:, bass.ds(i * 6 + 3 * k, 3)], ALU.is_lt, ALU.mult,
                                                 accum_out=delta).then_inc(dve_own, own.one())
                        dve.wait_ge(dve_own, own.all())
                        dve.tensor_scalar(trial[:, 1 - k, :], cut["trials"][:, bass.ds(i * 8 + 4 * (k + 1), 4)],
                                          trial[:, k, 3:4], delta, ALU.add, ALU.add).then_inc(trials_ready, 1)
                dve.wait_ge(trials_ready, (ROUNDS + 1) * (phase + 1))
                dve.tensor_copy(sc[:, 15:16].bitcast(U16)[:, 1 - phase:2 - phase], prefix).then_inc(dve_own, own.one())
                if phase == 0:
                    dve.tensor_scalar(marks[1], upper, prefix, None, ALU.is_lt, ALU.add,
                                      accum_out=sc[:, 2:3]).then_inc(count_ready, 1)
                    dve.wait_ge(count_ready, ROUNDS + 1)
                    dve.tensor_scalar(marks[0], upper, prefix, 65535.0, ALU.not_equal, ALU.mult).then_inc(dve_own, own.one())
                    dve.wait_ge(dve_own, own.all())
                    dve.tensor_tensor(lower, lower, marks[0], ALU.max).then_inc(dve_own, own.one())
                    dve.wait_ge(count_spread, ROUNDS + 1)
                    dve.tensor_scalar(wanted_below, banks[:, 4, 3:4], -1.0, CAP - 0.5, ALU.mult, ALU.add).then_inc(dve_own, own.one())
                    dve.wait_ge(dve_own, own.all())
            dve.wait_ge(dve_own, own.all())
            dve.tensor_scalar(seen, far, sc[:, 15:16], None, ALU.is_lt, ALU.add,
                              accum_out=sc[:, 2:3]).then_inc(count_ready, 1)
            dve.wait_ge(count_spread, 2 * (ROUNDS + 1))
            dve.tensor_scalar(sc[:, 11:12], banks[:, 4, 4:5], -1.0, float(CAP), ALU.mult, ALU.add).then_inc(dve_own, own.one())
            dve.wait_ge(dve_own, own.all())
            for n, column in enumerate((15, 11, 1, 5)):
                ins = dve.tensor_scalar(spread_in[:, n, :], cut["first_of_expert"], sc[:, column:column + 1], None, ALU.mult)
            ins.then_inc(spread_in_ready, 1)
            dve.wait_ge(spread_done, 1)
            dve.tensor_copy(spread[:, :, :].rearrange("p a b -> p (a b)"), banks[:, 5, 0:4 * E]).then_inc(dve_own, own.one())

            dve.memset(keep[:, :, :], 1.0).then_inc(dve_own, own.one())
            dve.wait_ge(dve_own, own.all())
            dve.memset(keep[:, :, 0:1], 0.0).then_inc(dve_own, own.one())
            dve.wait_ge(gone_in, 32)
            dve.wait_ge(dve_own, own.all())
            for half in range(2):
                part = slice(half * E, (half + 1) * E)
                cutoff = spread[:, 0, :].unsqueeze(2).broadcast_to([P, E, L])
                dve.tensor_tensor(below[:, part], gone[:, part], cutoff, ALU.is_lt).then_inc(dve_own, own.one())
                dve.tensor_tensor(equal[:, part], gone[:, part], cutoff, ALU.is_equal).then_inc(dve_own, own.one())
            dve.wait_ge(dve_own, own.all())
            flat = lambda a: a[:, :, :].rearrange("p a b -> p (a b)")
            dve.tensor_tensor_scan(flat(n_below), flat(keep), flat(below), 0.0, ALU.mult, ALU.add).then_inc(dve_own, own.one())
            dve.tensor_tensor_scan(flat(n_equal), flat(keep), flat(equal), 0.0, ALU.mult, ALU.add).then_inc(dve_own, own.one())
            dve.wait_ge(dve_own, own.all())
            for n, a in enumerate((n_below, n_equal)):
                dve.tensor_copy(tot[:, :, n * E:(n + 1) * E],
                                a[:, :, L - 1:L].rearrange("p (h e) a -> p h (e a)", h=2)).then_inc(totals_ready, 1)
            dve.wait_ge(offsets_ready, 1)
            dve.tensor_copy(off[:, :, :].rearrange("p a b -> p (a b)"), banks[:, 6, 0:32]).then_inc(dve_own, own.one())
            dve.wait_ge(dve_own, own.all())
            wanted = spread[:, 1, :].unsqueeze(1).broadcast_to([P, 2, E])
            halves = lambda n: blocks_[:, n, :].rearrange("p (h e) -> p h e", h=2)
            dve.tensor_tensor(halves(0), wanted, off[:, :, E:2 * E], ALU.subtract).then_inc(dve_own, own.one())
            dve.tensor_tensor(halves(1), wanted, off[:, :, E:2 * E], ALU.min).then_inc(dve_own, own.one())
            dve.wait_ge(dve_own, own.all())
            dve.tensor_scalar(blocks_[:, 0, :], blocks_[:, 0, :], 0.0, None, ALU.max).then_inc(dve_own, own.one())
            dve.tensor_tensor(halves(1), halves(1), off[:, :, 0:E], ALU.add).then_inc(dve_own, own.one())
            dve.wait_ge(dve_own, own.all())
            dve.tensor_tensor(n_equal[:, :, :], n_equal[:, :, :],
                              blocks_[:, 0, :].unsqueeze(2).broadcast_to([P, TB, L]), ALU.min).then_inc(dve_own, own.one())
            dve.tensor_tensor(n_below[:, :, :], n_below[:, :, :],
                              blocks_[:, 1, :].unsqueeze(2).broadcast_to([P, TB, L]), ALU.add).then_inc(dve_own, own.one())
            dve.wait_ge(dve_own, own.all())
            dve.memset(in_front[0:1, 0:E, :], 0.0).then_inc(dve_own, own.one())
            dve.tensor_tensor(rank[:, :, 0:L], n_below[:, :, :], n_equal[:, :, :], ALU.add).then_inc(dve_own, own.one())
            for n, name in enumerate(("base_high", "base_low")):
                dve.tensor_copy(rank[:, :, L + n:L + n + 1].rearrange("p (h e) a -> p h (e a)", h=2),
                                cut[name].unsqueeze(2).broadcast_to([P, 2, E])).then_inc(dve_own, own.one())
            dve.wait_ge(vectors_in, 64)
            dve.tensor_copy(slots16, slots).then_inc(dve_own, own.one())
            dve.wait_ge(dve_own, own.all())
            dve.nop().then_inc(rank_ready, 1)
            dve.wait_ge(front_in, 32)
            dve.tensor_tensor(rank[:, :, :], rank[:, :, :], in_front[:, :, :], ALU.subtract).then_inc(dve_own, own.one())
            dve.wait_ge(dve_own, own.all())

            def mark(e):
                if e:
                    dve.wait_ge(row_ready, 2 * e)
                for half in range(2):
                    ins = dve.tensor_scalar(onehot[:, half, :], slots16, blocks_[:, 1, half * E + e:half * E + e + 1],
                                            None, ALU.is_ge)
                ins.then_inc(onehot_ready, 1)

            def choose(e):
                for q in range(2):
                    dve.wait_ge(row_ready, 2 * e + q + 1)
                    rows = banks[:, 7, 0:4 * (L + 2)].rearrange("p (m t) -> p m t", m=4)
                    dve.tensor_tensor(marked[:, :, :], rows[:, :, 0:L],
                                      cut["slot_numbers"][:, 4 * q:4 * q + 4].unsqueeze(2).broadcast_to([P, 4, L]),
                                      ALU.is_le).then_inc(dve_own, own.one())
                    dve.tensor_copy(base2[:, :, :], rows[:, :, L:L + 2]).then_inc(row_used, 1)
                    dve.wait_ge(dve_own, own.all())
                    dve.wait_ge(row_used, 2 * e + q + 1)
                    dve.tensor_reduce(place[:, 0, :], marked[:, :, :], AX.X, ALU.add).then_inc(dve_own, own.one())
                    dve.scalar_tensor_tensor(place[:, 1, :], base2[:, :, 0], float(P), base2[:, :, 1],
                                             ALU.mult, ALU.add).then_inc(dve_own, own.one())
                    dve.wait_ge(dve_own, own.all())
                    dve.tensor_tensor(index[:, e * SLOT_TILES + 4 * q:e * SLOT_TILES + 4 * q + 4], place[:, 0, :],
                                      place[:, 1, :], ALU.add).then_inc(index_ready, 1)
                dve.wait_ge(index_ready, 2 * e + 2)
                if e + 1 < E:
                    mark(e + 1)

            def prepare(e):
                slot = e % 3
                dve.wait_ge(found_in[e % 2], 128 * (e // 2 + 1))
                for m in range(SLOT_TILES):
                    ins = dve.bn_stats(fstats[:, m, :], found[:, e * SLOT_TILES + m, :])
                ins.then_inc(dve_own, own.one())
                dve.wait_ge(dve_own, own.all())
                mean0, sq0, mean1, sq1 = (fstats[:, :, n] for n in (1, 2, 4, 5))
                diff, total, half_var, mean_sum, rstd, mean, shift, score = (
                    fsmall[:, slot, n, :] for n in range(8))
                square = diff
                dve.tensor_tensor(diff, mean0, mean1, ALU.subtract).then_inc(dve_own, own.one())
                dve.tensor_tensor(total, sq0, sq1, ALU.add).then_inc(dve_own, own.one())
                dve.tensor_tensor(mean_sum, mean0, mean1, ALU.add).then_inc(dve_own, own.one())
                dve.wait_ge(dve_own, own.all())
                dve.tensor_tensor(diff, diff, diff, ALU.mult).then_inc(dve_own, own.one())
                dve.tensor_scalar(mean, mean_sum, 0.5, None, ALU.mult).then_inc(dve_own, own.one())
                dve.wait_ge(dve_own, own.all())
                dve.scalar_tensor_tensor(total, diff, D / 4.0, total, ALU.mult, ALU.add).then_inc(dve_own, own.one())
                dve.wait_ge(dve_own, own.all())
                dve.tensor_scalar(diff, total, 1.0 / D, EPS, ALU.mult, ALU.add).then_inc(dve_own, own.one())
                dve.wait_ge(dve_own, own.all())
                dve.tensor_scalar(rstd.bitcast(I32), diff.bitcast(I32), -0.5, float(0x5f3759df), ALU.mult, ALU.add
                                  ).then_inc(dve_own, own.one())
                dve.tensor_scalar(half_var, diff, -0.5, None, ALU.mult).then_inc(dve_own, own.one())
                for _ in range(3):
                    dve.wait_ge(dve_own, own.all())
                    dve.tensor_tensor(square, rstd, rstd, ALU.mult).then_inc(dve_own, own.one())
                    dve.wait_ge(dve_own, own.all())
                    dve.tensor_tensor(square, square, half_var, ALU.mult).then_inc(dve_own, own.one())
                    dve.wait_ge(dve_own, own.all())
                    dve.scalar_tensor_tensor(rstd, square, 1.5, rstd, ALU.add, ALU.mult).then_inc(dve_own, own.one())
                dve.wait_ge(dve_own, own.all())
                dve.scalar_tensor_tensor(shift, mean, -1.0, rstd, ALU.mult, ALU.mult).then_inc(rstd3_ready, 1)
                for m in range(SLOT_TILES):
                    ins = dve.scalar_tensor_tensor(adds[:, e * SLOT_TILES + m, :], found[:, e * SLOT_TILES + m, :],
                                                   mean[:, m:m + 1], wr_all[:, :, e], ALU.subtract, ALU.mult,
                                                   accum_out=score[:, m:m + 1])
                ins.then_inc(dve_own, own.one())
                dve.wait_ge(dve_own, own.all())
                dve.tensor_tensor(score, score, rstd, ALU.mult).then_inc(dve_own, own.one())
                dve.wait_ge(dve_own, own.all())
                dve.tensor_tensor(score, score, spread[:, 2, e:e + 1].broadcast_to([P, SLOT_TILES]),
                                  ALU.subtract).then_inc(score_ready, 1)

            def collect(e):
                weight = fsmall[:, e % 3, 3, :]
                dve.wait_ge(weight_ready, e + 1)
                dve.tensor_tensor(weight, fsmall[:, e % 3, 1, :],
                                  spread[:, 3, e:e + 1].broadcast_to([P, SLOT_TILES]), ALU.mult).then_inc(dve_own, own.one())
                for g in range(2):
                    dve.wait_ge(down_ready, 2 * e + g + 1)
                    dst = adds[:, e * SLOT_TILES + 4 * g:e * SLOT_TILES + 4 * g + 4, :]
                    dve.tensor_tensor(dst, banks[:, 5 + g, :].rearrange("p (m d) -> p m d", m=4),
                                      b2_all[:, e:e + 1, :].broadcast_to([P, 4, D]), ALU.add).then_inc(down_copied, 1)
                    dve.wait_ge(down_copied, 2 * e + g + 1)
                    dve.wait_ge(dve_own, own.all())
                    dve.tensor_tensor(dst, dst, weight[:, 4 * g:4 * g + 4].unsqueeze(2).broadcast_to([P, 4, D]),
                                      ALU.mult).then_inc(adds_ready, 1)

            dve.wait_ge(b1_ready, 1)
            mark(0)
            for e in range(AHEAD):
                choose(e)
            prepare(0)
            prepare(1)
            for e in range(E):
                if 2 * e + AHEAD < E:
                    choose(2 * e + AHEAD)
                if e + 2 < E:
                    prepare(e + 2)
                if 2 * e + 1 + AHEAD < E:
                    choose(2 * e + 1 + AHEAD)
                collect(e)

        @block.gpsimd
        def _(pool):
            pool.memset(natural[:, :], float(np.e)).then_inc(powers_ready, 1)
            pool.memset(powers[:, :], -0.5).then_inc(powers_ready, 1)
            pool.wait_ge(powers_ready, 2)
            for h in range(2):
                if h:
                    pool.wait_ge(t2_ready, 4 * CHUNKS * h)
                for cc in turns(pool, 0, CHUNKS // 2):
                    for slot in range(2):
                        it = 2 * cc + (slot + CHUNKS * h)
                        pool.wait_ge(var_ready, it + 1)
                        pool.tensor_tensor(small[:, slot, 4, :], small[:, slot, 2, :], powers[0:L, :],
                                           ALU.pow).then_inc(rstd_ready, 1)
                        pool.wait_ge(rstd_ready, it + 1)
                        last_tiles = bass.ds(cc * (2 * HB) + (HB * slot + ACT_END), HB - ACT_END)
                        mean, scale = (small[:, slot, n, ACT_END:HB].unsqueeze(2).broadcast_to([L, HB - ACT_END, D])
                                       for n in (5, 4))
                        pool.tensor_tensor(staged[:, 2, 0:HB - ACT_END], hid[:, last_tiles, :], mean,
                                           ALU.subtract).then_inc(centred, 1)
                        pool.wait_ge(centred, it + 1)
                        pool.tensor_tensor(xn[0:L, :, last_tiles].rearrange("p k b -> p b k"), staged[:, 2, 0:HB - ACT_END],
                                           scale, ALU.mult).then_inc(xn_pool, 1)
                pool.wait_ge(y_added, 32 * (h + 1))
                for cc in turns(pool, 0, CHUNKS // 2, peel=h == 0):
                    for slot in range(2):
                        it = 2 * cc + (slot + CHUNKS * h)
                        for n in range(ACT_GROUPS, 4):
                            if due(4 * it + (n - 3)):
                                pool.wait_ge(t2_ready, 4 * it + (n - 3))
                            pool.tensor_copy(staged[:, 2], hid[:, bass.ds(cc * (2 * HB) + (HB * slot + 4 * n), 4), :]
                                             ).then_inc(staged_pool, 1)
                        pool.wait_ge(var2_ready, it + 1)
                        pool.tensor_tensor(small[:, slot, 4, :], small[:, slot, 2, :], powers[0:L, :],
                                           ALU.pow).then_inc(rstd2_ready, 1)
            rows = out.rearrange("b f d -> (b f) d")

            def find(e):
                if e > 1:
                    pool.wait_ge(found_in[e % 2], 128 * (e // 2))
                for m in range(SLOT_TILES):
                    pool.wait_ge(index_ready, 2 * e + m // 4 + 1)
                    n = e * SLOT_TILES + m
                    pool.indirect_dma_start(found[:, n, :], None, rows,
                                            bass.IndirectOffsetOnAxis(ap=index[:, n:n + 1], axis=0)
                                            ).then_inc(found_in[e % 2], 16)

            def numerators(e):
                pool.wait_ge(score_ready, e + 1)
                pool.tensor_tensor(fsmall[:, e % 3, 1, :], natural[:, :], fsmall[:, e % 3, 7, :],
                                   ALU.pow).then_inc(weight_ready, 1)

            def add(e):
                if e:
                    pool.wait_ge(added, 128 * e)
                for m in range(SLOT_TILES):
                    pool.wait_ge(adds_ready, 2 * e + m // 4 + 1)
                    n = e * SLOT_TILES + m
                    pool.indirect_dma_start(rows, bass.IndirectOffsetOnAxis(ap=index[:, n:n + 1], axis=0),
                                            adds[:, n, :], None, compute_op=ALU.add, oob_is_err=True,
                                            bounds_check=ROWS * FRAMES - 1).then_inc(added, 16)

            pool.wait_ge(rows_out, 16 * 16)
            for e in range(AHEAD):
                find(e)
            numerators(0)
            numerators(1)
            for e in range(AHEAD, E):
                find(e)
                if e % 2 == 0 or e == E - 1:
                    numerators(e // 2 if e % 2 == 0 else (E + 1) // 2)
            for slot in range(2):
                pool.wait_ge(found_in[slot], 128 * (E // 2))
            for e in range(E):
                add(e)
                if e + 5 < E:
                    numerators(e + 5)
            pool.wait_ge(added, 128 * E)


_INS = ["x", "L0_attn_nu", "L0_attn_theta", "L0_attn_gamma_real", "L0_attn_gamma_imag",
        "L0_ffn_Wr", "L0_ffn_W1", "L0_ffn_b1", "L0_ffn_W2", "L0_ffn_b2"]


def kernel(**inputs):
    import numpy as _np
    import concourse.bacc as _bacc
    from concourse import mybir as _mybir
    from concourse.bass_utils import run_bass_kernel_spmd as _run

    nc = _bacc.Bacc("TRN2", target_bir_lowering=False, num_devices=1)
    arrays, args = {}, []
    for name in _INS:
        a = _np.ascontiguousarray(inputs[name])
        arrays[f"in_{name}"] = a
        args.append(nc.dram_tensor(f"in_{name}", a.shape, _mybir.dt.from_np(a.dtype), kind="ExternalInput").ap())
    args.append(nc.dram_tensor("out_0", (ROWS, FRAMES, D), _mybir.dt.float32, kind="ExternalOutput").ap())
    build(nc, *args)
    r = _run(nc, [arrays], core_ids=[0])
    return r.results[0]["out_0"]
```

```python
from contextlib import ExitStack

import numpy as np
import concourse.bass as bass
from concourse import mybir

ALU = mybir.AluOpType
ACT = mybir.ActivationFunctionType
AX = mybir.AxisListType
F32 = mybir.dt.float32
F16 = mybir.dt.float16
I32 = mybir.dt.int32
U16 = mybir.dt.uint16

P = 128
D = 128
ROWS, SAMPLES = 32, 120000
FRAMES = SAMPLES // D + 1
TAIL = SAMPLES % D
CHUNKS = 8
L = -(-FRAMES // CHUNKS)
LAST = FRAMES - (CHUNKS - 1) * L
HB = ROWS // 2
COLS = HB * CHUNKS
PADDED = L * CHUNKS
EPS = 1e-5
E, F, CAP = 8, 512, 1024
FC = F // P
GROUPS = ((0, 32), (32, 64), (64, 128))
SEGS = P // E
SEG = ROWS * PADDED // SEGS
ROWS_SEG = ROWS // SEGS
FAR = 1e38
ROUNDS = 8
SLOT_TILES = CAP // P
ALL_FOUND = 2
AHEAD = 4
ROWS_FIRST = 3
RING, SLOTS = 8, 4
TURN = RING * SLOTS
DVE_TILES = 8
ACT_TILES = 4
ACT_MID, ACT_END = DVE_TILES + ACT_TILES // 2, DVE_TILES + ACT_TILES
ACT_GROUPS = 3

TWO_PI = 2 * np.pi
C1 = 6.28125
C2 = float(np.float32(int((TWO_PI - C1) * 2**21) / 2**21))
C3 = float(np.float32(TWO_PI - C1 - C2))
MAGIC = 1.5 * 2.0**23
PI_IN = 3.1415925


def constants():
    k, t = np.arange(D)[:, None].astype(np.float64), np.arange(D)[None, :].astype(np.float64)
    scale = np.full((D, 1), np.sqrt(2.0 / D))
    scale[0, 0] = np.sqrt(1.0 / D)
    basis = (scale * np.cos(np.pi * (2.0 * t + 1.0) * k / (2.0 * D))).astype(np.float32)
    p = np.arange(P)
    times = np.concatenate([np.arange(L + 1), np.arange(L - 1, -1, -1)])
    group = (p[:, None] % E == p[None, :] % E).astype(np.float32)
    block = np.arange(2 * P).reshape(2, P).T
    base = (block // CHUNKS) * FRAMES + (block % CHUNKS) * L
    unit = np.append(4.0 ** np.arange(ROUNDS - 1, -1, -1), 0.0)
    trials = (unit[:, None] * np.array([1, 2, 3, 0]) - np.array([0, 0, 0.5, 0])).reshape(-1)
    units = np.repeat(unit, 3)
    parts = {
        "basis_t": basis.T,
        "identity": np.eye(P),
        "times": np.tile(times, (P, 1)),
        "ones": np.ones((P, P)),
        "group": group,
        "other_group": (group - 1) * 3e38,
        "before": (p[:, None] < p[None, :]),
        "first_of_expert": (p[:, None] == np.arange(E)[None, :]),
        "slot_numbers": p[:, None] + P * np.arange(SLOT_TILES)[None, :],
        "base_high": base // P,
        "base_low": base % P,
        "trials": np.tile(trials, (P, 1)),
        "units": np.tile(units, (P, 1)),
        "slots_row": np.tile(np.arange(CAP), (P, 1)),
    }
    table, at = [], {}
    n = 0
    for name, a in parts.items():
        a = np.ascontiguousarray(a, np.float32) if a.dtype != np.float32 else a
        at[name] = (n, n + a.shape[1])
        n += a.shape[1]
        table.append(a)
    return np.concatenate(table, axis=1), at


class Steps:

    def __init__(self, eng):
        self.eng, self.n, self.base = eng, 0, 0

    def one(self):
        self.n += 1
        return 1

    def all(self):
        return self.base + self.n

    def loop(self, start, end, per, peel=False):
        at = self.n
        first = start
        if peel:
            yield start
            assert self.n == at + per, (self.n - at, per)
            first = start + 1
        with self.eng.Fori(first, end) as i:
            self.base, self.n = i * per + (at - start * per), 0
            yield i
            assert self.n == per, (self.n, per)
        self.base, self.n = 0, at + (end - start) * per


def turns(eng, start, end, peel=False):
    if peel:
        yield start
        start += 1
    with eng.Fori(start, end) as i:
        yield i



def due(value):
    return not isinstance(value, int) or value > 0




def build(nc, x, nu, theta, gamma_r, gamma_i, Wr, W1, b1, W2, b2, out):
    table, at = constants()
    const_dram = nc.inline_tensor(table, name="constants").ap()
    zeros_dram = nc.inline_tensor(np.zeros((HB, D - TAIL), np.float32), name="zeros").ap()
    toeplitz = nc.dram_tensor("toeplitz", [L + 2, D, P], F32).ap()
    away_dram = nc.dram_tensor("away", [E, ROWS * PADDED], F32).ap()
    scales_dram = nc.dram_tensor("scales", [ROWS * PADDED], F32).ap()
    logits_dram = nc.dram_tensor("logits", [E, ROWS * PADDED], F32).ap()
    NC1 = at["slots_row"][0]
    NT = 2 * L + 1

    with ExitStack() as ctx:
        def sb(name, shape, dt=F32):
            return ctx.enter_context(nc.sbuf_tensor(name, shape, dt))

        const = sb("const", [P, NC1])
        cut = {n: const[:, a:b] for n, (a, b) in at.items() if b <= NC1}
        wr_c = sb("wr_c", [P, E])
        mu = sb("mu", [P, 3])
        state_w = sb("state_w", [L, D, 2])
        powers = sb("powers", [P, HB])
        hid_all = sb("hid", [P, COLS, D])
        hid = hid_all[0:L]
        xn_all = sb("xn", [P, D, COLS])
        xn = xn_all[0:L + 2]
        ring = sb("ring", [L + 2, SLOTS, RING, P])
        xin_all = sb("xin", [P, 2, HB, D])
        xin = xin_all[0:L]
        xt_all = sb("xt", [P, 2, 4 * D])
        xt = xt_all[:, :, 0:4 * L].rearrange("p s (a b) -> p s a b", a=4)
        staged = sb("staged", [L, 3, 4, D])
        stats = sb("stats", [L, 2, HB, 6])
        small = sb("small", [L, 2, 7, HB])
        lstage = sb("lstage", [P, 2, 4 * L])
        scales = cut["times"][0:HB, 0:2 * L].rearrange("p (s t) -> p s t", s=2)
        setup = sb("setup", [P, 6, L + P])
        par = sb("par", [P, 6])
        ends = xin_all[:, :, :, :].rearrange("p a b c -> p (a b c)").rearrange("p (r i n) -> p r i n", r=D // 16, i=4)
        e2 = sb("e2", [P, 2, COLS])
        s2 = sb("s2", [P, 2, COLS])
        carry = sb("carry", [P, 2, HB])
        w1_ring = sb("w1_ring", [P, 2, F])
        w2_ring = sb("w2_ring", [P, 2, FC, D])
        b2_all = sb("b2_all", [P, E, D])
        wr_all = sb("wr_all", [P, D, E])
        b1_rows = sb("b1_rows", [E * FC, P])
        b1_cols = sb("b1_cols", [P, E * FC])

        free = {"hid": [hid_all[:, :, :].rearrange("p a b -> p (a b)"), 0],
                "xn": [xn_all[:, :, :].rearrange("p a b -> p (a b)"), 0],
                "xin": [xin_all[:, :, :, :].rearrange("p a b c -> p (a b c)"), 0],
                "setup": [setup[:, :, :].rearrange("p a b -> p (a b)"), 0]}

        def take(where, words):
            region, n = free[where]
            free[where][1] = n + words
            assert n + words <= region.shape[1], where
            return region[:, n:n + words]

        TB = 2 * E
        found = take("hid", E * SLOT_TILES * D).rearrange("p (a b) -> p a b", b=D)
        adds = take("hid", E * SLOT_TILES * D).rearrange("p (a b) -> p a b", b=D)
        far = take("xn", SEG)
        seen = take("xn", SEG)
        take("xn", 2 * FC * 512 - 2 * SEG)
        acts = xn_all[:, :, :].rearrange("p a b -> p (a b)")[:, 0:2 * FC * 512].rearrange(
            "p (s f n) -> p s f n", s=2, f=FC)
        gone = take("xn", TB * L).rearrange("p (a b) -> p a b", b=L)
        normed_at = free["xn"][1]
        work = [take("xn", TB * L) for _ in range(4)]
        upper, lower = (work[0].bitcast(U16)[:, n * SEG:(n + 1) * SEG] for n in range(2))
        marks = [seen.bitcast(U16)[:, n * SEG:(n + 1) * SEG] for n in range(2)]
        far_scale, marks_act = work[1][:, 0:SEG], work[1].bitcast(U16)[:, 0:SEG]
        exps = work[2][:, 0:SEG]
        below, equal, n_below, n_equal = (
            room.bitcast(F16)[:, 0:TB * L].rearrange("p (a b) -> p a b", b=L) for room in work)
        keep = take("xin", TB * L // 2).bitcast(F16).rearrange("p (a b) -> p a b", b=L)
        rank = take("xn", TB * (L + 2) // 2).bitcast(F16).rearrange("p (a b) -> p a b", b=L + 2)
        slots = take("setup", CAP)
        slots16 = take("xin", CAP // 2).bitcast(F16)
        onehot = take("xn", 2 * CAP // 2).bitcast(F16).rearrange("p (a b) -> p a b", b=CAP)
        in_front = take("xin", TB * (L + 2) // 2).bitcast(F16).rearrange("p (a b) -> p a b", b=L + 2)
        sc = sb("sc", [P, 16])
        tot = sb("tot", [P, 2, TB])
        off = sb("off", [P, 2, TB])
        trial = sb("trial", [P, 2, 4])
        passed = sb("passed", [P, 3])
        spread = sb("spread", [P, 4, E])
        spread_in = sb("spread_in", [P, 4, E])
        bounds = sb("bounds", [P, 2, TB])
        mall = take("xin", P)
        mrow = take("xin", P)[0:1, :]
        group16 = take("setup", P // 2).bitcast(F16)
        limits = take("xin", TB).bitcast(F16).rearrange("p (a b) -> p a b", b=TB)
        scores, parts, weight = (take("setup", E * SLOT_TILES).rearrange("p (e m) -> p e m", m=SLOT_TILES)
                                 for _ in range(3))
        counts = sb("counts", [P, 4], F16)
        normed = xn_all[:, :, :].rearrange("p a b -> p (a b)")[
            :, normed_at:normed_at + 2 * SLOT_TILES * D].rearrange("p (s m d) -> p s m d", s=2, m=SLOT_TILES)
        marked = take("xin", 4 * L).rearrange("p (a b) -> p a b", b=L)
        place = sb("place", [P, 3, 4])
        base2 = sb("base2", [P, 4, 2])
        index = sb("index", [P, E * SLOT_TILES], I32)
        fstats = sb("fstats", [P, SLOT_TILES, 6])
        fsmall = sb("fsmall", [P, 3, 7, SLOT_TILES])
        natural = sb("natural", [P, SLOT_TILES])
        banks = ctx.enter_context(nc.psum_tensor("banks", [P, 8, 512], F32))
        def sem(name):
            return ctx.enter_context(nc.semaphore(name))

        const_in = sem("const_in")
        params_in = sem("params_in")
        wr_in = sem("wr_in")
        a_ready = sem("a_ready")
        rate_ready = sem("rate_ready")
        decay_ready = sem("decay_ready")
        reduced_ready = sem("reduced_ready")
        trig_ready = sem("trig_ready")
        tables_ready = sem("tables_ready")
        turned_tables = sem("turned_tables")
        toeplitz_out = sem("toeplitz_out")
        state_w_ready = sem("state_w_ready")
        wr_sum = sem("wr_sum")
        wr_ready = sem("wr_ready")
        kernel_ready = sem("kernel_ready")
        powers_ready = sem("powers_ready")
        dve_own = sem("dve_own")
        xt_ready = sem("xt_ready")
        xt_copied = sem("xt_copied")
        h_ready = sem("h_ready")
        h_copied = sem("h_copied")
        var_ready = sem("var_ready")
        rstd_ready = sem("rstd_ready")
        nb_ready = sem("nb_ready")
        xn_dve = sem("xn_dve")
        xn_act = sem("xn_act")
        centred = sem("centred")
        xn_pool = sem("xn_pool")
        e_ready = sem("e_ready")
        e_copied = sem("e_copied")
        s_ready = sem("s_ready")
        y_ready = sem("y_ready")
        y_added = sem("y_added")
        var2_ready = sem("var2_ready")
        rstd2_ready = sem("rstd2_ready")
        staged_act = sem("staged_act")
        staged_pool = sem("staged_pool")
        t2_ready = sem("t2_ready")
        l_part = sem("l_part")
        t2_copied = sem("t2_copied")
        scales_turned = sem("scales_turned")
        l_copied = sem("l_copied")
        rows_out = sem("rows_out")
        vectors_in = sem("vectors_in")
        logits_in = sem("logits_in")
        far_ready = sem("far_ready")
        lower_ready = sem("lower_ready")
        far_out = sem("far_out")
        gone_in = sem("gone_in")
        sum_ready = sem("sum_ready")
        b1_turned = sem("b1_turned")
        b1_ready = sem("b1_ready")
        peak_ready = sem("peak_ready")
        peak_turned = sem("peak_turned")
        peak_row = sem("peak_row")
        peak_spread = sem("peak_spread")
        sum_spread = sem("sum_spread")
        trials_ready = sem("trials_ready")
        count_ready = sem("count_ready")
        sign_ready = sem("sign_ready")
        count_act = sem("count_act")
        count_spread = sem("count_spread")
        spread_in_ready = sem("spread_in_ready")
        spread_done = sem("spread_done")
        totals_ready = sem("totals_ready")
        offsets_ready = sem("offsets_ready")
        onehot_ready = sem("onehot_ready")
        row_ready = sem("row_ready")
        row_used = sem("row_used")
        index_ready = sem("index_ready")
        rank_ready = sem("rank_ready")
        steps_ready = sem("steps_ready")
        front_in = sem("front_in")
        rstd3_ready = sem("rstd3_ready")
        norm_ready = sem("norm_ready")
        score_ready = sem("score_ready")
        weight_ready = sem("weight_ready")
        ft_ready = sem("ft_ready")
        ft_copied = sem("ft_copied")
        up_ready = sem("up_ready")
        gelu_ready = sem("gelu_ready")
        down_ready = sem("down_ready")
        down_copied = sem("down_copied")
        adds_ready = sem("adds_ready")
        added = sem("added")
        e_moved = [sem(f"e_moved{group}") for group in range(3)]
        s_moved = [sem(f"s_moved{group}") for group in range(3)]
        x_in = [sem(f"x_in{slot}") for slot in range(2)]
        ring_in = [sem(f"ring_in{slot}") for slot in range(SLOTS)]
        l_out = [sem(f"l_out{slot}") for slot in range(2)]
        weights_in = [sem(f"weights_in{slot}") for slot in range(2)]
        found_in = [sem(f"found_in{slot}") for slot in range(2)]

        def frames(h, c, rows):
            return bass.AP(x.tensor, c * (L * D) + h * HB * SAMPLES, [[D, rows], [SAMPLES, HB], [1, D]])

        def out_rows(h, c, rows):
            return bass.AP(out.tensor, c * (L * D) + h * HB * FRAMES * D, [[D, rows], [FRAMES * D, HB], [1, D]])

        R_, ANG, RED, SIN, COS, Q = (setup[:, n, 0:NT] for n in range(6))
        KPAD = setup[:, 0, 0:L - 1 + P]

        block = ctx.enter_context(nc.Block())

        @block.sync
        def _(sp):
            sp.dma_start(const[:, :], const_dram[:, 0:NC1]).then_inc(const_in, 16)
            for n, v in enumerate((nu, theta, gamma_r, gamma_i)):
                sp.dma_start(par[:, n:n + 1], v.rearrange("(p a) -> p a", a=1)).then_inc(params_in, 16)
            sp.dma_start(wr_c[:, :], Wr).then_inc(wr_in, 16)
            step = setup[:, 0, :].ap[0][0]

            def toeplitz_rows(j):
                rows = bass.AP(KPAD.tensor, KPAD.offset + 16 * j * step + L - 1, [[step, 16], [-1, L], [1, P]])
                sp.dma_start(bass.AP(toeplitz.tensor, 16 * j * P, [[P, 16], [D * P, L], [1, P]]),
                             rows).then_inc(toeplitz_out, 16)

            def weights(e, slot):
                sp.dma_start(w1_ring[:, slot], bass.AP(W1.tensor, e * (D * F) + slot * D * F,
                                                       [[F, D], [1, F]])).then_inc(weights_in[slot], 16)
                sp.dma_start(w2_ring[:, slot], bass.AP(W2.tensor, e * (D * F) + slot * D * F,
                                                       [[D, P], [P * D, FC], [1, D]])).then_inc(weights_in[slot], 16)

            def load_logits(half):
                for dst, src, step in ((far_scale, scales_dram, 0), (far, logits_dram, ROWS * PADDED)):
                    sp.dma_start(dst[half * P // 2:(half + 1) * P // 2, :],
                                 bass.AP(src.tensor, half * (SEGS // 2) * SEG, [[SEG, SEGS // 2], [step, E], [1, SEG]])
                                 ).then_inc(logits_in, 16)

            for h in range(2):
                if h == 0:
                    for c in range(CHUNKS - 2):
                        if c >= 2:
                            sp.wait_ge(xt_ready, 4 * c - 4)
                        sp.dma_start(xin[:, c % 2], frames(h, c, L)).then_inc(x_in[c % 2], 16)
                        if c == 2:
                            sp.wait_ge(kernel_ready, 4)
                            sp.dma_start(bass.AP(toeplitz.tensor, L * D * P, [[P, D], [D * P, 2], [1, P]]),
                                         setup[:, 3:5, 1:P + 1]).then_inc(toeplitz_out, 16)
                        if c >= 2:
                            toeplitz_rows(2 * c - 4)
                            toeplitz_rows(2 * c - 3)
                else:
                    with sp.Fori(1, CHUNKS // 2 - 1) as cc:
                        for slot in range(2):
                            sp.wait_ge(xt_ready, 8 * cc + (4 * slot + 32 * h - 4))
                            sp.dma_start(xin[:, slot], frames(h, 2 * cc + slot, L)).then_inc(x_in[slot], 16)
                sp.wait_ge(xt_ready, 32 * h + 20)
                sp.dma_start(xin[:, 0], frames(h, CHUNKS - 2, L)).then_inc(x_in[0], 16)
                sp.wait_ge(xt_ready, 32 * h + 24)
                sp.dma_start(xin[0:LAST - 1, 1], frames(h, CHUNKS - 1, LAST - 1)).then_inc(x_in[1], 16)
                tail = bass.AP(x.tensor, h * HB * SAMPLES + (FRAMES - 1) * D, [[1, 1], [SAMPLES, HB], [1, TAIL]])
                sp.dma_start(xin[LAST - 1:LAST, 1, :, 0:TAIL], tail).then_inc(x_in[1], 16)
                sp.dma_start(xin[LAST - 1:LAST, 1, :, TAIL:D],
                             zeros_dram.rearrange("(a b) c -> a b c", a=1)).then_inc(x_in[1], 16)

                if h == 0:
                    sp.wait_ge(toeplitz_out, 16 * 9)
                def fill(i, slot):
                    if due(8 * i + (2 * slot + 32 * h - 6)):
                        sp.wait_ge(y_ready, 8 * i + (2 * slot + 32 * h - 6))
                    sp.dma_start(ring[:, slot].rearrange("p k t -> p (k t)"), bass.AP(
                        toeplitz.tensor, i * (TURN * P) + slot * RING * P,
                        [[D * P, L + 2], [1, RING * P]])).then_inc(ring_in[slot], 16)

                for slot in range(SLOTS):
                    fill(0, slot)

                def move_ends(g):
                    first, end = GROUPS[g]
                    sp.wait_ge(e_copied, 8 * h + end // 16)
                    for ri in range(2):
                        sp.dma_start(e2[first:end, ri, :],
                                     ends[ri:97 + ri:32, first // 16:end // 16]).then_inc(e_moved[g], 16)

                def move_states(g):
                    first, end = GROUPS[g]
                    sp.wait_ge(s_ready, 3 * h + g + 1)
                    for ri in range(2):
                        sp.dma_start(xn[L + ri:L + ri + 1, first:end, :], s2[first:end, ri, :]).then_inc(s_moved[g], 16)

                for g in range(2):
                    move_ends(g)
                for g in range(2):
                    move_states(g)
                move_ends(2)
                for slot in range(SLOTS):
                    fill(1, slot)
                move_states(2)
                with sp.Fori(2, D // TURN) as i:
                    for slot in range(SLOTS):
                        fill(i, slot)

                if h == 0:
                    for slot in range(2):
                        sp.dma_start(xin[:, slot], frames(1, slot, L)).then_inc(x_in[slot], 16)
                else:
                    sp.dma_start(b2_all[:, :, :].rearrange("p e d -> p (e d)"),
                                 bass.AP(b2.tensor, 0, [[0, P], [1, E * D]])).then_inc(vectors_in, 16)
                    sp.dma_start(wr_all[:, :, :].rearrange("p d e -> p (d e)"),
                                 bass.AP(Wr.tensor, 0, [[0, P], [1, E * D]])).then_inc(vectors_in, 16)
                    sp.dma_start(b1_rows[:, :], b1.rearrange("e (f p) -> (e f) p", p=P)).then_inc(vectors_in, 16)
                    sp.dma_start(slots, const_dram[:, NC1:NC1 + CAP]).then_inc(vectors_in, 16)
                    for slot in range(2):
                        weights(0, slot)

                    sp.wait_ge(l_out[0], 80 * CHUNKS // 2)
                    sp.wait_ge(l_out[1], 80 * CHUNKS // 2)
                    sp.wait_ge(y_ready, 64)
                    load_logits(0)

                def store_logits(c, slot):
                    for j in range(4):
                        sp.dma_start(
                            bass.AP(logits_dram.tensor, c * L + (h * HB + 4 * j) * PADDED,
                                    [[ROWS * PADDED, E], [PADDED, 4], [1, L]]),
                            lstage[32 * j:32 * j + E, slot, :].rearrange("p (b t) -> p b t", b=4),
                        ).then_inc(l_out[slot], 16)
                    sp.dma_start(bass.AP(scales_dram.tensor, c * L + h * HB * PADDED, [[PADDED, HB], [1, L]]),
                                 scales[:, slot, :]).then_inc(l_out[slot], 16)

                sp.wait_ge(y_added, 32 * (h + 1))
                def store_rows(c):
                    rows = LAST if c == CHUNKS - 1 else L
                    sp.dma_start(out_rows(h, c, rows), hid[0:rows, HB * c:HB * (c + 1), :]).then_inc(rows_out, 16)

                for c in range(ROWS_FIRST):
                    store_rows(c)
                for c in range(CHUNKS):
                    sp.wait_ge(l_copied, c + (CHUNKS * h + 1))
                    store_logits(c, c % 2)
                    if c + ROWS_FIRST < CHUNKS:
                        store_rows(c + ROWS_FIRST)
            sp.wait_ge(rows_out, 16 * 16)
            sp.wait_ge(l_out[0], 80 * 8)
            sp.wait_ge(l_out[1], 80 * 8)
            sp.wait_ge(y_ready, 64)
            load_logits(1)
            sp.wait_ge(far_ready, 1)
            sp.dma_start(bass.AP(away_dram.tensor, 0, [[SEG, SEGS], [ROWS * PADDED, E], [1, SEG]]),
                         far).then_inc(far_out, 16)
            sp.wait_ge(far_out, 16)
            for half in range(2):
                sp.dma_start(gone[:, half * E:(half + 1) * E, :],
                             bass.AP(away_dram.tensor, half * P * L, [[L, P], [ROWS * PADDED, E], [1, L]])
                             ).then_inc(gone_in, 16)
            sp.wait_ge(rank_ready, 1)
            sp.dma_start(in_front[1:P, :, :], rank[0:P - 1, :, :]).then_inc(front_in, 16)
            sp.dma_start(in_front[0:1, E:TB, :], rank[P - 1:P, 0:E, :]).then_inc(front_in, 16)
            with sp.Fori(1, E // 2) as i:
                for slot in range(2):
                    sp.wait_ge(down_ready, i * 4 + (2 * slot - 2))
                    weights(i * 2, slot)

        @block.scalar
        def _(act):
            act.wait_ge(params_in, 64)
            act.activation(par[:, 4:5], par[:, 0:1], ACT.Exp).then_inc(a_ready, 1)
            act.wait_ge(const_in, 16)
            act.wait_ge(rate_ready, 1)
            act.activation(R_, cut["times"], ACT.Exp, scale=par[:, 5:6]).then_inc(decay_ready, 1)
            act.wait_ge(reduced_ready, 1)
            act.activation(SIN, RED, ACT.Sin).then_inc(trig_ready, 1)
            act.wait_ge(reduced_ready, 2)
            act.activation(COS, ANG, ACT.Sin).then_inc(trig_ready, 1)
            for h in range(2):
                def copy_xt(n, G):
                    act.wait_ge(xt_ready, G + 1)
                    if due(G - 1):
                        act.wait_ge(h_ready, G - 1)
                    act.activation(xt[:, n % 2], banks[:, n % 2, 0:4 * L].rearrange("p (a b) -> p a b", a=4),
                                   ACT.Copy).then_inc(xt_copied, 1)

                def copy_h(n, slot, G, cc):
                    act.wait_ge(h_ready, G + 1)
                    act.activation(hid[:, bass.ds(cc * (2 * HB) + (HB * slot + 4 * n), 4), :],
                                   banks[0:L, 2 + n % 4, :].rearrange("p (a b) -> p a b", a=4),
                                   ACT.Copy).then_inc(h_copied, 1)

                def normalise(c, slot, first, last):
                    if first == DVE_TILES:
                        act.wait_ge(nb_ready, c + (CHUNKS * h + 1))
                    for b in range(first, last):
                        ins = act.activation(xn[0:L, :, bass.ds(c * HB + b, 1)].rearrange("p k a -> p (k a)"),
                                             hid[:, bass.ds(c * HB + b, 1), :].rearrange("p a k -> p (a k)"),
                                             ACT.Identity, bias=small[:, slot, 6, b:b + 1],
                                             scale=small[:, slot, 4, b:b + 1])
                    if last == ACT_END:
                        ins.then_inc(xn_act, 1)


                def chunk(cc, slot, first=False, last=False):
                    G0 = 8 * cc + (4 * slot + 32 * h)
                    for n in range(4):
                        if not (last and n == 3):
                            copy_xt(n + 1, G0 + (n + 1))
                        copy_h(n, slot, G0 + n, cc)
                        if n >= 2 and not first:
                            normalise(2 * cc + (slot - 1), 1 - slot, *((DVE_TILES, ACT_MID), (ACT_MID, ACT_END))[n - 2])

                if h:
                    act.wait_ge(rows_out, 16 * CHUNKS)
                    act.wait_ge(l_part, 4 * CHUNKS)
                copy_xt(0, 32 * h)
                chunk(0, 0, first=True)
                chunk(0, 1)
                for cc in turns(act, 1, CHUNKS // 2 - 1):
                    for slot in range(2):
                        chunk(cc, slot)
                if h == 0:
                    for n in range(2):
                        act.wait_ge(turned_tables, n + 1)
                        act.activation(state_w[:, :, n], banks[0:L, 6 + n, 0:D], ACT.Copy).then_inc(state_w_ready, 1)
                chunk(CHUNKS // 2 - 1, 0)
                chunk(CHUNKS // 2 - 1, 1, last=True)
                normalise(CHUNKS - 1, 1, DVE_TILES, ACT_END)

                for r in range(8):
                    act.wait_ge(e_ready, 8 * h + r + 1)
                    act.activation(ends[0:98, r], banks[0:98, 6 + r % 2, :].rearrange("p (a b) -> p a b", a=4),
                                   ACT.Copy).then_inc(e_copied, 1)

                def stage(c, n):
                    it = c + CHUNKS * h
                    before = (4 * it - 1, 4 * it - 2, 4 * it + 1)[n]
                    if due(before):
                        act.wait_ge(t2_ready, before)
                    act.activation(staged[:, n % 2], hid[:, bass.ds(c * HB + 4 * n, 4), :],
                                   ACT.Copy).then_inc(staged_act, 1)

                def logits_out(c, slot, stored):
                    it = c + CHUNKS * h
                    act.wait_ge(l_part, 4 * it + 4)
                    if due(stored):
                        act.wait_ge(l_out[slot], stored)
                    act.activation(lstage[0:104, slot, :], banks[0:104, 4 + slot, 0:4 * L], ACT.Copy)
                    act.wait_ge(scales_turned, it + 1)
                    act.activation(scales[:, slot, :], banks[0:HB, 6 + slot, 0:L], ACT.Copy).then_inc(l_copied, 1)

                def turned(cc, slot, stored=None, last=False):
                    c = 2 * cc + slot
                    for n in range(4):
                        if n < ACT_GROUPS - 1:
                            stage(c, n + 1)
                        elif n == 3 and not last:
                            stage(c + 1, 0)
                        G = 4 * c + (n + 32 * h)
                        act.wait_ge(t2_ready, G + 1)
                        if due(G - 1):
                            act.wait_ge(l_part, G - 1)
                        act.activation(xt[:, n % 2], banks[:, n % 2, 0:4 * L].rearrange("p (a b) -> p a b", a=4),
                                       ACT.Copy).then_inc(t2_copied, 1)
                        if n == 1 and stored is not None:
                            logits_out(c - 1, 1 - slot, stored)

                act.wait_ge(y_added, 32 * (h + 1))
                stage(0, 0)
                turned(0, 0)
                turned(0, 1, 320 * h)
                with act.Fori(1, CHUNKS // 2 - 1) as cc:
                    turned(cc, 0, 80 * cc + (320 * h - 80))
                    turned(cc, 1, 80 * cc + 320 * h)
                cc = CHUNKS // 2 - 1
                turned(cc, 0, 80 * cc + (320 * h - 80))
                turned(cc, 1, 80 * cc + 320 * h, last=True)
                logits_out(2 * cc + 1, 1, 80 * cc + 320 * h)

            act.wait_ge(far_ready, 1)
            act.activation(exps, far, ACT.Exp, scale=-1.0, accum_out=sc[:, 4:5]).then_inc(sum_ready, 1)
            for phase, source in enumerate((upper, lower)):
                for i in turns(act, 0, ROUNDS // 2):
                    for k in range(2):
                        act.wait_ge(trials_ready, 2 * i + ((ROUNDS + 1) * phase + k + 1))
                        act.activation(marks_act, source, ACT.Sign, scale=-1.0, bias=trial[:, k, 2:3],
                                       accum_out=sc[:, 7:8]).then_inc(sign_ready, 1)
                        act.wait_ge(sign_ready, 2 * i + (ROUNDS * phase + k + 1))
                        act.activation(counts[:, 2:3], sc[:, 7:8], ACT.Identity, scale=0.5, bias=sc[:, 6:7]
                                       ).then_inc(count_act, 1)
            act.activation(sc[:, 7:8], sc[:, 7:8], ACT.Gelu)
            act.wait_ge(b1_turned, 1)
            act.activation(b1_cols[:, :], banks[:, 2, 0:E * FC], ACT.Copy).then_inc(b1_ready, 1)

            def normalise_rows(e):
                act.wait_ge(rstd3_ready, e + 1)
                for m in range(SLOT_TILES):
                    ins = act.activation(normed[:, e % 2, m, :], found[:, e * SLOT_TILES + m, :], ACT.Identity,
                                         bias=fsmall[:, e % 3, 6, m:m + 1], scale=fsmall[:, e % 3, 4, m:m + 1])
                    if m % 4 == 3:
                        ins.then_inc(norm_ready, 1)

            normalise_rows(0)
            for e in range(E):
                for g in range(2):
                    n = 2 * e + g
                    act.wait_ge(ft_ready, n + 1)
                    act.activation(xt_all[:, g], banks[:, 0, :], ACT.Copy).then_inc(ft_copied, 1)
                    if g and e + 1 < E:
                        normalise_rows(e + 1)
                    if n >= 2:
                        act.wait_ge(down_ready, n - 1)
                    for f in range(FC):
                        act.wait_ge(up_ready, FC * n + f + 1)
                        act.activation(acts[:, g, f], banks[:, 1 + f, :], ACT.Gelu,
                                       bias=b1_cols[:, FC * e + f:FC * e + f + 1]).then_inc(gelu_ready, 1)

        @block.tensor
        def _(pe):
            pe.wait_ge(const_in, 16)
            pe.wait_ge(wr_in, 16)
            pe.matmul(banks[:, 2, 0:E], cut["ones"], wr_c[:, :], start=True, stop=True).then_inc(wr_sum, 1)
            pe.wait_ge(wr_ready, 1)
            for h in range(2):
                def turn(n, G, cc, x1):
                    if n == 0:
                        pe.wait_ge(x_in[0], 16 * cc + (64 * h + 16))
                    if n == 4:
                        pe.wait_ge(x_in[1], x1)
                    if due(G - 1):
                        pe.wait_ge(xt_copied, G - 1)
                    for i in range(4):
                        mm = pe.transpose(banks[:, n % 2, i * L:(i + 1) * L], xin[:, n // 4, 4 * (n % 4) + i, :],
                                          cut["identity"][0:L, 0:L])
                    mm.then_inc(xt_ready, 1)

                def dct(n, G):
                    pe.wait_ge(xt_copied, G + 1)
                    if due(G - 3):
                        pe.wait_ge(h_copied, G - 3)
                    for i in range(4):
                        mm = pe.matmul(banks[0:L, 2 + n % 4, i * D:(i + 1) * D], xt[:, n % 2, i, :],
                                       cut["basis_t"], start=True, stop=True)
                    mm.then_inc(h_ready, 1)

                def eight(cc, x1):
                    G0 = 8 * cc + 32 * h
                    turn(0, G0, cc, x1)
                    for n in range(8):
                        if n < 7:
                            turn(n + 1, G0 + (n + 1), cc, x1)
                        dct(n, G0 + n)

                if due(32 * h):
                    pe.wait_ge(t2_copied, 32 * h)
                for cc in turns(pe, 0, CHUNKS // 2 - 1, peel=h == 0):
                    eight(cc, 16 * cc + (96 * h + 16))
                if h == 0:
                    pe.wait_ge(tables_ready, 2)
                    for n, src in enumerate((ANG, RED)):
                        pe.transpose(banks[0:L, 6 + n, 0:D], src[:, L + 1:NT],
                                     cut["identity"]).then_inc(turned_tables, 1)
                eight(CHUNKS // 2 - 1, 96 * h + 96)

                pe.wait_ge(state_w_ready, 2)
                pe.wait_ge(xn_dve, CHUNKS * (h + 1) - 1)
                pe.wait_ge(xn_act, CHUNKS * (h + 1) - 1)
                pe.wait_ge(xn_pool, CHUNKS * (h + 1) - 1)
                if due(CHUNKS * h):
                    pe.wait_ge(l_copied, CHUNKS * h)
                for r in range(8):
                    if due(8 * h + r - 1):
                        pe.wait_ge(e_copied, 8 * h + r - 1)
                    first, end = next(group for group in GROUPS if 16 * r < group[1])
                    for i in range(4):
                        for j in range(4):
                            k = first + (end - first) // 4 * j + 4 * (r - first // 16) + i
                            mm = pe.matmul(banks[32 * j:32 * j + 2, 6 + r % 2, i * COLS:(i + 1) * COLS - HB],
                                           state_w[:, k, :], xn[0:L, k, 0:COLS - HB], start=True, stop=True)
                    mm.then_inc(e_ready, 1)

                def products(i):
                    for n in range(8):
                        slot = n // 2
                        if n % 2 == 0:
                            pe.wait_ge(ring_in[slot], 16 * i + (64 * h + 16))
                        if due(8 * i + (n + 32 * h - 3)):
                            pe.wait_ge(y_added, 8 * i + (n + 32 * h - 3))
                        for q in range(4):
                            mm = pe.matmul(banks[0:L, 2 + n % 4, q * COLS:(q + 1) * COLS],
                                           ring[:, slot, 4 * (n % 2) + q, 0:L],
                                           xn[:, bass.ds(i * TURN + 4 * n + q, 1), :].rearrange("p a n -> p (a n)"),
                                           start=True, stop=True)
                        mm.then_inc(y_ready, 1)

                pe.wait_ge(xn_dve, CHUNKS * (h + 1))
                pe.wait_ge(xn_act, CHUNKS * (h + 1))
                pe.wait_ge(xn_pool, CHUNKS * (h + 1))
                for i in range(D // TURN):
                    pe.wait_ge(s_moved[min(i, 2)], 32 * (h + 1))
                    products(i)

                def turn2(n, c):
                    it = c + CHUNKS * h
                    if n < ACT_GROUPS:
                        pe.wait_ge(staged_act, it * ACT_GROUPS + (n + 1))
                    else:
                        pe.wait_ge(staged_pool, it * (4 - ACT_GROUPS) + (n - ACT_GROUPS + 1))
                    if due(4 * it + (n - 1)):
                        pe.wait_ge(t2_copied, 4 * it + (n - 1))
                    for i in range(4):
                        mm = pe.transpose(banks[:, n % 2, i * L:(i + 1) * L], staged[:, 2 if n == 3 else n % 2, i, :],
                                          cut["identity"][0:L, 0:L])
                    mm.then_inc(t2_ready, 1)

                def logits(n, c, slot):
                    it = c + CHUNKS * h
                    pe.wait_ge(t2_copied, 4 * it + (n + 1))
                    if n == 0 and due(it - 1):
                        pe.wait_ge(l_copied, it - 1)
                    pe.matmul(banks[32 * n:32 * n + E, 4 + slot, 0:4 * L], wr_c[:, :], xt_all[:, n % 2, 0:4 * L],
                              start=True, stop=True).then_inc(l_part, 1)

                def turn_scales(c, slot):
                    it = c + CHUNKS * h
                    pe.wait_ge(rstd2_ready, it + 1)
                    if due(it - 1):
                        pe.wait_ge(l_copied, it - 1)
                    pe.transpose(banks[0:HB, 6 + slot, 0:L], small[:, slot, 4, :], cut["identity"][0:L, 0:L]
                                 ).then_inc(scales_turned, 1)

                def rows_chunk(cc, slot, first=False, last=False):
                    c = 2 * cc + slot
                    for n in range(4):
                        if n < 3:
                            turn2(n + 1, c)
                        elif not last:
                            turn2(0, c + 1)
                        if n == 0 and not first:
                            turn_scales(c - 1, 1 - slot)
                        logits(n, c, slot)

                pe.wait_ge(y_added, 32 * (h + 1))
                turn2(0, 0)
                rows_chunk(0, 0, first=True)
                rows_chunk(0, 1)
                for cc in turns(pe, 1, CHUNKS // 2 - 1):
                    rows_chunk(cc, 0)
                    rows_chunk(cc, 1)
                rows_chunk(CHUNKS // 2 - 1, 0)
                rows_chunk(CHUNKS // 2 - 1, 1, last=True)
                turn_scales(CHUNKS - 1, 1)

            pe.wait_ge(peak_ready, 1)
            pe.wait_ge(l_copied, 16)
            pe.transpose(banks[0:1, 0, 0:P], sc[:, 0:1], cut["identity"]).then_inc(peak_turned, 1)
            pe.wait_ge(peak_row, 1)
            pe.matmul(banks[:, 1, 0:P], cut["ones"][0:1, :], mrow[:, :], start=True, stop=True).then_inc(peak_spread, 1)
            pe.wait_ge(vectors_in, 64)
            pe.transpose(banks[:, 2, 0:E * FC], b1_rows[:, :],
                         cut["identity"][0:E * FC, 0:E * FC]).then_inc(b1_turned, 1)
            pe.wait_ge(sum_ready, 1)
            pe.matmul(banks[:, 3, 0:1], cut["group"], sc[:, 4:5], start=True, stop=True).then_inc(sum_spread, 1)
            for phase in range(2):
                for i in turns(pe, 0, ROUNDS):
                    pe.wait_ge(count_ready, i + ((ROUNDS + 1) * phase + 1))
                    pe.wait_ge(count_act, i + (ROUNDS * phase + 1))
                    pe.matmul(banks[:, 4, 0:3], group16, counts[:, 0:3], start=True, stop=True).then_inc(count_spread, 1)
                pe.wait_ge(count_ready, (ROUNDS + 1) * (phase + 1))
                pe.matmul(banks[:, 4, 3 + phase:4 + phase], cut["group"], sc[:, 2:3],
                          start=True, stop=True).then_inc(count_spread, 1)
            pe.wait_ge(spread_in_ready, 1)
            pe.matmul(banks[:, 5, 0:4 * E], cut["ones"], spread_in[:, :, :].rearrange("p a b -> p (a b)"),
                      start=True, stop=True).then_inc(spread_done, 1)
            pe.wait_ge(totals_ready, 2)
            pe.matmul(banks[:, 6, 0:2 * TB], cut["before"], tot[:, :, :].rearrange("p a b -> p (a b)"),
                      start=True, stop=False)
            pe.matmul(banks[:, 6, 16:32], cut["ones"], tot[:, 0, :], start=False, stop=True).then_inc(offsets_ready, 1)
            def ranks(e, q):
                if q == 0:
                    pe.wait_ge(onehot_ready, e + 1)
                if 2 * e + q:
                    pe.wait_ge(row_used, 2 * e + q)
                for m in range(4):
                    for half in range(2):
                        mm = pe.matmul(banks[:, 7, m * (L + 2):(m + 1) * (L + 2)],
                                       onehot[:, half, (4 * q + m) * P:(4 * q + m + 1) * P],
                                       rank[:, e + half * E, :], start=half == 0, stop=half == 1)
                mm.then_inc(row_ready, 1)

            def ffn_turn(n):
                if n < 2 * E:
                    pe.wait_ge(norm_ready, n + 1)
                    if n:
                        pe.wait_ge(ft_copied, n)
                    for m in range(4):
                        mm = pe.transpose(banks[:, 0, m * P:(m + 1) * P], normed[:, n // 2 % 2, 4 * (n % 2) + m, :],
                                          cut["identity"])
                    mm.then_inc(ft_ready, 1)

            pe.wait_ge(steps_ready, 1)
            for e in range(AHEAD):
                for q in range(2):
                    ranks(e, q)
            ffn_turn(0)
            for n in range(2 * E + 1):
                if n < 2 * E:
                    e, g = n // 2, n % 2
                    if g == 0:
                        pe.wait_ge(weights_in[e % 2], 32 * (e // 2 + 1))
                    pe.wait_ge(ft_copied, n + 1)
                    for f in range(FC):
                        if n:
                            pe.wait_ge(gelu_ready, FC * (n - 1) + f + 1)
                        pe.matmul(banks[:, 1 + f, :], w1_ring[:, e % 2, f * P:(f + 1) * P], xt_all[:, g],
                                  start=True, stop=True).then_inc(up_ready, 1)
                    ffn_turn(n + 1)
                if n + AHEAD < E:
                    ranks(n + AHEAD, 0)
                if n:
                    e, g = (n - 1) // 2, (n - 1) % 2
                    pe.wait_ge(gelu_ready, FC * n)
                    if n > 2:
                        pe.wait_ge(down_copied, n - 2)
                    for m in range(4):
                        for f in range(FC):
                            mm = pe.matmul(banks[:, 5 + g, m * D:(m + 1) * D], acts[:, g, f, m * P:(m + 1) * P],
                                           w2_ring[:, e % 2, f, :], start=f == 0, stop=f == FC - 1)
                    mm.then_inc(down_ready, 1)
                if n + AHEAD < E:
                    ranks(n + AHEAD, 1)

        @block.vector
        def _(dve):
            own = Steps(dve)
            dve.memset(banks[0:98, 6:8, :], 0.0)
            dve.memset(s2[:, :, 0:HB], 0.0)
            dve.wait_ge(wr_sum, 1)
            dve.scalar_tensor_tensor(wr_c[:, :], banks[:, 2, 0:E], -1.0 / D, wr_c[:, :],
                                     ALU.mult, ALU.add).then_inc(wr_ready, 1)
            dve.wait_ge(params_in, 64)
            dve.wait_ge(a_ready, 1)
            dve.tensor_scalar(par[:, 5:6], par[:, 4:5], -1.0, None, ALU.mult).then_inc(rate_ready, 1)
            dve.wait_ge(const_in, 16)
            dve.tensor_scalar(ANG, cut["times"], par[:, 1:2], None, ALU.mult).then_inc(dve_own, own.one())
            for n, (dst, quarter) in enumerate(((RED, 0.0), (ANG, 0.25))):
                dve.wait_ge(dve_own, own.all())
                dve.tensor_scalar(Q, ANG, float(1 / TWO_PI), quarter, ALU.mult, ALU.add).then_inc(dve_own, own.one())
                dve.wait_ge(dve_own, own.all())
                dve.tensor_scalar(Q, Q, MAGIC, -MAGIC, ALU.add, ALU.add).then_inc(dve_own, own.one())
                src = ANG
                for part in (C1, C2, C3):
                    dve.wait_ge(dve_own, own.all())
                    dve.scalar_tensor_tensor(dst, Q, -part, src, ALU.mult, ALU.add).then_inc(dve_own, own.one())
                    src = dst
                if n:
                    dve.wait_ge(dve_own, own.all())
                    dve.tensor_scalar(dst, dst, float(np.pi / 2), None, ALU.add).then_inc(dve_own, own.one())
                dve.wait_ge(dve_own, own.all())
                dve.tensor_scalar(dst, dst, PI_IN, -PI_IN, ALU.min, ALU.max).then_inc(reduced_ready, 1)
            dve.wait_ge(decay_ready, 1)
            dve.wait_ge(trig_ready, 2)
            dve.tensor_tensor(ANG, COS, R_, ALU.mult).then_inc(tables_ready, 1)
            dve.tensor_tensor(RED, SIN, R_, ALU.mult).then_inc(tables_ready, 1)
            dve.wait_ge(tables_ready, 2)
            dve.tensor_copy(mu[:, 0:1], ANG[:, L:L + 1]).then_inc(dve_own, own.one())
            dve.tensor_copy(mu[:, 1:2], RED[:, L:L + 1]).then_inc(dve_own, own.one())
            dve.tensor_scalar(mu[:, 2:3], RED[:, L:L + 1], -1.0, None, ALU.mult).then_inc(dve_own, own.one())
            N1 = L + 1
            dve.tensor_scalar(Q[:, 0:N1], RED[:, 0:N1], par[:, 3:4], None, ALU.mult).then_inc(dve_own, own.one())
            dve.memset(KPAD[:, 0:L - 1], 0.0).then_inc(dve_own, own.one())
            dve.memset(KPAD[:, 2 * L - 1:], 0.0)
            dve.memset(setup[:, 3:5, L + 1:P + 1], 0.0).then_inc(kernel_ready, 1)
            dve.wait_ge(dve_own, own.all())
            dve.scalar_tensor_tensor(SIN[:, 0:N1], ANG[:, 0:N1], par[:, 2:3], Q[:, 0:N1],
                                     ALU.mult, ALU.subtract).then_inc(kernel_ready, 1)
            dve.wait_ge(kernel_ready, 2)
            dve.tensor_scalar(Q[:, 0:N1], ANG[:, 0:N1], par[:, 3:4], None, ALU.mult).then_inc(dve_own, own.one())
            dve.tensor_copy(KPAD[:, L - 1:2 * L - 1], SIN[:, 0:L]).then_inc(kernel_ready, 1)
            dve.wait_ge(dve_own, own.all())
            dve.scalar_tensor_tensor(COS[:, 0:N1], RED[:, 0:N1], par[:, 2:3], Q[:, 0:N1],
                                     ALU.mult, ALU.add).then_inc(dve_own, own.one())
            dve.wait_ge(dve_own, own.all())
            dve.tensor_scalar(COS[:, 0:N1], COS[:, 0:N1], -1.0, None, ALU.mult).then_inc(kernel_ready, 1)

            def halves_stats(c, slot, n):
                for b in range(4 * n, 4 * n + 4):
                    ins = dve.bn_stats(stats[:, slot, b, :],
                                       hid[:, bass.ds(c * HB + b, 1), :].rearrange("p a k -> p (a k)"))
                if n == 3:
                    ins.then_inc(dve_own, own.one())

            def moments(slot, ready, between=lambda step: None):
                between(0)
                dve.wait_ge(dve_own, own.all())
                mean0, sq0, mean1, sq1 = (stats[:, slot, :, n] for n in (1, 2, 4, 5))
                diff, total, var, mean_sum, _, mean = (small[:, slot, n, :] for n in range(6))
                dve.tensor_tensor(diff, mean0, mean1, ALU.subtract).then_inc(dve_own, own.one())
                dve.tensor_tensor(total, sq0, sq1, ALU.add).then_inc(dve_own, own.one())
                dve.tensor_tensor(mean_sum, mean0, mean1, ALU.add).then_inc(dve_own, own.one())
                between(1)
                dve.wait_ge(dve_own, own.all())
                dve.tensor_tensor(diff, diff, diff, ALU.mult).then_inc(dve_own, own.one())
                dve.tensor_scalar(mean, mean_sum, 0.5, None, ALU.mult).then_inc(dve_own, own.one())
                between(2)
                dve.wait_ge(dve_own, own.all())
                dve.scalar_tensor_tensor(total, diff, D / 4.0, total, ALU.mult, ALU.add).then_inc(dve_own, own.one())
                between(3)
                dve.wait_ge(dve_own, own.all())
                dve.tensor_scalar(var, total, 1.0 / D, EPS, ALU.mult, ALU.add).then_inc(ready, 1)

            for h in range(2):
                def normalise(c, slot, first, last):
                    for b in range(first, last):
                        ins = dve.tensor_scalar(xn[0:L, :, bass.ds(c * HB + b, 1)].rearrange("p k a -> p (k a)"),
                                                hid[:, bass.ds(c * HB + b, 1), :].rearrange("p a k -> p (a k)"),
                                                small[:, slot, 5, b:b + 1], small[:, slot, 4, b:b + 1],
                                                ALU.subtract, ALU.mult)
                    if last == DVE_TILES:
                        ins.then_inc(xn_dve, 1)

                def bias(c, slot):
                    dve.wait_ge(rstd_ready, c + (CHUNKS * h + 1))
                    dve.scalar_tensor_tensor(small[:, slot, 6, :], small[:, slot, 5, :], -1.0, small[:, slot, 4, :],
                                             ALU.mult, ALU.mult).then_inc(nb_ready, 1)

                def front(cc, slot, first=False):
                    c = 2 * cc + slot
                    it = c + CHUNKS * h
                    for n in range(4):
                        dve.wait_ge(h_copied, 4 * it + (n + 1))
                        halves_stats(c, slot, n)
                        if n == 1 and not first:
                            bias(c - 1, 1 - slot)
                        if n in (1, 2) and not first:
                            normalise(c - 1, 1 - slot, 2 * n - 2, 2 * n)
                    if due(it - 1):
                        dve.wait_ge(xn_act, it - 1)
                        dve.wait_ge(xn_pool, it - 1)
                    if first:
                        moments(slot, var_ready)
                    else:
                        moments(slot, var_ready)
                        normalise(c - 1, 1 - slot, 4, DVE_TILES)

                if due(32 * h):
                    dve.wait_ge(y_ready, 32 * h)
                front(0, 0, first=True)
                front(0, 1)
                for cc in own.loop(1, CHUNKS // 2 - 1, 14):
                    front(cc, 0)
                    front(cc, 1)
                front(CHUNKS // 2 - 1, 0)
                front(CHUNKS // 2 - 1, 1)
                bias(CHUNKS - 1, 1)
                normalise(CHUNKS - 1, 1, 0, DVE_TILES)

                def states(g):
                    part = slice(*GROUPS[g])

                    def state(ri, c):
                        return s2[part, ri, HB * c:HB * (c + 1)]

                    def end(ri, c):
                        return e2[part, ri, HB * c:HB * (c + 1)]

                    if due(32 * h):
                        dve.wait_ge(s_moved[g], 32 * h)
                    dve.wait_ge(e_moved[g], 32 * (h + 1))
                    for ri in range(2):
                        dve.tensor_copy(state(ri, 1), end(ri, 0)).then_inc(dve_own, own.one())
                    for c in range(2, CHUNKS):
                        dve.wait_ge(dve_own, own.all())
                        for ri in range(2):
                            dve.scalar_tensor_tensor(carry[part, ri, :], state(0, c - 1), mu[part, ri:ri + 1],
                                                     end(ri, c - 1), ALU.mult, ALU.add).then_inc(dve_own, own.one())
                        dve.wait_ge(dve_own, own.all())
                        for ri in range(2):
                            m = (2, 0)[ri]
                            dve.scalar_tensor_tensor(state(ri, c), state(1, c - 1), mu[part, m:m + 1],
                                                     carry[part, ri, :], ALU.mult, ALU.add).then_inc(dve_own, own.one())
                    dve.wait_ge(dve_own, own.all())
                    dve.nop().then_inc(s_ready, 1)

                def add_products(i):
                    for n in range(8):
                        dve.wait_ge(y_ready, 8 * i + (n + 32 * h + 1))
                        rows = hid[:, :, bass.ds(i * TURN + 4 * n, 4)]
                        dve.tensor_tensor(rows, rows, banks[0:L, 2 + n % 4, :].rearrange("p (k n) -> p n k", k=4),
                                          ALU.add).then_inc(y_added, 1)

                states(0)
                states(1)
                add_products(0)
                states(2)
                for i in turns(dve, 1, D // TURN):
                    add_products(i)
                dve.wait_ge(y_added, 32 * (h + 1))

                def rows_moments(cc, slot):
                    c = 2 * cc + slot
                    it = c + CHUNKS * h
                    for n in range(4):
                        halves_stats(c, slot, n)
                    if due(it - 1):
                        dve.wait_ge(scales_turned, it - 1)
                    moments(slot, var2_ready)

                rows_moments(0, 0)
                rows_moments(0, 1)
                for cc in own.loop(1, CHUNKS // 2 - 1, 14):
                    rows_moments(cc, 0)
                    rows_moments(cc, 1)
                rows_moments(CHUNKS // 2 - 1, 0)
                rows_moments(CHUNKS // 2 - 1, 1)

            dve.memset(keep[:, :, :], 1.0).then_inc(dve_own, own.one())
            dve.memset(in_front[0:1, 0:E, :], 0.0).then_inc(dve_own, own.one())
            dve.wait_ge(dve_own, own.all())
            dve.memset(keep[:, :, 0:1], 0.0).then_inc(dve_own, own.one())
            for n, name in enumerate(("base_high", "base_low")):
                dve.tensor_copy(rank[:, :, L + n:L + n + 1].rearrange("p (h e) a -> p h (e a)", h=2),
                                cut[name].unsqueeze(2).broadcast_to([P, 2, E])).then_inc(dve_own, own.one())
            dve.wait_ge(vectors_in, 64)
            dve.tensor_copy(slots16, slots).then_inc(dve_own, own.one())
            dve.tensor_copy(group16, cut["group"]).then_inc(dve_own, own.one())
            dve.wait_ge(logits_in, 64)
            dve_far = far.rearrange("p (r n) -> p r n", r=ROWS_SEG)
            dve.tensor_tensor(far, far, far_scale, ALU.mult).then_inc(dve_own, own.one())
            dve.wait_ge(dve_own, own.all())
            dve.memset(dve_far[:, :, FRAMES:PADDED], -FAR).then_inc(dve_own, own.one())
            dve.wait_ge(dve_own, own.all())
            dve.tensor_reduce(sc[:, 0:1], far, AX.X, ALU.max).then_inc(peak_ready, 1)
            dve.wait_ge(peak_turned, 1)
            dve.tensor_copy(mrow[:, :], banks[0:1, 0, 0:P]).then_inc(peak_row, 1)
            dve.wait_ge(peak_spread, 1)
            dve.tensor_tensor(mall, banks[:, 1, 0:P], cut["group"], ALU.mult).then_inc(dve_own, own.one())
            dve.wait_ge(dve_own, own.all())
            dve.tensor_tensor(mall, mall, cut["other_group"], ALU.add).then_inc(dve_own, own.one())
            dve.wait_ge(dve_own, own.all())
            dve.tensor_reduce(sc[:, 1:2], mall, AX.X, ALU.max).then_inc(dve_own, own.one())
            dve.wait_ge(dve_own, own.all())
            dve.tensor_scalar(far, far, -1.0, sc[:, 1:2], ALU.mult, ALU.add).then_inc(far_ready, 1)
            prefix, delta, wanted_below = trial[:, 0, 3:4], sc[:, 3:4], sc[:, 9:10]
            dve.memset(sc[:, 6:7], SEG / 2.0).then_inc(dve_own, own.one())
            dve.memset(wanted_below, CAP - 0.5).then_inc(dve_own, own.one())
            dve.wait_ge(far_ready, 1)
            pairs = far.bitcast(U16).rearrange("p (n a) -> p n a", a=2)
            dve.tensor_copy(upper, pairs[:, :, 1:2].rearrange("p n a -> p (n a)")).then_inc(dve_own, own.one())
            for phase, source in enumerate((upper, lower)):
                dve.tensor_copy(trial[:, 0, :], cut["trials"][:, 0:4]).then_inc(trials_ready, 1)
                for i in own.loop(0, ROUNDS // 2, 2):
                    for k in range(2):
                        turn = 2 * i + ((ROUNDS + 1) * phase + k + 1)
                        dve.wait_ge(trials_ready, turn)
                        for n in range(2):
                            ins = dve.tensor_scalar(marks[n], source, trial[:, k, n:n + 1], None, ALU.is_lt, ALU.add,
                                                    accum_out=counts[:, n:n + 1])
                        ins.then_inc(count_ready, 1)
                        dve.wait_ge(count_spread, turn)
                        dve.scalar_tensor_tensor(passed[:, :], banks[:, 4, 0:3], wanted_below,
                                                 cut["units"][:, bass.ds(i * 6 + 3 * k, 3)], ALU.is_lt, ALU.mult,
                                                 accum_out=delta).then_inc(dve_own, own.one())
                        dve.wait_ge(dve_own, own.all())
                        dve.tensor_scalar(trial[:, 1 - k, :], cut["trials"][:, bass.ds(i * 8 + 4 * (k + 1), 4)],
                                          trial[:, k, 3:4], delta, ALU.add, ALU.add).then_inc(trials_ready, 1)
                dve.wait_ge(trials_ready, (ROUNDS + 1) * (phase + 1))
                dve.tensor_copy(sc[:, 15:16].bitcast(U16)[:, 1 - phase:2 - phase], prefix).then_inc(dve_own, own.one())
                if phase == 0:
                    dve.tensor_scalar(marks[1], upper, prefix, None, ALU.is_lt, ALU.add,
                                      accum_out=sc[:, 2:3]).then_inc(count_ready, 1)
                    dve.wait_ge(count_ready, ROUNDS + 1)
                    dve.tensor_scalar(marks[0], upper, prefix, 65535.0,
                                      ALU.not_equal, ALU.mult).then_inc(dve_own, own.one())
                    dve.wait_ge(dve_own, own.all())
                    dve.wait_ge(lower_ready, 1)
                    dve.tensor_tensor(lower, lower, marks[0], ALU.max).then_inc(dve_own, own.one())
                    dve.wait_ge(count_spread, ROUNDS + 1)
                    dve.tensor_scalar(wanted_below, banks[:, 4, 3:4], -1.0, CAP - 0.5,
                                      ALU.mult, ALU.add).then_inc(dve_own, own.one())
                    dve.wait_ge(dve_own, own.all())
            dve.wait_ge(dve_own, own.all())
            dve.tensor_scalar(seen, far, sc[:, 15:16], None, ALU.is_lt, ALU.add,
                              accum_out=sc[:, 2:3]).then_inc(count_ready, 1)
            dve.wait_ge(count_spread, 2 * (ROUNDS + 1))
            dve.wait_ge(sum_spread, 1)
            dve.reciprocal(sc[:, 5:6], banks[:, 3, 0:1]).then_inc(dve_own, own.one())
            dve.tensor_scalar(sc[:, 11:12], banks[:, 4, 4:5], -1.0, float(CAP),
                              ALU.mult, ALU.add).then_inc(dve_own, own.one())
            dve.wait_ge(dve_own, own.all())
            for n, column in enumerate((15, 11, 1, 5)):
                ins = dve.tensor_scalar(spread_in[:, n, :], cut["first_of_expert"], sc[:, column:column + 1],
                                        None, ALU.mult)
            ins.then_inc(spread_in_ready, 1)
            dve.wait_ge(spread_done, 1)
            dve.tensor_copy(spread[:, :, :].rearrange("p a b -> p (a b)"),
                            banks[:, 5, 0:4 * E]).then_inc(dve_own, own.one())

            def mark(e):
                if e:
                    dve.wait_ge(row_ready, 2 * e)
                for half in range(2):
                    ins = dve.tensor_scalar(onehot[:, half, :], slots16, bounds[:, 1, half * E + e:half * E + e + 1],
                                            None, ALU.is_ge)
                ins.then_inc(onehot_ready, 1)

            dve.wait_ge(gone_in, 32)
            dve.wait_ge(dve_own, own.all())
            for half in range(2):
                part = slice(half * E, (half + 1) * E)
                cutoff = spread[:, 0, :].unsqueeze(2).broadcast_to([P, E, L])
                dve.tensor_tensor(below[:, part], gone[:, part], cutoff, ALU.is_lt).then_inc(dve_own, own.one())
                dve.tensor_tensor(equal[:, part], gone[:, part], cutoff, ALU.is_equal).then_inc(dve_own, own.one())
            dve.wait_ge(dve_own, own.all())
            flat = lambda a: a[:, :, :].rearrange("p a b -> p (a b)")
            dve.tensor_tensor_scan(flat(n_below), flat(keep), flat(below), 0.0,
                                   ALU.mult, ALU.add).then_inc(dve_own, own.one())
            dve.tensor_tensor_scan(flat(n_equal), flat(keep), flat(equal), 0.0,
                                   ALU.mult, ALU.add).then_inc(dve_own, own.one())
            dve.wait_ge(dve_own, own.all())
            for n, a in enumerate((n_below, n_equal)):
                dve.tensor_copy(tot[:, :, n * E:(n + 1) * E],
                                a[:, :, L - 1:L].rearrange("p (h e) a -> p h (e a)", h=2)).then_inc(totals_ready, 1)
            dve.wait_ge(offsets_ready, 1)
            dve.tensor_copy(off[:, :, :].rearrange("p a b -> p (a b)"), banks[:, 6, 0:32]).then_inc(dve_own, own.one())
            dve.wait_ge(dve_own, own.all())
            wanted = spread[:, 1, :].unsqueeze(1).broadcast_to([P, 2, E])
            halves = lambda n: bounds[:, n, :].rearrange("p (h e) -> p h e", h=2)
            dve.tensor_tensor(halves(0), wanted, off[:, :, E:2 * E], ALU.subtract).then_inc(dve_own, own.one())
            dve.tensor_tensor(halves(1), wanted, off[:, :, E:2 * E], ALU.min).then_inc(dve_own, own.one())
            dve.wait_ge(dve_own, own.all())
            dve.tensor_scalar(bounds[:, 0, :], bounds[:, 0, :], 0.0, None, ALU.max).then_inc(dve_own, own.one())
            dve.tensor_tensor(halves(1), halves(1), off[:, :, 0:E], ALU.add).then_inc(dve_own, own.one())
            dve.wait_ge(dve_own, own.all())
            dve.tensor_copy(limits[:, :, :], bounds[:, 0:2, :]).then_inc(dve_own, own.one())
            dve.wait_ge(dve_own, own.all())
            dve.tensor_tensor(n_equal[:, :, :], n_equal[:, :, :],
                              limits[:, 0, :].unsqueeze(2).broadcast_to([P, TB, L]), ALU.min).then_inc(dve_own, own.one())
            dve.tensor_tensor(n_below[:, :, :], n_below[:, :, :],
                              limits[:, 1, :].unsqueeze(2).broadcast_to([P, TB, L]), ALU.add).then_inc(dve_own, own.one())
            dve.wait_ge(dve_own, own.all())
            dve.tensor_tensor(rank[:, :, 0:L], n_below[:, :, :], n_equal[:, :, :],
                              ALU.add).then_inc(dve_own, own.one())
            dve.wait_ge(dve_own, own.all())
            dve.nop().then_inc(rank_ready, 1)
            mark(0)
            dve.wait_ge(front_in, 32)
            dve.tensor_tensor(rank[:, :, :], rank[:, :, :], in_front[:, :, :], ALU.subtract).then_inc(steps_ready, 1)

            def choose(e):
                for q in range(2):
                    dve.wait_ge(row_ready, 2 * e + q + 1)
                    rows = banks[:, 7, 0:4 * (L + 2)].rearrange("p (m t) -> p m t", m=4)
                    dve.tensor_tensor(marked[:, :, :], rows[:, :, 0:L],
                                      cut["slot_numbers"][:, 4 * q:4 * q + 4].unsqueeze(2).broadcast_to([P, 4, L]),
                                      ALU.is_le).then_inc(dve_own, own.one())
                    dve.tensor_copy(base2[:, :, :], rows[:, :, L:L + 2]).then_inc(row_used, 1)
                    dve.wait_ge(dve_own, own.all())
                    dve.wait_ge(row_used, 2 * e + q + 1)
                    dve.tensor_reduce(place[:, 0, :], marked[:, :, :], AX.X, ALU.add).then_inc(dve_own, own.one())
                    dve.scalar_tensor_tensor(place[:, 1, :], base2[:, :, 0], float(P), base2[:, :, 1],
                                             ALU.mult, ALU.add).then_inc(dve_own, own.one())
                    dve.wait_ge(dve_own, own.all())
                    dve.tensor_tensor(index[:, e * SLOT_TILES + 4 * q:e * SLOT_TILES + 4 * q + 4], place[:, 0, :],
                                      place[:, 1, :], ALU.add).then_inc(index_ready, 1)
                dve.wait_ge(index_ready, 2 * e + 2)
                if e + 1 < E:
                    mark(e + 1)

            def prepare(e):
                slot = e % 3
                dve.wait_ge(found_in[e % 2], 128 * (e // 2 + 1))
                for m in range(SLOT_TILES):
                    ins = dve.bn_stats(fstats[:, m, :], found[:, e * SLOT_TILES + m, :])
                ins.then_inc(dve_own, own.one())
                dve.wait_ge(dve_own, own.all())
                mean0, sq0, mean1, sq1 = (fstats[:, :, n] for n in (1, 2, 4, 5))
                diff, total, half_var, mean_sum, rstd, mean, shift = (
                    fsmall[:, slot, n, :] for n in range(7))
                score = scores[:, e, :]
                square = diff
                dve.tensor_tensor(diff, mean0, mean1, ALU.subtract).then_inc(dve_own, own.one())
                dve.tensor_tensor(total, sq0, sq1, ALU.add).then_inc(dve_own, own.one())
                dve.tensor_tensor(mean_sum, mean0, mean1, ALU.add).then_inc(dve_own, own.one())
                dve.wait_ge(dve_own, own.all())
                dve.tensor_tensor(diff, diff, diff, ALU.mult).then_inc(dve_own, own.one())
                dve.tensor_scalar(mean, mean_sum, 0.5, None, ALU.mult).then_inc(dve_own, own.one())
                dve.wait_ge(dve_own, own.all())
                dve.scalar_tensor_tensor(total, diff, D / 4.0, total, ALU.mult, ALU.add).then_inc(dve_own, own.one())
                dve.wait_ge(dve_own, own.all())
                dve.tensor_scalar(diff, total, 1.0 / D, EPS, ALU.mult, ALU.add).then_inc(dve_own, own.one())
                dve.wait_ge(dve_own, own.all())
                dve.tensor_scalar(rstd.bitcast(I32), diff.bitcast(I32), -0.5, float(0x5f3759df),
                                  ALU.mult, ALU.add).then_inc(dve_own, own.one())
                dve.tensor_scalar(half_var, diff, -0.5, None, ALU.mult).then_inc(dve_own, own.one())
                for _ in range(3):
                    dve.wait_ge(dve_own, own.all())
                    dve.tensor_tensor(square, rstd, rstd, ALU.mult).then_inc(dve_own, own.one())
                    dve.wait_ge(dve_own, own.all())
                    dve.tensor_tensor(square, square, half_var, ALU.mult).then_inc(dve_own, own.one())
                    dve.wait_ge(dve_own, own.all())
                    dve.scalar_tensor_tensor(rstd, square, 1.5, rstd, ALU.add, ALU.mult).then_inc(dve_own, own.one())
                dve.wait_ge(dve_own, own.all())
                dve.scalar_tensor_tensor(shift, mean, -1.0, rstd, ALU.mult, ALU.mult).then_inc(rstd3_ready, 1)
                for m in range(SLOT_TILES):
                    ins = dve.scalar_tensor_tensor(adds[:, e * SLOT_TILES + m, :], found[:, e * SLOT_TILES + m, :],
                                                   mean[:, m:m + 1], wr_all[:, :, e], ALU.subtract, ALU.mult,
                                                   accum_out=score[:, m:m + 1])
                ins.then_inc(dve_own, own.one())
                dve.wait_ge(dve_own, own.all())
                dve.tensor_tensor(score, score, rstd, ALU.mult).then_inc(dve_own, own.one())
                dve.wait_ge(dve_own, own.all())
                dve.tensor_tensor(score, score, spread[:, 2, e:e + 1].broadcast_to([P, SLOT_TILES]),
                                  ALU.subtract).then_inc(score_ready, 1)

            def collect(e):
                for g in range(2):
                    dve.wait_ge(down_ready, 2 * e + g + 1)
                    dve.tensor_tensor(adds[:, e * SLOT_TILES + 4 * g:e * SLOT_TILES + 4 * g + 4, :],
                                      banks[:, 5 + g, :].rearrange("p (m d) -> p m d", m=4),
                                      b2_all[:, e:e + 1, :].broadcast_to([P, 4, D]), ALU.add).then_inc(down_copied, 1)

            def weigh(e, g):
                if g == 0:
                    dve.wait_ge(weight_ready, e + 1)
                    dve.tensor_tensor(weight[:, e, :], parts[:, e, :],
                                      spread[:, 3, e:e + 1].broadcast_to([P, SLOT_TILES]), ALU.mult).then_inc(dve_own, own.one())
                    dve.wait_ge(dve_own, own.all())
                dve.wait_ge(down_copied, 2 * e + g + 1)
                dst = adds[:, e * SLOT_TILES + 4 * g:e * SLOT_TILES + 4 * g + 4, :]
                dve.tensor_tensor(dst, dst, weight[:, e, 4 * g:4 * g + 4].unsqueeze(2).broadcast_to([P, 4, D]),
                                  ALU.mult).then_inc(adds_ready, 1)

            dve.wait_ge(b1_ready, 1)
            for e in range(AHEAD - 1):
                choose(e)
            prepare(0)
            choose(AHEAD - 1)
            prepare(1)
            for e in range(E):
                if 2 * e + AHEAD < E:
                    choose(2 * e + AHEAD)
                if e + 2 < E:
                    prepare(e + 2)
                if 2 * e + 1 + AHEAD < E:
                    choose(2 * e + 1 + AHEAD)
                if e == ALL_FOUND:
                    for g in range(2 * ALL_FOUND):
                        weigh(g // 2, g % 2)
                collect(e)
                if e >= ALL_FOUND:
                    for g in range(2):
                        weigh(e, g)

        @block.gpsimd
        def _(pool):
            pool.memset(natural[:, :], float(np.e)).then_inc(powers_ready, 1)
            pool.memset(powers[:, :], -0.5).then_inc(powers_ready, 1)
            pool.wait_ge(powers_ready, 2)
            for h in range(2):
                if h:
                    pool.wait_ge(t2_ready, 4 * CHUNKS * h)
                for cc in turns(pool, 0, CHUNKS // 2):
                    for slot in range(2):
                        it = 2 * cc + (slot + CHUNKS * h)
                        pool.wait_ge(var_ready, it + 1)
                        pool.tensor_tensor(small[:, slot, 4, :], small[:, slot, 2, :], powers[0:L, :],
                                           ALU.pow).then_inc(rstd_ready, 1)
                        pool.wait_ge(rstd_ready, it + 1)
                        last_tiles = bass.ds(cc * (2 * HB) + (HB * slot + ACT_END), HB - ACT_END)
                        mean, scale = (small[:, slot, n, ACT_END:HB].unsqueeze(2).broadcast_to([L, HB - ACT_END, D])
                                       for n in (5, 4))
                        pool.tensor_tensor(staged[:, 2, 0:HB - ACT_END], hid[:, last_tiles, :], mean,
                                           ALU.subtract).then_inc(centred, 1)
                        pool.wait_ge(centred, it + 1)
                        pool.tensor_tensor(xn[0:L, :, last_tiles].rearrange("p k b -> p b k"),
                                           staged[:, 2, 0:HB - ACT_END], scale, ALU.mult).then_inc(xn_pool, 1)
                pool.wait_ge(y_added, 32 * (h + 1))
                for cc in turns(pool, 0, CHUNKS // 2, peel=h == 0):
                    for slot in range(2):
                        it = 2 * cc + (slot + CHUNKS * h)
                        for n in range(ACT_GROUPS, 4):
                            if due(4 * it + (n - 3)):
                                pool.wait_ge(t2_ready, 4 * it + (n - 3))
                            pool.tensor_copy(staged[:, 2], hid[:, bass.ds(cc * (2 * HB) + (HB * slot + 4 * n), 4), :]
                                             ).then_inc(staged_pool, 1)
                        pool.wait_ge(var2_ready, it + 1)
                        pool.tensor_tensor(small[:, slot, 4, :], small[:, slot, 2, :], powers[0:L, :],
                                           ALU.pow).then_inc(rstd2_ready, 1)
            rows = out.rearrange("b f d -> (b f) d")

            def find(e):
                if e > 1:
                    pool.wait_ge(found_in[e % 2], 128 * (e // 2))
                for m in range(SLOT_TILES):
                    pool.wait_ge(index_ready, 2 * e + m // 4 + 1)
                    n = e * SLOT_TILES + m
                    pool.indirect_dma_start(found[:, n, :], None, rows,
                                            bass.IndirectOffsetOnAxis(ap=index[:, n:n + 1], axis=0)
                                            ).then_inc(found_in[e % 2], 16)

            def numerators(e):
                pool.wait_ge(score_ready, e + 1)
                pool.tensor_tensor(parts[:, e, :], natural[:, :], scores[:, e, :],
                                   ALU.pow).then_inc(weight_ready, 1)

            def add(e):
                if e:
                    pool.wait_ge(added, 128 * e)
                for m in range(SLOT_TILES):
                    pool.wait_ge(adds_ready, 2 * e + m // 4 + 1)
                    n = e * SLOT_TILES + m
                    pool.indirect_dma_start(rows, bass.IndirectOffsetOnAxis(ap=index[:, n:n + 1], axis=0),
                                            adds[:, n, :], None, compute_op=ALU.add, oob_is_err=True,
                                            bounds_check=ROWS * FRAMES - 1).then_inc(added, 16)

            pool.wait_ge(far_ready, 1)
            pairs = far.bitcast(U16).rearrange("p (n a) -> p n a", a=2)
            pool.tensor_copy(lower, pairs[:, :, 0:1].rearrange("p n a -> p (n a)")).then_inc(lower_ready, 1)

            pool.wait_ge(rows_out, 16 * 16)
            for e in range(E):
                find(e)
            for slot in range(2):
                pool.wait_ge(found_in[slot], 128 * (E // 2))
            for e in range(2):
                numerators(e)
            for e in range(E):
                add(e)
                if e + 2 < E:
                    numerators(e + 2)
            pool.wait_ge(added, 128 * E)


_INS = ["x", "L0_attn_nu", "L0_attn_theta", "L0_attn_gamma_real", "L0_attn_gamma_imag",
        "L0_ffn_Wr", "L0_ffn_W1", "L0_ffn_b1", "L0_ffn_W2", "L0_ffn_b2"]


def kernel(**inputs):
    import numpy as _np
    import concourse.bacc as _bacc
    from concourse import mybir as _mybir
    from concourse.bass_utils import run_bass_kernel_spmd as _run

    nc = _bacc.Bacc("TRN2", target_bir_lowering=False, num_devices=1)
    arrays, args = {}, []
    for name in _INS:
        a = _np.ascontiguousarray(inputs[name])
        arrays[f"in_{name}"] = a
        args.append(nc.dram_tensor(f"in_{name}", a.shape, _mybir.dt.from_np(a.dtype), kind="ExternalInput").ap())
    args.append(nc.dram_tensor("out_0", (ROWS, FRAMES, D), _mybir.dt.float32, kind="ExternalOutput").ap())
    build(nc, *args)
    r = _run(nc, [arrays], core_ids=[0])
    return r.results[0]["out_0"]
```
